# Optimizing a Trainium2 kernel written in Bass

```python
import numpy as np
import jax
import jax.numpy as jnp

def _softmax(x, axis=-1):
    return jax.nn.softmax(x, axis=axis)

def _gelu(x):
    return jax.nn.gelu(x, approximate=True)

def _silu(x):
    return jax.nn.silu(x)

def _sigmoid(x):
    return jax.nn.sigmoid(x)

def _layernorm(x, axis=-1, eps=1e-05):
    m = jnp.mean(x, axis=axis, keepdims=True)
    v = jnp.var(x, axis=axis, keepdims=True)
    return (x - m) / jnp.sqrt(v + eps)

def _scatter_add(tgt, idx, src, axis=0):
    return tgt.at[idx].add(src)

def _segment_sum(src, seg, n):
    return jax.ops.segment_sum(src, seg, n)
kernel_name = 'mk_gnn_preln_d4_gnn_r32_3db40d'

def setup_inputs(seed: int=0):
    np.random.seed(seed)
    _w = jnp.asarray

    def _rec_inputs():
        import jax
        import jax.numpy as jnp
        _gk = jax.random.key(seed)
        x = -0.0002117 + 1 * jax.random.normal(jax.random.fold_in(_gk, 1), (3125, 256), jnp.float32)
        src = jax.random.randint(jax.random.fold_in(_gk, 2), (50000,), 0, 3125, jnp.int32)
        dst = jnp.minimum((3125 * jax.random.uniform(jax.random.fold_in(_gk, 3), (50000,)) ** 2.0).astype(jnp.int32), 99999)
        _o = jnp.argsort(dst, stable=True)
        src = src[_o]
        dst = dst[_o]
        edge_type_16 = jax.random.randint(jax.random.fold_in(_gk, 12), (50000,), 0, 16, jnp.int32)
        edge_type_8 = jax.random.randint(jax.random.fold_in(_gk, 13), (50000,), 0, 8, jnp.int32)
        edge_weight = -0.000423496 + 0.100023 * jax.random.normal(jax.random.fold_in(_gk, 14), (50000,), jnp.float32)
        node_type_4 = jax.random.randint(jax.random.fold_in(_gk, 15), (3125,), 0, 4, jnp.int32)
        return (x, src, dst, edge_type_16, edge_type_8, edge_weight, node_type_4)
    x, src, dst, edge_type_16, edge_type_8, edge_weight, node_type_4 = _rec_inputs()

    def _L0_gnn_setup():
        import jax, jax.numpy as jnp
        import numpy as np
        N_NODES = 3125
        N_EDGES = 100000
        D = 256
        key = jax.random.key(seed)
        ks = jax.random.split(key, 6)
        x = jax.random.normal(ks[0], (N_NODES, D), dtype=jnp.float32)
        edge_src = jax.random.randint(ks[1], (N_EDGES,), 0, N_NODES, dtype=jnp.int32)
        edge_dst = jax.random.randint(ks[2], (N_EDGES,), 0, N_NODES, dtype=jnp.int32)
        w = jnp.ones((1,), dtype=jnp.float32) * 3.0
        W1 = jax.random.normal(ks[3], (64, D), dtype=jnp.float32) * 0.05
        W2 = jax.random.normal(ks[4], (32, 64), dtype=jnp.float32) * 0.1
        W3 = jax.random.normal(ks[5], (D, 32), dtype=jnp.float32) * 0.1
        return {'x': x, 'edge_src': edge_src, 'edge_dst': edge_dst, 'w': w, 'W1': W1, 'W2': W2, 'W3': W3}
    _L0_gnn_all = _L0_gnn_setup()
    _L0_gnn_in = {k: v for k, v in _L0_gnn_all.items() if k in ('w', 'W1', 'W2', 'W3')}
    del _L0_gnn_all

    def _L1_gnn_setup():
        import jax, jax.numpy as jnp
        import numpy as np
        N_NODES = 625
        N_EDGES = 10000
        IN_DIM = 256
        OUT_DIM = 256
        N_HEADS = 4
        D_K = OUT_DIM // N_HEADS
        N_NTYPES = 4
        N_RELS = 8
        SQRT_DK = float(np.sqrt(D_K))

        def _typed_matmul(x, W, node_type):
            all_t = jnp.einsum('ni,tio->tno', x, W)
            return all_t[node_type, jnp.arange(x.shape[0])]
        key = jax.random.key(seed)
        ks = jax.random.split(key, 12)
        xav = lambda k, shape, fan: jax.random.normal(k, shape, jnp.float32) * (1.0 / np.sqrt(fan))
        return {'h': jax.random.normal(ks[0], (N_NODES, IN_DIM), jnp.float32), 'k_linears': xav(ks[1], (N_NTYPES, IN_DIM, OUT_DIM), IN_DIM), 'q_linears': xav(ks[2], (N_NTYPES, IN_DIM, OUT_DIM), IN_DIM), 'v_linears': xav(ks[3], (N_NTYPES, IN_DIM, OUT_DIM), IN_DIM), 'a_linears': xav(ks[4], (N_NTYPES, OUT_DIM, OUT_DIM), OUT_DIM), 'relation_att': xav(ks[5], (N_RELS, N_HEADS, D_K, D_K), D_K), 'relation_msg': xav(ks[6], (N_RELS, N_HEADS, D_K, D_K), D_K), 'relation_pri': jnp.ones((N_RELS, N_HEADS), jnp.float32), 'skip': jnp.ones((N_NTYPES,), jnp.float32), 'node_type': jax.random.randint(ks[7], (N_NODES,), 0, N_NTYPES), 'etype': jnp.sort(jax.random.randint(ks[8], (N_EDGES,), 0, N_RELS)), 'row_idx': jax.random.randint(ks[9], (N_EDGES,), 0, N_NODES), 'col_idx': jax.random.randint(ks[10], (N_EDGES,), 0, N_NODES)}
    _L1_gnn_all = _L1_gnn_setup()
    _L1_gnn_in = {k: v for k, v in _L1_gnn_all.items() if k in ('k_linears', 'q_linears', 'v_linears', 'a_linears', 'relation_att', 'relation_msg', 'relation_pri', 'skip')}
    del _L1_gnn_all

    def _L2_gnn_setup():
        import jax, jax.numpy as jnp
        import numpy as np
        N_NODES = 50000
        N_EDGES = 25000
        HDIM = 256
        NUMRELS = 16

        def _gru_cell(x, h, w_ih, w_hh, b_ih, b_hh):
            gi = x @ w_ih.T + b_ih
            gh = h @ w_hh.T + b_hh
            i_r, i_z, i_n = jnp.split(gi, 3, axis=-1)
            h_r, h_z, h_n = jnp.split(gh, 3, axis=-1)
            r = jax.nn.sigmoid(i_r + h_r)
            z = jax.nn.sigmoid(i_z + h_z)
            n = jnp.tanh(i_n + r * h_n)
            return (1.0 - z) * n + z * h
        key = jax.random.key(seed)
        ks = jax.random.split(key, 9)
        h = jax.random.normal(ks[0], (N_NODES, HDIM), dtype=jnp.float32)
        relvectors = jax.random.normal(ks[1], (NUMRELS, HDIM), dtype=jnp.float32)
        s = 1.0 / np.sqrt(HDIM)
        w_ih = jax.random.uniform(ks[2], (3 * HDIM, HDIM), minval=-s, maxval=s, dtype=jnp.float32)
        w_hh = jax.random.uniform(ks[3], (3 * HDIM, HDIM), minval=-s, maxval=s, dtype=jnp.float32)
        b_ih = jax.random.uniform(ks[4], (3 * HDIM,), minval=-s, maxval=s, dtype=jnp.float32)
        b_hh = jax.random.uniform(ks[5], (3 * HDIM,), minval=-s, maxval=s, dtype=jnp.float32)
        edge_src = jax.random.randint(ks[6], (N_EDGES,), 0, N_NODES, dtype=jnp.int32)
        edge_dst = jax.random.randint(ks[7], (N_EDGES,), 0, N_NODES, dtype=jnp.int32)
        edge_rel = jax.random.randint(ks[8], (N_EDGES,), 0, NUMRELS, dtype=jnp.int32)
        return {'h': h, 'relvectors': relvectors, 'w_ih': w_ih, 'w_hh': w_hh, 'b_ih': b_ih, 'b_hh': b_hh, 'edge_src': edge_src, 'edge_dst': edge_dst, 'edge_rel': edge_rel}
    _L2_gnn_all = _L2_gnn_setup()
    _L2_gnn_in = {k: v for k, v in _L2_gnn_all.items() if k in ('relvectors', 'w_ih', 'w_hh', 'b_ih', 'b_hh')}
    del _L2_gnn_all

    def _L3_gnn_setup():
        import jax, jax.numpy as jnp
        import numpy as np
        BLOCK_DIMS = [8] * 32

        def _mask_indices():
            d = sum(BLOCK_DIMS)
            mask = np.ones((d, d), dtype=np.int8)
            off = 0
            for b in BLOCK_DIMS:
                mask[off:off + b, off:off + b] = 0
                off += b
            rows, cols = np.nonzero(mask)
            return (d, rows.astype(np.int32), cols.astype(np.int32))
        key = jax.random.key(seed)
        k1, k2 = jax.random.split(key)
        d, rows, cols = _mask_indices()
        N = 15625
        X = jax.random.normal(k1, (N, d), dtype=jnp.float32)
        w_est = 0.1 * jax.random.normal(k2, (rows.shape[0],), dtype=jnp.float32)
        return {'X': X, 'w_est': w_est, 'rows': jnp.asarray(rows), 'cols': jnp.asarray(cols)}
    _L3_gnn_all = _L3_gnn_setup()
    _L3_gnn_in = {k: v for k, v in _L3_gnn_all.items() if k in ()}
    del _L3_gnn_all
    return {'x': x, 'src': src, 'dst': dst, 'edge_type_16': edge_type_16, 'edge_type_8': edge_type_8, 'edge_weight': edge_weight, 'node_type_4': node_type_4, 'L0_gnn_w': _L0_gnn_in['w'], 'L0_gnn_W1': _L0_gnn_in['W1'], 'L0_gnn_W2': _L0_gnn_in['W2'], 'L0_gnn_W3': _L0_gnn_in['W3'], 'L1_gnn_k_linears': _L1_gnn_in['k_linears'], 'L1_gnn_q_linears': _L1_gnn_in['q_linears'], 'L1_gnn_v_linears': _L1_gnn_in['v_linears'], 'L1_gnn_a_linears': _L1_gnn_in['a_linears'], 'L1_gnn_relation_att': _L1_gnn_in['relation_att'], 'L1_gnn_relation_msg': _L1_gnn_in['relation_msg'], 'L1_gnn_relation_pri': _L1_gnn_in['relation_pri'], 'L1_gnn_skip': _L1_gnn_in['skip'], 'L2_gnn_relvectors': _L2_gnn_in['relvectors'], 'L2_gnn_w_ih': _L2_gnn_in['w_ih'], 'L2_gnn_w_hh': _L2_gnn_in['w_hh'], 'L2_gnn_b_ih': _L2_gnn_in['b_ih'], 'L2_gnn_b_hh': _L2_gnn_in['b_hh']}

def reference(x, src, dst, edge_type_16, edge_type_8, edge_weight, node_type_4, L0_gnn_w, L0_gnn_W1, L0_gnn_W2, L0_gnn_W3, L1_gnn_k_linears, L1_gnn_q_linears, L1_gnn_v_linears, L1_gnn_a_linears, L1_gnn_relation_att, L1_gnn_relation_msg, L1_gnn_relation_pri, L1_gnn_skip, L2_gnn_relvectors, L2_gnn_w_ih, L2_gnn_w_hh, L2_gnn_b_ih, L2_gnn_b_hh):
    import jax
    import jax.numpy as jnp

    def _L0_gnn_ref(x, edge_src, edge_dst, w, W1, W2, W3):
        import jax, jax.numpy as jnp
        import numpy as np
        N_NODES = 3125
        N_EDGES = 100000
        D = 256
        agg = jax.ops.segment_sum(x[edge_dst], edge_src, num_segments=N_NODES)
        y = agg + w * x
        h = jax.nn.relu(jnp.einsum('nd,hd->nh', y, W1))
        h = jax.nn.relu(jnp.einsum('nh,gh->ng', h, W2))
        h = jax.nn.relu(jnp.einsum('ng,og->no', h, W3))
        return h + x

    def _L1_gnn_ref(h, k_linears, q_linears, v_linears, a_linears, relation_att, relation_msg, relation_pri, skip, node_type, etype, row_idx, col_idx):
        import jax, jax.numpy as jnp
        import numpy as np
        N_NODES = 625
        N_EDGES = 10000
        IN_DIM = 256
        OUT_DIM = 256
        N_HEADS = 4
        D_K = OUT_DIM // N_HEADS
        N_NTYPES = 4
        N_RELS = 8
        SQRT_DK = float(np.sqrt(D_K))

        def _typed_matmul(x, W, node_type):
            all_t = jnp.einsum('ni,tio->tno', x, W)
            return all_t[node_type, jnp.arange(x.shape[0])]
        n = h.shape[0]
        k = _typed_matmul(h, k_linears, node_type).reshape(n, N_HEADS, D_K)
        q = _typed_matmul(h, q_linears, node_type).reshape(n, N_HEADS, D_K)
        v = _typed_matmul(h, v_linears, node_type).reshape(n, N_HEADS, D_K)
        q_att = jnp.einsum('nhd,rhde->rnhe', q, relation_att)
        v_msg = jnp.einsum('nhd,rhde->rnhe', v, relation_msg)
        aw_q_edge = q_att[etype, col_idx]
        msg_edge = v_msg[etype, row_idx]
        attn_score = jnp.sum(aw_q_edge * k[row_idx], axis=-1)
        score = attn_score * (relation_pri[etype] / SQRT_DK)
        m = jax.ops.segment_max(score, col_idx, num_segments=n)
        ex = jnp.exp(score - m[col_idx])
        denom = jax.ops.segment_sum(ex, col_idx, num_segments=n)
        alpha = ex / denom[col_idx]
        agg = jax.ops.segment_sum(alpha[..., None] * msg_edge, col_idx, num_segments=n)
        agg = agg.reshape(n, OUT_DIM)
        out = _typed_matmul(agg, a_linears, node_type)
        out = jax.nn.sigmoid(skip)[node_type][:, None] * out
        return out

    def _L2_gnn_ref(h, relvectors, w_ih, w_hh, b_ih, b_hh, edge_src, edge_dst, edge_rel):
        import jax, jax.numpy as jnp
        import numpy as np
        N_NODES = 50000
        N_EDGES = 25000
        HDIM = 256
        NUMRELS = 16

        def _gru_cell(x, h, w_ih, w_hh, b_ih, b_hh):
            gi = x @ w_ih.T + b_ih
            gh = h @ w_hh.T + b_hh
            i_r, i_z, i_n = jnp.split(gi, 3, axis=-1)
            h_r, h_z, h_n = jnp.split(gh, 3, axis=-1)
            r = jax.nn.sigmoid(i_r + h_r)
            z = jax.nn.sigmoid(i_z + h_z)
            n = jnp.tanh(i_n + r * h_n)
            return (1.0 - z) * n + z * h
        msg = h[edge_src] + relvectors[edge_rel]
        red = jax.ops.segment_sum(msg, edge_dst, num_segments=h.shape[0])
        return _gru_cell(red, h, w_ih, w_hh, b_ih, b_hh)

    def _L3_gnn_ref(X, w_est, rows, cols):
        import jax, jax.numpy as jnp
        import numpy as np
        BLOCK_DIMS = [8] * 32

        def _mask_indices():
            d = sum(BLOCK_DIMS)
            mask = np.ones((d, d), dtype=np.int8)
            off = 0
            for b in BLOCK_DIMS:
                mask[off:off + b, off:off + b] = 0
                off += b
            rows, cols = np.nonzero(mask)
            return (d, rows.astype(np.int32), cols.astype(np.int32))
        d = X.shape[1]
        W = jnp.zeros((d, d), dtype=X.dtype).at[rows, cols].set(w_est)
        return X @ W
    h = jnp.maximum(_layernorm(x, axis=-1), 0.0)
    x = x + _L0_gnn_ref(h, src, dst, L0_gnn_w, L0_gnn_W1, L0_gnn_W2, L0_gnn_W3)
    h = jnp.maximum(_layernorm(x, axis=-1), 0.0)
    x = x + _L1_gnn_ref(h, L1_gnn_k_linears, L1_gnn_q_linears, L1_gnn_v_linears, L1_gnn_a_linears, L1_gnn_relation_att, L1_gnn_relation_msg, L1_gnn_relation_pri, L1_gnn_skip, node_type_4, edge_type_8, src, dst)
    h = jnp.maximum(_layernorm(x, axis=-1), 0.0)
    x = x + _L2_gnn_ref(h, L2_gnn_relvectors, L2_gnn_w_ih, L2_gnn_w_hh, L2_gnn_b_ih, L2_gnn_b_hh, src, dst, edge_type_16)
    h = jnp.maximum(_layernorm(x, axis=-1), 0.0)
    x = x + _L3_gnn_ref(h, edge_weight, src, dst)
    return x

_drawn_inputs = setup_inputs


def setup_inputs(seed=0):
    import zlib

    import numpy as np

    out = dict(_drawn_inputs(seed))
    spreads = {'L1_gnn_relation_pri': (1.0, 0.6), 'L1_gnn_skip': (1.0, 0.6)}
    factors = {'L2_gnn_b_ih': 8.0, 'L2_gnn_b_hh': 8.0}
    for name, (base, spread) in spreads.items():
        noise = np.random.default_rng([zlib.crc32(name.encode()), seed]).standard_normal(out[name].shape)
        drawn = base * np.exp(spread * noise) if base else spread * noise
        out[name] = jnp.asarray(drawn.astype(out[name].dtype))
    for name, factor in factors.items():
        out[name] = (out[name] * factor).astype(out[name].dtype)
    return out
```

```python
from contextlib import ExitStack

import concourse.bass as bass
from concourse import mybir

ALU = mybir.AluOpType
ACT = mybir.ActivationFunctionType
F32 = mybir.dt.float32
F16 = mybir.dt.float16
BF16 = mybir.dt.bfloat16
I32 = mybir.dt.int32
AX_X = mybir.AxisListType.X

E, N, D = 50000, 3125, 256
PL = 125
NB = N // PL
EJ = E // PL
ET = 128
NP = (E + NB * (2 * ET - 1)) // (2 * ET)
RING = 8
ROUND = 2 * RING
NT = (2 * NP // ROUND + 1) * ROUND
NR, NH, DK, NTY, NE16 = 8, 4, 64, 4, 16
H1, H2 = 64, 32
EPS = 1e-5
MAGIC = 12582912.0
LROWS = (E // (PL * ET) + 1) * PL * ET
FAR = LROWS + 1.0
LOW = -1e30
AW = D + NE16


class Steps:

    def __init__(self, eng, sem):
        self.eng, self.sem, self.n, self.at = eng, sem, 0, 0

    def mark(self, ins):
        ins.then_inc(self.sem, 1)
        self.n += 1

    def settle(self):
        self.eng.wait_ge(self.sem, self.at + self.n)

    def then(self, ins):
        self.mark(ins)
        self.settle()

    def enter(self, i, per):
        self.outer, self.per = self.n, per
        self.at, self.n = self.outer + i * per, 0

    def leave(self, trips):
        assert self.n == self.per, (self.n, self.per)
        self.at, self.n = 0, self.outer + trips * self.per


class Carver:

    def __init__(self, tensor, at=0):
        self.tensor, self.at = tensor, at

    def take(self, lanes, *shape, dt=F32):
        words = 1
        for n in shape:
            words *= n
        words = (words + 1) // 2 if dt in (F16, BF16) else words
        assert self.at + words <= self.tensor.shape[1], (self.at, words)
        piece = self.tensor[0:lanes, self.at:self.at + words]
        self.at += words
        if dt != F32:
            piece = piece.bitcast(dt)
        names = "abcd"[:len(shape)]
        if len(shape) > 1:
            sizes = dict(zip(names, shape))
            piece = piece.rearrange(f"p ({' '.join(names)}) -> p {' '.join(names)}", **sizes)
        return piece


def build(nc, x_in, src_in, dst_in, r16_in, r8_in, ew_in, nty_in, w_in, w1t_in, w2t_in, w3t_in,
          wk_in, wq_in, wv_in, wa_in, att_in, msg_in, pri_in, skip_in, relt_in, wih_in, whh_in, bias_in, out):
    ctx = ExitStack()
    with ctx:
        def sb(name, shape, dt=F32):
            return ctx.enter_context(nc.sbuf_tensor(name, shape, dt))

        def sem(name):
            return ctx.enter_context(nc.semaphore(name))

        def dram(name, shape, dt=F32):
            return nc.dram_tensor(name, shape, dt).ap()

        ps = ctx.enter_context(nc.psum_tensor("ps", [128, 8, 512], F32))

        lane = sb("lane", [128, 1])
        col = sb("col", [128, NT])
        col16 = sb("col16", [128, NT], F16)
        ones = sb("ones", [PL, EJ])
        ident = sb("ident", [128, 128])
        identb = sb("identb", [128, 128], BF16)
        after = sb("after", [128, 128])
        after16 = sb("after16", [128, 128], F16)
        ones16 = sb("ones16", [128, 128], F16)
        zeros16 = sb("zeros16", [1, 512], F16)
        eps = sb("eps", [PL, 1])

        x = sb("x", [PL, NB, D])
        h = sb("h", [PL, NB, D])
        q = sb("q", [PL, NB, D])
        acc = sb("acc", [PL, NB, AW])
        m_all = sb("m_all", [PL, NB, NH])
        tmask = sb("tmask", [PL, NTY, NB])
        gmask = sb("gmask", [PL, NTY, NB])
        score = sb("score", [128, NT, NH])
        locA = sb("locA", [128, NT])
        idxA = sb("idxA", [128, NT], I32)
        locB = sb("locB", [128, NT])
        relB = sb("relB", [128, NT])
        idxR = sb("idxR", [128, NT], I32)
        idxS = sb("idxS", [128, NT], I32)
        pairsA = sb("pairsA", [PL, NB + 1], I32)
        pairsB = sb("pairsB", [PL, NB + 1], I32)
        roundsA = sb("roundsA", [PL, 1], I32)
        roundsB = sb("roundsB", [PL, 1], I32)
        rows = sb("rows", [128, RING, D])
        islot = sb("islot", [128, 2, RING], I32)
        wout = sb("wout", [128, 2, D])
        n_list = sb("n_list", [PL, 1], I32)

        st6 = sb("st6", [PL, NB, 6])
        mean = sb("mean", [PL, NB])
        var = sb("var", [PL, NB])
        std = sb("std", [PL, NB])
        rstd = sb("rstd", [PL, NB])
        shift = sb("shift", [PL, NB])
        half = sb("half", [PL, NB])

        w_sb = sb("w_sb", [PL, 1])
        w1t = sb("w1t", [128, 2, H1])
        w2t = sb("w2t", [H1, H2])
        w3t = sb("w3t", [H2, D])
        row_b = sb("row_b", [PL, D])
        rowT = sb("rowT", [128, 2, PL])
        h1T = sb("h1T", [H1, PL])
        h2T = sb("h2T", [H2, PL])

        arena = sb("arena", [128, 12288])
        c = Carver(arena)
        src_i, dst_i, r16_i, r8_i = (c.take(PL, EJ, dt=I32) for _ in range(4))
        ew = c.take(PL, EJ)
        rec = c.take(PL, EJ, 2)
        src, dst, r16, r8 = (c.take(PL, EJ) for _ in range(4))
        s_lane, s_tile, d_lane, d_tile = (c.take(PL, EJ) for _ in range(4))
        fa = c.take(PL, 2, EJ)
        fb = c.take(PL, 3, EJ)
        tmp, incl, pos, to_tile, to_lane = (c.take(PL, EJ) for _ in range(5))
        keyhot = c.take(PL, EJ, dt=F16)
        tilehot = c.take(PL, 4, NT, dt=F16)
        qc = Carver(q[:].rearrange("p b d -> p (b d)"))
        lanehot = qc.take(PL, 4, 3, ET, dt=F16)
        dest = qc.take(PL, EJ, dt=I32)
        dslot = qc.take(PL, 4, 1, dt=I32)
        rslot = qc.take(PL, 4, 2)
        base, rnd = qc.take(PL, 1), qc.take(PL, 1)
        rowoff = qc.take(PL, 2)
        fill = acc[0:PL, 0:4, :].rearrange("p a b -> p (a b)")[:, 0:LROWS * 2 // PL]
        sc = Carver(score[:].rearrange("p a b -> p (a b)"))
        dec, dec2 = sc.take(128, NT), sc.take(128, NT)

        c = Carver(arena)
        wk, wq, wv = (c.take(128, NTY, 2, D) for _ in range(3))
        wa_at = c.at
        wa = c.take(128, NTY, 2, D)
        bdk = c.take(128, 2, NR, 128)
        bdm = c.take(128, 2, NR, 128)
        ac = Carver(acc[:].rearrange("p b d -> p (b d)"))
        stage_k, stage_v = ac.take(PL, NR, D), ac.take(PL, NR, D)
        diag = sb("diag", [PL, NTY, PL])
        typedT = sb("typedT", [128, 2, NTY * PL])
        kvT = sb("kvT", [128, 4, PL])
        pri = sb("pri", [128, NR, NH])
        nty = sb("nty", [PL, NB], I32)
        skip = sb("skip", [PL, NTY])

        c = Carver(arena)
        hotT = c.take(128, 2, 128)
        neg = c.take(128, 2, 128, dt=BF16)
        prod = c.take(128, 2, D)
        s4 = c.take(128, 2, NH)
        sdiag = c.take(128, 2, NH, 128)
        wrow = c.take(128, 2, D + NH)
        m_run, m_new = c.take(128, NH), c.take(128, NH)
        den, rden = c.take(PL, NH), c.take(PL, NH)
        relhot = c.take(128, 2, NE16)
        sd4 = c.take(128, 2, NH)
        hot = sb("hot", [128, 2, 128])
        col1 = sb("col1", [128, 128])
        assert c.at <= wa_at
        c_edges = c.at
        c = Carver(arena, wa_at + NTY * 2 * D)
        wih = c.take(128, 2, 3 * D)
        whh = c.take(128, 2, 3 * D)
        relw = c.take(NE16 + 1, 3 * D)
        c = Carver(arena, c_edges)
        bhn = c.take(NE16 + 1, D)
        relt = c.take(128, 2, NE16 + 1)
        bias = c.take(2, 3 * D)
        pick, pick_h = c.take(2, NE16 + 1), c.take(2, NE16 + 1)
        gT = c.take(128, 4, PL)
        cntT = c.take(NE16 + 1, PL)
        accrow = c.take(PL, AW + 1)
        rz, gn, gt = c.take(PL, 2 * D), c.take(PL, D), c.take(PL, D)
        assert c.at <= wa_at
        lrec = sb("lrec", [128, 2])
        lsd = sb("lsd", [128, 4])
        leq = sb("leq", [128, 128])
        ldiag = sb("ldiag", [128, 128])
        ones128 = sb("ones128", [128, 128])
        lS = rows[:, 0, :]
        lVC = rows[:, 1:3, :]
        lcov = rows[:, 3:5, :]

        elist = dram("elist", [LROWS, 2])
        tab_h0 = dram("tab_h0", [N, D])
        tab_h2 = dram("tab_h2", [N, D])
        tab_k = dram("tab_k", [N * NR, D])
        tab_v = dram("tab_v", [N * NR, D])

        edges_in, x_in_s, small_in, attn_in, gru_in = (sem(n) for n in ("edges_in", "x_in_s", "small_in", "attn_in", "gru_in"))
        dve_step, act_step = sem("dve_step"), sem("act_step")
        cols_made, consts = sem("cols_made"), sem("consts")
        key_ready, key_counted = sem("key_ready"), sem("key_counted")
        tot_ready, tot_summed = sem("tot_ready"), sem("tot_summed")
        hot_ready, hot_placed = sem("hot_ready"), sem("hot_placed")
        sorted_by = sem("sorted_by")
        fill_done, list_filled, dest_ready, slot_ready = (sem(n) for n in ("fill_done", "list_filled", "dest_ready", "slot_ready"))
        scattered = [sem(f"scattered{n}") for n in range(4)]
        var_ready, std_ready, rstd_ready, h_rows = (sem(n) for n in ("var_ready", "std_ready", "rstd_ready", "h_rows"))
        table_out, base_ready = sem("table_out"), sem("base_ready")
        landed = [[sem(f"landed{s}_{n}") for n in range(RING)] for s in range(2)]
        row_ready = [sem(f"row_ready{s}") for s in range(4)]
        row_used = [sem(f"row_used{s}") for s in range(4)]
        pool_pass, pe_pass, dve_pass = sem("pool_pass"), sem("pe_pass"), sem("dve_pass")
        islot_ready = [sem(f"islot_ready{s}") for s in range(4)]
        ring_idle = sem("ring_idle")
        hot_made = [sem(f"hot_made{s}") for s in range(4)]
        bucket_summed = [sem(f"bucket_summed{s}") for s in range(4)]
        bucket_read = [sem(f"bucket_read{s}") for s in range(4)]
        y_ready, y_turned, yT_ready, h1_made, h1_relu, h2_made, h2_relu, o_made, n1_step = (
            sem(n) for n in ("y_ready", "y_turned", "yT_ready", "h1_made", "h1_relu", "h2_made", "h2_relu", "o_made", "n1_step"))
        l_in, l_dve, l_pe, l_act, l_w = (sem(n) for n in ("l_in", "l_dve", "l_pe", "l_act", "l_w"))
        blocks_cleared, hrow_ready, diag_made, typed_turned, typedT_ready, kvq_made, kvT_ready, q_copied = (
            sem(n) for n in ("blocks_cleared", "hrow_ready", "diag_made", "typed_turned", "typedT_ready", "kvq_made", "kvT_ready", "q_copied"))
        bank_full, bank_read_a, bank_read_v, tabs_out, stage_free = (
            sem(n) for n in ("bank_full", "bank_read_a", "bank_read_v", "tabs_out", "stage_free"))
        hot_turned = [None] + [sem(f"hot_turned{s}") for s in (1, 2)]
        hotT_made = [None] + [sem(f"hotT_made{s}") for s in (1, 2)]
        tile_done = [None] + [sem(f"tile_done{s}") for s in (1, 2)]
        q_edge, s_ready, sdiag_ready, max_read, m_step, m_bucket = (
            sem(n) for n in ("q_edge", "s_ready", "sdiag_ready", "max_read", "m_step", "m_bucket"))
        m_edge, sd_ready, ex_ready = (sem(n) for n in ("m_edge", "sd_ready", "ex_ready"))
        agg_ready, agg_turned, aggT_ready, att_made, n3_step = (
            sem(n) for n in ("agg_ready", "agg_turned", "aggT_ready", "att_made", "n3_step"))
        relt_cleared, relw_made, relw_ready, g_rows, g_turned, gT_ready, cntT_ready, gates_made = (
            sem(n) for n in ("relt_cleared", "relw_made", "relw_ready", "g_rows", "g_turned", "gT_ready", "cntT_ready", "gates_made"))
        rz_ready, gt_ready, gn_ready, gru_done, n5_step = (
            sem(n) for n in ("rz_ready", "gt_ready", "gn_ready", "gru_done", "n5_step"))
        gate_ready, score_kept = sem("gate_ready"), sem("score_kept")
        f_row, f_turned, fT_ready, f_made, out_ready = (sem(n) for n in ("f_row", "f_turned", "fT_ready", "f_made", "out_ready"))
        out_done = sem("out_done")

        block = ctx.enter_context(nc.Block())

        def flat(ap):
            return ap.rearrange("p a b -> p (a b)")

        def bounds(eng, pairs, b):
            lo = eng.value_load(pairs[0:1, bass.ds(b, 1)], min_val=0, max_val=NP)
            hi = eng.value_load(pairs[0:1, bass.ds(b + 1, 1)], min_val=0, max_val=NP)
            return lo, hi

        def spare_rows(eng, s, pairs, rings):
            first = eng.value_load(pairs[0:1, NB:NB + 1], min_val=1, max_val=NP)
            rounds = eng.value_load(rings[0:1, 0:1], min_val=1, max_val=NT // ROUND)
            with eng.Fori(first * 2, rounds * ROUND) as t:
                eng.wait_ge(row_used[s], t + RING)
                eng.wait_ge(row_ready[s], t + 1)
                eng.sem_inc(row_used[s], 1)

        def pairs_in_all(eng, pairs):
            return eng.value_load(pairs[0:1, NB:NB + 1], min_val=1, max_val=NP)

        @block.sync
        def _(sp):
            for t, a in ((src_i, src_in), (dst_i, dst_in), (r16_i, r16_in), (r8_i, r8_in), (ew, ew_in)):
                sp.dma_start(t, a.rearrange("(p j) -> p j", p=PL)).then_inc(edges_in, 16)
            sp.dma_start(x[:], x_in.rearrange("(p b) d -> p b d", p=PL)).then_inc(x_in_s, 16)
            sp.dma_start(nty[:], nty_in.rearrange("(p b) -> p b", p=PL)).then_inc(small_in, 16)
            sp.dma_start(w_sb[:], w_in.rearrange("(a b) -> a b", a=1).broadcast_to([PL, 1])).then_inc(small_in, 16)
            sp.dma_start(w1t[:], w1t_in.rearrange("(c p) n -> p c n", p=128)).then_inc(small_in, 16)
            sp.dma_start(w2t[:], w2t_in).then_inc(small_in, 16)
            sp.dma_start(w3t[:], w3t_in).then_inc(small_in, 16)
            sp.dma_start(pri[:], pri_in.rearrange("(a r) h -> a (r h)", a=1).broadcast_to([128, NR * NH]).rearrange("p (r h) -> p r h", r=NR)).then_inc(small_in, 16)
            sp.dma_start(skip[:], skip_in.rearrange("(a t) -> a t", a=1).broadcast_to([PL, NTY])).then_inc(small_in, 16)
            sp.wait_ge(fill_done, 1)
            sp.dma_start(elist.rearrange("(p c) k -> p (c k)", p=PL), fill).then_inc(list_filled, 16)

            def write_table(tab):
                sp.dma_start(tab.rearrange("(p b) d -> p b d", p=PL), h[:]).then_inc(table_out, 16)

            def relay(s, rings):
                count = sp.value_load(rings[0:1, 0:1], min_val=1, max_val=NT // ROUND)
                past = count * max(s - 1, 0) if s > 1 else 0
                with sp.Fori(past, past + count) as i:
                    for n in range(ROUND):
                        sp.wait_ge(landed[min(s, 1)][n % RING], i * 32 + 16 * (n // RING + 1))
                        sp.sem_inc(row_ready[s], 1)
                sp.sem_inc(ring_idle, 1)

            sp.wait_ge(h_rows, NB)
            write_table(tab_h0)
            sp.wait_ge(sorted_by, 1)
            relay(0, roundsA)
            sp.wait_ge(sorted_by, 2)
            for n in range(4):
                sp.wait_ge(scattered[n], 16 * EJ // 4)
            for t, a in ((wk, wk_in), (wq, wq_in), (wv, wv_in), (wa, wa_in)):
                for k in range(NTY):
                    sp.dma_start(t[:, k], a[k].rearrange("(c p) n -> p c n", p=128)).then_inc(attn_in, 16)
            sp.wait_ge(blocks_cleared, 1)
            for t, a in ((bdk, att_in), (bdm, msg_in)):
                for two in range(2):
                    for cc in range(2):
                        sp.dma_start(t[64 * two:64 * two + 64, cc, :, 64 * two:64 * two + 64],
                                     a[:, 2 * cc + two]).then_inc(attn_in, 16)
            n_l = sp.value_load(n_list[0:1, 0:1], min_val=1, max_val=LROWS // ET)
            with sp.Fori(0, n_l) as t:
                sp.wait_ge(l_w, t + 1)
                sp.dma_start(lrec[:].rearrange("p (a k) -> p a k", a=1),
                             elist.rearrange("(t p) k -> p t k", p=ET)[:, bass.ds(t, 1), :]).then_inc(l_in, 16)
            sp.sem_inc(stage_free, 1)
            with sp.Fori(0, NB) as b:
                sp.wait_ge(bank_read_a, b * 4 + 6)
                sp.wait_ge(bank_read_v, b * 4 + 6)
                for tab, stg in ((tab_k, stage_k), (tab_v, stage_v)):
                    sp.dma_start(tab.rearrange("(p b r) d -> p b (r d)", p=PL, r=NR)[:, bass.ds(b, 1), :],
                                 stg.rearrange("p (a r) n -> p a (r n)", a=1)).then_inc(tabs_out, 16)
                sp.wait_ge(tabs_out, b * 32 + 32)
                sp.sem_inc(stage_free, 1)
            sp.wait_ge(tabs_out, 32 * NB)
            sp.dma_start(wih, wih_in.rearrange("(c p) n -> p c n", p=128)).then_inc(gru_in, 16)
            sp.dma_start(whh, whh_in.rearrange("(c p) n -> p c n", p=128)).then_inc(gru_in, 16)
            sp.wait_ge(relt_cleared, 1)
            sp.dma_start(relt[:, :, 0:NE16], relt_in.rearrange("(c p) n -> p c n", p=128)).then_inc(gru_in, 16)
            sp.dma_start(bias, bias_in).then_inc(gru_in, 16)
            relay(1, roundsB)
            relay(2, roundsB)
            sp.wait_ge(h_rows, 3 * NB)
            write_table(tab_h2)
            relay(3, roundsB)
            with sp.Fori(0, NB) as b:
                sp.wait_ge(out_ready, b + 2)
                sp.dma_start(out.rearrange("(p b) d -> p b d", p=PL)[:, bass.ds(b, 1), :], x[:, bass.ds(b, 1), :]).then_inc(out_done, 16)
            sp.wait_ge(out_done, 16 * NB)
            sp.wait_ge(tabs_out, 32 * NB)
            sp.wait_ge(table_out, 32)
            sp.wait_ge(list_filled, 16)

        @block.gpsimd
        def _(pool):
            nc.gpsimd.iota(lane[:], [[0, 1]], base=0, channel_multiplier=1, allow_small_or_imprecise_dtypes=True)
            nc.gpsimd.iota(col[:], [[1, NT]], base=0, channel_multiplier=0,
                           allow_small_or_imprecise_dtypes=True).then_inc(cols_made, 1)
            nc.gpsimd.memset(fill, -1.0).then_inc(fill_done, 1)
            for s in range(4):
                pool.sem_inc(row_used[s], RING)

            pool.wait_ge(list_filled, 16)
            with pool.Fori(0, EJ // 4) as i:
                for n in range(4):
                    pool.wait_ge(slot_ready, i * 4 + (n + 1))
                    pool.sem_inc(pool_pass, 1)
                    pool.indirect_dma_start(
                        out=elist, out_offset=bass.IndirectOffsetOnAxis(ap=dslot[:, n, :], axis=0),
                        in_=rslot[:, n, :], in_offset=None, bounds_check=LROWS - 1, oob_is_err=False,
                    ).then_inc(scattered[n], 16)

            def gather(s, table, idx, rings):
                count = pool.value_load(rings[0:1, 0:1], min_val=1, max_val=NT // ROUND)
                with pool.Fori(0, count) as i:
                    for g in range(2):
                        pool.wait_ge(row_used[s], i * ROUND + (RING * g + 1))
                        pool.sem_inc(pool_pass, 1)
                        nc.gpsimd.tensor_copy(islot[:, g, :], idx[:, bass.ds(i * ROUND + RING * g, RING)]).then_inc(islot_ready[s], 1)
                        pool.wait_ge(islot_ready[s], i * 2 + (g + 1))
                        for n in range(RING):
                            pool.wait_ge(row_used[s], i * ROUND + (RING * g + n + 1))
                            pool.sem_inc(pool_pass, 1)
                            pool.indirect_dma_start(
                                out=rows[:, n, :], out_offset=None, in_=table,
                                in_offset=bass.IndirectOffsetOnAxis(ap=islot[:, g, n:n + 1], axis=0),
                            ).then_inc(landed[min(s, 1)][n], 16)
                pool.wait_ge(row_used[s], count * ROUND + RING)
                pool.sem_inc(pool_pass, 1)

            pool.wait_ge(sorted_by, 1)
            pool.wait_ge(table_out, 16)
            gather(0, tab_h0, idxA, roundsA)
            pool.wait_ge(ring_idle, 1)
            pool.wait_ge(tabs_out, 32 * NB)
            gather(1, tab_k, idxR, roundsB)
            pool.wait_ge(ring_idle, 2)
            gather(2, tab_v, idxR, roundsB)
            pool.wait_ge(ring_idle, 3)
            pool.wait_ge(table_out, 32)
            gather(3, tab_h2, idxS, roundsB)

        @block.vector
        def _(dve):
            st = Steps(dve, dve_step)
            V = nc.vector

            def rounded(out, x, shift, scale):
                st.then(V.tensor_scalar(out, x, shift, scale, ALU.add, ALU.mult))
                st.then(V.tensor_scalar(out, out, MAGIC, -MAGIC, ALU.add, ALU.add))

            def axpy(out, x, a, y):
                st.then(V.scalar_tensor_tensor(out, x, a, y, ALU.mult, ALU.add))

            def norm(k):
                st.settle()
                st.then(V.tensor_tensor(mean[:], st6[:, :, 1], st6[:, :, 4], ALU.add))
                V.tensor_scalar(mean[:], mean[:], 0.5, None, ALU.mult)
                V.tensor_tensor(half[:], st6[:, :, 1], st6[:, :, 4], ALU.subtract)
                st.then(V.tensor_tensor(var[:], st6[:, :, 2], st6[:, :, 5], ALU.add))
                st.then(V.tensor_tensor(half[:], half[:], half[:], ALU.mult))
                st.then(V.tensor_scalar(half[:], half[:], 0.25, None, ALU.mult))
                V.scalar_tensor_tensor(var[:], var[:], 1.0 / D, half[:], ALU.mult, ALU.add).then_inc(var_ready, 1)
                dve.wait_ge(std_ready, k)
                st.then(V.reciprocal(rstd[:], std[:]))
                V.scalar_tensor_tensor(shift[:], mean[:], -1.0, rstd[:], ALU.mult, ALU.mult).then_inc(rstd_ready, 1)

            dve.wait_ge(cols_made, 1)
            V.tensor_copy(col16[:], col[:])
            V.memset(ones[:], 1.0)
            V.memset(ones16[:], 1.0)
            V.memset(ones128[:], 1.0)
            V.memset(zeros16[:], 0.0)
            V.memset(eps[:], EPS)
            V.memset(wout[:], 0.0)
            V.tensor_scalar(col1[:], col[:, 0:128], 1.0, None, ALU.add)
            V.tensor_scalar(ident[:], col[:, 0:128], lane[:, 0:1], None, ALU.is_equal)
            V.tensor_scalar(identb[:], col[:, 0:128], lane[:, 0:1], None, ALU.is_equal)
            V.tensor_scalar(after[:], col[:, 0:128], lane[:, 0:1], None, ALU.is_gt)
            V.tensor_scalar(after16[:], col[:, 0:128], lane[:, 0:1], -1.0, ALU.is_gt, ALU.add).then_inc(consts, 1)
            dve.wait_ge(consts, 1)
            dve.wait_ge(edges_in, 80)
            V.tensor_copy(src, src_i)
            V.tensor_copy(dst, dst_i)
            V.tensor_copy(r16, r16_i)
            V.tensor_copy(rec[:, :, 1], ew)
            st.then(V.tensor_copy(r8, r8_i))
            st.then(V.tensor_scalar(tmp, dst, float(D), None, ALU.is_lt))
            st.then(V.scalar_tensor_tensor(tmp, src, float(D), tmp, ALU.is_lt, ALU.mult))
            axpy(rec[:, :, 0], src, float(D), dst)
            V.tensor_tensor_scan(incl, ones[:], tmp, 0.0, ALU.mult, ALU.add).then_inc(tot_ready, 1)
            dve.wait_ge(tot_ready, 1)
            dve.wait_ge(tot_summed, 1)
            V.tensor_scalar(rowoff[:, 0:1], ps[0:PL, 0, 0:1], -1.0 - FAR, None, ALU.add)
            rounded(rowoff[:, 1:2], ps[0:PL, 0, 1:2], (ET - 1) / 2.0, 1.0 / ET)
            V.scalar_tensor_tensor(incl, incl, rowoff[:, 0:1], tmp, ALU.add, ALU.mult)
            st.then(V.tensor_scalar(n_list[:], rowoff[:, 1:2], 1.0, None, ALU.max))
            V.tensor_scalar(dest, incl, FAR, None, ALU.add).then_inc(dest_ready, 1)

            rounded(s_lane, src, -float(NB // 2), 1.0 / NB)
            axpy(s_tile, s_lane, -float(NB), src)
            rounded(d_lane, dst, -float(NB // 2), 1.0 / NB)
            axpy(d_tile, d_lane, -float(NB), dst)
            rounded(fa[:, 1, :], dst, -3.5, 1.0 / 8)
            axpy(tmp, fa[:, 1, :], -8.0, dst)
            st.then(V.tensor_scalar(tmp, tmp, 256.0, 1.0, ALU.mult, ALU.add))
            st.then(V.tensor_tensor(fa[:, 0, :], tmp, s_lane, ALU.add))
            axpy(tmp, r16, 128.0, d_lane)
            st.then(V.tensor_scalar(fb[:, 0, :], tmp, 1.0, None, ALU.add))
            axpy(tmp, src, float(NR), r8)
            rounded(fb[:, 1, :], tmp, -7.5, 1.0 / 16)
            axpy(fb[:, 2, :], fb[:, 1, :], -16.0, tmp)

            dve.wait_ge(x_in_s, 16)
            with dve.Fori(0, NB) as b:
                st.enter(b, 1)
                st.mark(V.bn_stats(st6[:, bass.ds(b, 1), :], x[:, bass.ds(b, 1), :]))
                st.leave(NB)
            norm(1)

            def rank(which, key, pairs, rings):
                V.memset(pos, 0.0)
                V.memset(pairs[:, 0:1], 0)
                st.then(V.memset(base, 0.0))
                with dve.Fori(0, NB) as b:
                    st.enter(b, 8)
                    V.tensor_scalar(keyhot, key, col[0:PL, bass.ds(b, 1)], None, ALU.is_equal).then_inc(key_ready, 1)
                    dve.wait_ge(key_counted, b + (1 + which * NB))
                    st.then(V.tensor_tensor_scan(incl, ones[:], ps[0:PL, 0, 0:EJ], 0.0, ALU.mult, ALU.add))
                    st.then(V.tensor_tensor(tmp, incl, ps[0:PL, 1, 0:EJ], ALU.add))
                    st.then(V.scalar_tensor_tensor(tmp, tmp, base, keyhot, ALU.add, ALU.mult))
                    st.mark(V.tensor_tensor(pos, pos, tmp, ALU.add))
                    st.then(V.tensor_scalar(rnd, incl[:, EJ - 1:EJ], ET - 0.5, 0.5 / ET, ALU.add, ALU.mult))
                    st.then(V.tensor_scalar(rnd, rnd, MAGIC, MAGIC + 1.0, ALU.add, ALU.max))
                    st.then(V.tensor_scalar(rnd, rnd, -MAGIC, 2.0 * ET, ALU.add, ALU.mult))
                    V.tensor_tensor(base, base, rnd, ALU.add).then_inc(base_ready, 1)
                    dve.wait_ge(base_ready, b + (1 + which * NB))
                    st.then(V.tensor_scalar(pairs[:, bass.ds(b + 1, 1)], base, 0.5 / ET, None, ALU.mult))
                    st.leave(NB)
                rounded(rnd, base, (ROUND // 2 + 1.0) * ET, 1.0 / (ROUND * ET))
                V.tensor_copy(rings[:], rnd)
                rounded(to_tile, pos, -(ET - 1) / 2.0, 1.0 / ET)
                axpy(to_lane, to_tile, -float(ET), pos)

            def place(which, fields, nf):
                def hots(n, j):
                    V.tensor_scalar(tilehot[:, n, :], col16[0:PL, :], to_tile[:, j], None, ALU.is_equal)
                    for f in range(nf):
                        last = V.tensor_scalar(lanehot[:, n, f, :], col16[0:PL, 0:ET], to_lane[:, j], fields[:, f, j],
                                               ALU.is_equal, ALU.mult)
                    last.then_inc(hot_ready, 1)

                for n in range(4):
                    hots(n, slice(n, n + 1))
                with dve.Fori(1, EJ // 4) as i:
                    for n in range(4):
                        dve.wait_ge(hot_placed, i * 4 + (n + which * EJ - 3))
                        hots(n, bass.ds(i * 4 + n, 1))
                dve.wait_ge(hot_placed, (which + 1) * EJ)

            rank(0, s_tile, pairsA, roundsA)
            place(0, fa, 2)
            rounded(dec, ps[:, 2, 0:NT], -64.0, 1.0 / 256)
            axpy(locA[:], dec, -256.0, ps[:, 2, 0:NT])
            axpy(dec, ps[:, 3, 0:NT], 8.0, dec)
            V.tensor_copy(idxA[:], dec).then_inc(sorted_by, 1)
            st.settle()
            dve.wait_ge(sorted_by, 1)

            def edge_hots(s, loc, n, t):
                if s in (1, 2):
                    dve.wait_ge(tile_done[s], t + 1)
                else:
                    dve.wait_ge(row_used[s], t + (RING - 1))
                V.tensor_scalar(hot[:, n, :], col1[:], loc[:, bass.ds(t, 1)], None, ALU.is_equal).then_inc(hot_made[s], 1)

            with dve.Fori(0, NB) as b:
                lo, hi = bounds(dve, pairsA, b)
                with dve.Fori(lo, hi) as P:
                    for n in range(2):
                        edge_hots(0, locA, n, P * 2 + n)

            rank(1, d_tile, pairsB, roundsB)
            place(1, fb, 3)
            rounded(relB[:], ps[:, 2, 0:NT], -62.5, 1.0 / 128)
            axpy(locB[:], relB[:], -128.0, ps[:, 2, 0:NT])
            st.then(V.tensor_copy(dec2, ps[:, 4, 0:NT]))
            axpy(dec2, ps[:, 3, 0:NT], 16.0, dec2)
            V.tensor_copy(idxR[:], dec2)
            rounded(dec, dec2, -3.5, 1.0 / NR)
            V.tensor_copy(idxS[:], dec).then_inc(sorted_by, 1)
            st.settle()
            dve.wait_ge(sorted_by, 2)

            V.memset(bdk, 0.0)
            V.memset(bdm, 0.0).then_inc(blocks_cleared, 1)

            dve.wait_ge(small_in, 16 * 7)
            dve.wait_ge(bucket_read[0], NB + 1)
            with dve.Fori(0, NB) as b:
                bb = bass.ds(b, 1)
                V.scalar_tensor_tensor(row_b[:], flat(h[:, bb, :]), w_sb[:, 0:1], flat(acc[:, bb, 0:D]),
                                       ALU.mult, ALU.add).then_inc(y_ready, 1)
                dve.wait_ge(o_made, b + 1)
                V.scalar_tensor_tensor(row_b[:], ps[0:PL, 3, 0:D], 0.0, flat(h[:, bb, :]), ALU.max, ALU.add).then_inc(n1_step, 1)
                dve.wait_ge(n1_step, b * 3 + 1)
                V.tensor_tensor(flat(x[:, bb, :]), flat(x[:, bb, :]), row_b[:], ALU.add).then_inc(n1_step, 1)
                dve.wait_ge(n1_step, b * 3 + 2)
                V.bn_stats(flat(st6[:, bb, :]), flat(x[:, bb, :])).then_inc(n1_step, 1)
            dve.wait_ge(n1_step, NB * 3)
            norm(2)

            n_l = dve.value_load(n_list[0:1, 0:1], min_val=1, max_val=LROWS // ET)
            dve.wait_ge(ring_idle, 1)
            dve.sem_inc(l_w, 1)
            with dve.Fori(0, n_l) as t:
                def seq(k, ins):
                    ins.then_inc(l_dve, 1)
                    dve.wait_ge(l_dve, t * 8 + k)
                dve.wait_ge(l_in, t * 16 + 16)
                seq(1, V.tensor_scalar(ldiag[:], ident[:], lrec[:, 0:1], None, ALU.mult))
                seq(2, V.tensor_scalar(lsd[:, 0:1], lrec[:, 0:1], -(D - 1) / 2.0, 1.0 / D, ALU.add, ALU.mult))
                seq(3, V.tensor_scalar(lsd[:, 0:1], lsd[:, 0:1], MAGIC, -MAGIC, ALU.add, ALU.add))
                seq(4, V.scalar_tensor_tensor(lsd[:, 1:2], lsd[:, 0:1], -float(D), lrec[:, 0:1], ALU.mult, ALU.add))
                dve.wait_ge(l_pe, t * 2 + 1)
                seq(5, V.scalar_tensor_tensor(leq[:], ps[:, 0, 0:128], lrec[:, 0:1], after[:], ALU.is_equal, ALU.mult))
                seq(6, V.tensor_reduce(lsd[:, 2:3], leq[:], AX_X, ALU.max))
                seq(7, V.tensor_scalar(lsd[:, 3:4], lsd[:, 2:3], -1.0, 1.0, ALU.mult, ALU.add))
                V.tensor_scalar(lS, col[:, 0:D], lsd[:, 0:1], lsd[:, 3:4], ALU.is_equal, ALU.mult)
                V.tensor_scalar(lVC[:, 0, :], col[:, 0:D], lsd[:, 1:2], lrec[:, 1:2], ALU.is_equal, ALU.mult)
                seq(8, V.tensor_scalar(lVC[:, 1, :], col[:, 0:D], lsd[:, 1:2], None, ALU.is_equal))
                dve.wait_ge(l_act, t + 1)
                dve.sem_inc(dve_pass, 1)
                V.copy_predicated(wout[:, 0, :], lcov[:, 0, :].bitcast(I32), ps[:, 1, 0:D])
                V.copy_predicated(wout[:, 1, :], lcov[:, 1, :].bitcast(I32), ps[:, 2, 0:D]).then_inc(l_w, 1)
                dve.wait_ge(l_w, t + 2)

            dve.wait_ge(attn_in, 16 * (4 * NTY + 8))
            st.then(V.tensor_copy(half[:], nty[:]))
            st.then(V.tensor_scalar(pri[:], pri[:], DK ** -0.5, None, ALU.mult))
            dve.wait_ge(gate_ready, 1)
            for k in range(NTY):
                st.then(V.tensor_scalar(tmask[:, k, :], half[:], float(k), None, ALU.is_equal))
                V.tensor_scalar(gmask[:, k, :], tmask[:, k, :], skip[:, k:k + 1], None, ALU.mult)
            for cc in range(2):
                for two in range(2):
                    blk = bdk[:, cc, :, 64 * two:64 * two + 64]
                    st.mark(V.tensor_tensor(blk, blk, pri[:, :, 2 * cc + two:2 * cc + two + 1].broadcast_to([128, NR, 64]), ALU.mult))
            st.settle()

            with dve.Fori(0, NB) as b:
                bb = bass.ds(b, 1)
                dve.wait_ge(typed_turned, b + 1)
                for k in range(NTY):
                    last = V.tensor_scalar(diag[:, k, :], ident[0:PL, 0:PL], tmask[:, k, bb], None, ALU.mult)
                last.then_inc(diag_made, 1)
                dve.wait_ge(kvq_made, b + 1)
                V.tensor_copy(flat(q[:, bb, :]), ps[0:PL, 0, 0:D]).then_inc(q_copied, 1)
                dve.wait_ge(stage_free, b + 1)
                for g in range(4):
                    dve.wait_ge(bank_full, b * 8 + (2 * g + 3))
                    V.tensor_copy((stage_k, stage_v)[g // 2][:, 4:8, 128 * (g % 2):128 * (g % 2) + 128],
                                  ps[0:PL, 4 + (2 * g + 1) % 4, :].rearrange("p (r n) -> p r n", r=4)).then_inc(bank_read_v, 1)

            dve.wait_ge(tabs_out, 32 * NB)
            V.memset(relt, 0.0).then_inc(relt_cleared, 1)
            st.then(V.memset(pick, 0.0))
            st.then(V.memset(pick[:, NE16:NE16 + 1], 1.0))
            V.tensor_scalar(pick_h, pick, lane[0:2, 0:1], None, ALU.mult)
            st.then(V.memset(accrow[:, AW:AW + 1], 1.0))

            with dve.Fori(0, NB) as b:
                bb = bass.ds(b, 1)
                lo, hi = bounds(dve, pairsB, b)
                V.memset(m_run, LOW).then_inc(m_bucket, 1)
                dve.wait_ge(m_bucket, b * 2 + 1)
                dve.sem_inc(dve_pass, 1)
                with dve.Fori(lo, hi) as P:
                    for n in range(2):
                        edge_hots(1, locB, n, P * 2 + n)
                    for n in range(2):
                        t = P * 2 + n
                        dve.wait_ge(q_edge, t + 1)
                        dve.wait_ge(row_ready[1], t + 1)
                        V.tensor_tensor(prod[:, n, :], ps[:, 2 + n, 0:D], flat(rows[:, bass.ds(P % (RING // 2) * 2 + n, 1), :]),
                                        ALU.mult).then_inc(row_used[1], 1)
                        dve.wait_ge(row_used[1], t + (RING + 1))
                        V.tensor_reduce(s4[:, n, :], prod[:, n, :].rearrange("p (h d) -> p h d", h=NH), AX_X, ALU.add).then_inc(s_ready, 1)
                    for n in range(2):
                        t = P * 2 + n
                        dve.wait_ge(tile_done[1], t + 3)
                        V.tensor_reduce(m_new[0:PL, :], ps[0:PL, 4 + n, :].rearrange("p (h e) -> p h e", h=NH), AX_X, ALU.max).then_inc(max_read, 1)
                        dve.wait_ge(max_read, t + 3)
                        V.tensor_tensor(m_run[0:PL, :], m_run[0:PL, :], m_new[0:PL, :], ALU.max).then_inc(m_step, 1)
                        dve.wait_ge(m_step, t + 1)
                V.tensor_copy(flat(m_all[:, bb, :]), m_run[0:PL, :]).then_inc(m_bucket, 1)
                dve.wait_ge(m_bucket, b * 2 + 2)

            spare_rows(dve, 1, pairsB, roundsB)
            with dve.Fori(0, NB) as b:
                bb = bass.ds(b, 1)
                lo, hi = bounds(dve, pairsB, b)
                with dve.Fori(lo, hi) as P:
                    for n in range(2):
                        edge_hots(2, locB, n, P * 2 + n)
                    for n in range(2):
                        t = P * 2 + n
                        dve.wait_ge(m_edge, t + 1)
                        V.tensor_tensor(sd4[:, n, :], flat(score[:, bass.ds(t, 1), :]), ps[:, 2 + n, 0:NH], ALU.subtract).then_inc(sd_ready, 1)
                    for n in range(2):
                        t = P * 2 + n
                        dve.wait_ge(ex_ready, t + 1)
                        dve.wait_ge(row_ready[2], t + 1)
                        V.tensor_tensor(wrow[:, n, 0:D].rearrange("p (h d) -> p h d", h=NH),
                                        flat(rows[:, bass.ds(P % (RING // 2) * 2 + n, 1), :]).rearrange("p (h d) -> p h d", h=NH),
                                        wrow[:, n, D:D + NH].rearrange("p (h a) -> p h a", a=1).broadcast_to([128, NH, DK]),
                                        ALU.mult).then_inc(row_used[2], 1)
                dve.wait_ge(bucket_summed[2], b + 1)
                V.tensor_copy(flat(acc[:, bb, 0:D + NH]), ps[0:PL, 7, 0:D + NH]).then_inc(bucket_read[2], 1)
            spare_rows(dve, 2, pairsB, roundsB)
            dve.wait_ge(bucket_read[2], NB + 1)

            with dve.Fori(0, NB) as b:
                bb = bass.ds(b, 1)
                V.tensor_scalar(den, flat(acc[:, bb, D:D + NH]), 1e-30, None, ALU.max).then_inc(n3_step, 1)
                dve.wait_ge(n3_step, b * 5 + 1)
                V.reciprocal(rden, den).then_inc(n3_step, 1)
                dve.wait_ge(n3_step, b * 5 + 2)
                dve.wait_ge(agg_turned, b + 1)
                V.tensor_tensor(row_b[:].rearrange("p (h d) -> p h d", h=NH), flat(acc[:, bb, 0:D]).rearrange("p (h d) -> p h d", h=NH),
                                rden.rearrange("p (h a) -> p h a", a=1).broadcast_to([PL, NH, DK]), ALU.mult).then_inc(n3_step, 1)
                for k in range(NTY):
                    last = V.tensor_scalar(diag[:, k, :], ident[0:PL, 0:PL], gmask[:, k, bb], None, ALU.mult)
                last.then_inc(agg_ready, 1)
                dve.wait_ge(n3_step, b * 5 + 3)
                dve.wait_ge(att_made, b + 1)
                V.tensor_tensor(flat(x[:, bb, :]), flat(x[:, bb, :]), ps[0:PL, 0, 0:D], ALU.add).then_inc(n3_step, 1)
                dve.wait_ge(n3_step, b * 5 + 4)
                V.bn_stats(flat(st6[:, bb, :]), flat(x[:, bb, :])).then_inc(n3_step, 1)
            dve.wait_ge(n3_step, NB * 5)
            norm(3)

            with dve.Fori(0, NB) as b:
                lo, hi = bounds(dve, pairsB, b)
                with dve.Fori(lo, hi) as P:
                    for n in range(2):
                        t = P * 2 + n
                        dve.wait_ge(row_used[3], t + (RING - 1))
                        V.tensor_scalar(relhot[:, n, :], col[:, 0:NE16], relB[:, bass.ds(t, 1)], None, ALU.is_equal)
                        edge_hots(3, locB, n, t)

            dve.wait_ge(bucket_read[3], NB + 1)
            with dve.Fori(0, NB) as b:
                bb = bass.ds(b, 1)

                def seq(k, ins):
                    ins.then_inc(n5_step, 1)
                    dve.wait_ge(n5_step, b * 6 + k)
                dve.wait_ge(g_turned, b + 2)
                V.tensor_copy(flat(gT), ps[:, 1, 0:4 * PL]).then_inc(gT_ready, 1)
                dve.wait_ge(rz_ready, b + 1)
                seq(1, V.tensor_tensor(gt, rz[:, 0:D], ps[0:PL, 5, 0:D], ALU.mult))
                V.tensor_tensor(gt, gt, ps[0:PL, 4, 0:D], ALU.add).then_inc(gt_ready, 1)
                dve.wait_ge(gn_ready, b + 1)
                seq(2, V.tensor_tensor(gt, flat(h[:, bb, :]), gn, ALU.subtract))
                seq(3, V.tensor_tensor(gt, gt, rz[:, D:2 * D], ALU.mult))
                seq(4, V.tensor_tensor(gt, gt, gn, ALU.add))
                seq(5, V.tensor_tensor(flat(x[:, bb, :]), flat(x[:, bb, :]), gt, ALU.add))
                seq(6, V.bn_stats(flat(st6[:, bb, :]), flat(x[:, bb, :])))
            norm(4)

            with dve.Fori(0, NB) as b:
                bb = bass.ds(b, 1)
                dve.wait_ge(f_made, b + 1)
                V.tensor_tensor(flat(x[:, bb, :]), flat(x[:, bb, :]), ps[0:PL, 2, 0:D], ALU.add).then_inc(out_ready, 1)

        @block.scalar
        def _(act):
            A = nc.scalar

            def norm(k):
                act.wait_ge(var_ready, k)
                A.activation(std[:], var[:], ACT.Sqrt, bias=eps[:, 0:1]).then_inc(std_ready, 1)
                act.wait_ge(rstd_ready, k)
                if k in (2, 4):
                    act.wait_ge(table_out, 8 * k)
                with act.Fori(0, NB) as b:
                    bb = bass.ds(b, 1)
                    A.activation(flat(h[:, bb, :]), flat(x[:, bb, :]), ACT.Relu, bias=shift[:, bb],
                                 scale=rstd[:, bb]).then_inc(h_rows, 1)
                act.wait_ge(h_rows, k * NB)

            norm(1)
            act.wait_ge(dest_ready, 1)
            for n in range(4):
                A.copy(dslot[:, n, :], dest[:, n:n + 1])
                A.copy(rslot[:, n, :], rec[:, n, :]).then_inc(slot_ready, 1)
            with act.Fori(1, EJ // 4) as i:
                for n in range(4):
                    j = bass.ds(i * 4 + n, 1)
                    act.wait_ge(scattered[n], i * 16)
                    A.copy(dslot[:, n, :], dest[:, j])
                    A.copy(rslot[:, n, :], flat(rec[:, j, :])).then_inc(slot_ready, 1)

            act.wait_ge(list_filled, 16)
            with act.Fori(0, NB) as b:
                act.wait_ge(bucket_summed[0], b + 1)
                A.copy(flat(acc[:, bass.ds(b, 1), 0:D]), ps[0:PL, 7, 0:D]).then_inc(bucket_read[0], 1)
            with act.Fori(0, NB) as b:
                act.wait_ge(y_turned, b + 1)
                A.copy(flat(rowT[:]), ps[:, 1, 0:2 * PL]).then_inc(yT_ready, 1)
                act.wait_ge(h1_made, b + 1)
                A.activation(h1T[:], ps[0:H1, 2, 0:PL], ACT.Relu).then_inc(h1_relu, 1)
                act.wait_ge(h2_made, b + 1)
                A.activation(h2T[:], ps[0:H2, 4, 0:PL], ACT.Relu).then_inc(h2_relu, 1)
            norm(2)
            n_l = act.value_load(n_list[0:1, 0:1], min_val=1, max_val=LROWS // ET)
            with act.Fori(0, n_l) as t:
                act.wait_ge(l_pe, t * 2 + 2)
                A.copy(lcov[:, 0, :], ps[:, 1, D:2 * D])
                A.copy(lcov[:, 1, :], ps[:, 2, D:2 * D]).then_inc(l_act, 1)
            A.activation(skip[:], skip[:], ACT.Sigmoid).then_inc(gate_ready, 1)
            with act.Fori(0, NB) as b:
                act.wait_ge(typed_turned, b + 1)
                A.copy(row_b[:], flat(h[:, bass.ds(b, 1), :])).then_inc(hrow_ready, 1)
                act.wait_ge(typed_turned, b + 2)
                A.copy(typedT[:], ps[:, 1:3, 0:NTY * PL]).then_inc(typedT_ready, 1)
                act.wait_ge(kvq_made, b + 1)
                A.copy(flat(kvT[:]), ps[:, 3, 0:4 * PL]).then_inc(kvT_ready, 1)
                act.wait_ge(stage_free, b + 1)
                for g in range(4):
                    act.wait_ge(bank_full, b * 8 + (2 * g + 2))
                    A.copy((stage_k, stage_v)[g // 2][:, 0:4, 128 * (g % 2):128 * (g % 2) + 128],
                           ps[0:PL, 4 + (2 * g) % 4, :].rearrange("p (r n) -> p r n", r=4)).then_inc(bank_read_a, 1)

            total = pairs_in_all(act, pairsB)
            with act.Fori(0, total) as P:
                for n in range(2):
                    t = P * 2 + n
                    act.wait_ge(hot_turned[1], t + 1)
                    A.copy(hotT[0:PL, n, :], ps[0:PL, n, 0:128]).then_inc(hotT_made[1], 1)
                    A.activation(neg[0:PL, n, :], ps[0:PL, n, 0:128], ACT.Copy, scale=-LOW, bias=LOW)
                for n in range(2):
                    t = P * 2 + n
                    act.wait_ge(s_ready, t + 1)
                    for k in range(NH):
                        last = A.activation(sdiag[:, n, k, :], ident[:], ACT.Copy, scale=s4[:, n, k:k + 1])
                    last.then_inc(sdiag_ready, 1)
                    A.copy(flat(score[:, bass.ds(t, 1), :]), s4[:, n, :]).then_inc(score_kept, 1)
            with act.Fori(0, total) as P:
                for n in range(2):
                    t = P * 2 + n
                    act.wait_ge(hot_turned[2], t + 1)
                    A.copy(hotT[0:PL, n, :], ps[0:PL, n, 0:128]).then_inc(hotT_made[2], 1)
                for n in range(2):
                    t = P * 2 + n
                    act.wait_ge(sd_ready, t + 1)
                    A.activation(wrow[:, n, D:D + NH], sd4[:, n, :], ACT.Exp).then_inc(ex_ready, 1)
            with act.Fori(0, NB) as b:
                act.wait_ge(agg_turned, b + 2)
                A.copy(typedT[:], ps[:, 1:3, 0:NTY * PL]).then_inc(aggT_ready, 1)
            norm(3)
            act.wait_ge(relw_made, 1)
            A.copy(relw[:, 0:2 * D], ps[0:NE16 + 1, 1, :])
            A.copy(relw[:, 2 * D:3 * D], ps[0:NE16 + 1, 2, 0:D])
            A.copy(bhn, ps[0:NE16 + 1, 2, D:2 * D]).then_inc(relw_ready, 1)
            with act.Fori(0, NB) as b:
                act.wait_ge(bucket_summed[3], b + 1)
                A.copy(flat(acc[:, bass.ds(b, 1), :]), ps[0:PL, 7, 0:AW]).then_inc(bucket_read[3], 1)
            act.wait_ge(bucket_read[3], NB + 1)
            with act.Fori(0, NB) as b:
                bb = bass.ds(b, 1)
                act.wait_ge(g_turned, b + 1)
                A.copy(accrow[:, 0:AW], flat(acc[:, bb, :]))
                A.copy(row_b[:], flat(h[:, bb, :])).then_inc(g_rows, 1)
                act.wait_ge(g_turned, b + 2)
                A.copy(cntT, ps[0:NE16 + 1, 2, 0:PL]).then_inc(cntT_ready, 1)
                act.wait_ge(gates_made, b + 1)
                A.activation(rz, ps[0:PL, 3, :], ACT.Sigmoid).then_inc(rz_ready, 1)
                act.wait_ge(gt_ready, b + 2)
                A.activation(gn, gt, ACT.Tanh).then_inc(gn_ready, 1)
            norm(4)
            with act.Fori(0, NB) as b:
                act.wait_ge(f_turned, b + 1)
                A.copy(row_b[:], flat(h[:, bass.ds(b, 1), :])).then_inc(f_row, 1)
                act.wait_ge(f_turned, b + 2)
                A.copy(flat(rowT[:]), ps[:, 1, 0:2 * PL]).then_inc(fT_ready, 1)

        @block.tensor
        def _(pe):
            M = nc.tensor.matmul
            for s in (1, 2):
                pe.sem_inc(tile_done[s], 2)
            pe.sem_inc(bank_read_a, 2)
            pe.sem_inc(bank_read_v, 2)
            pe.sem_inc(max_read, 2)
            for one in (typed_turned, q_copied, agg_turned, g_turned, f_turned, gt_ready, out_ready, bank_full,
                        bucket_read[0], bucket_read[2], bucket_read[3]):
                pe.sem_inc(one, 1)
            pe.wait_ge(consts, 1)
            pe.wait_ge(tot_ready, 1)
            M(ps[0:PL, 0, 0:1], after[0:PL, 0:PL], incl[:, EJ - 1:EJ], start=True, stop=True)
            M(ps[0:PL, 0, 1:2], ones[0:PL, 0:PL], incl[:, EJ - 1:EJ], start=True, stop=True).then_inc(tot_summed, 1)

            def count_keys(which):
                with pe.Fori(0, NB) as b:
                    pe.wait_ge(key_ready, b + (1 + which * NB))
                    M(ps[0:PL, 0, 0:EJ], ones16[0:PL, 0:PL], keyhot, start=True, stop=True)
                    M(ps[0:PL, 1, 0:EJ], after16[0:PL, 0:PL], keyhot, start=True, stop=True).then_inc(key_counted, 1)

            def place_edges(which, nf):
                def products(n, start, stop):
                    for f in range(nf):
                        last = M(ps[:, 2 + f, 0:NT], lanehot[:, n, f, :], tilehot[:, n, :], start=start, stop=stop)
                    last.then_inc(hot_placed, 1)

                for n in range(4):
                    pe.wait_ge(hot_ready, which * EJ + n + 1)
                    products(n, n == 0, False)
                with pe.Fori(1, EJ // 4 - 1) as i:
                    for n in range(4):
                        pe.wait_ge(hot_ready, i * 4 + (which * EJ + n + 1))
                        products(n, False, False)
                for n in range(4):
                    pe.wait_ge(hot_ready, which * EJ + EJ - 3 + n)
                    products(n, False, n == 3)

            def open_sum(width):
                M(ps[0:PL, 7, 0:width], zeros16[0:1, 0:PL], zeros16[0:1, 0:width], start=True, stop=False)

            def close_sum(s, width):
                M(ps[0:PL, 7, 0:width], zeros16[0:1, 0:PL], zeros16[0:1, 0:width], start=False, stop=True).then_inc(bucket_summed[s], 1)

            count_keys(0)
            place_edges(0, 2)
            pe.wait_ge(sorted_by, 1)
            with pe.Fori(0, NB) as b:
                lo, hi = bounds(pe, pairsA, b)
                pe.wait_ge(bucket_read[0], b + 1)
                open_sum(D)
                with pe.Fori(lo, hi) as P:
                    for n in range(2):
                        t = P * 2 + n
                        pe.wait_ge(hot_made[0], t + 1)
                        pe.wait_ge(row_ready[0], t + 1)
                        M(ps[0:PL, 7, 0:D], hot[:, n, 0:PL], flat(rows[:, bass.ds(P % (RING // 2) * 2 + n, 1), :]),
                          start=False, stop=False).then_inc(row_used[0], 1)
                close_sum(0, D)
            spare_rows(pe, 0, pairsA, roundsA)
            count_keys(1)
            place_edges(1, 3)

            pe.wait_ge(small_in, 16 * 7)
            with pe.Fori(0, NB) as b:
                pe.wait_ge(y_ready, b + 1)
                nc.tensor.transpose(ps[:, 1, 0:PL], row_b[:, 0:128], ident[0:PL, 0:PL])
                nc.tensor.transpose(ps[:, 1, PL:2 * PL], row_b[:, 128:256], ident[0:PL, 0:PL]).then_inc(y_turned, 1)
                pe.wait_ge(yT_ready, b + 1)
                M(ps[0:H1, 2, 0:PL], w1t[:, 0, :], rowT[:, 0, :], start=True, stop=False)
                M(ps[0:H1, 2, 0:PL], w1t[:, 1, :], rowT[:, 1, :], start=False, stop=True).then_inc(h1_made, 1)
                pe.wait_ge(h1_relu, b + 1)
                pe.sem_inc(pe_pass, 1)
                M(ps[0:H2, 4, 0:PL], w2t[:], h1T[:], start=True, stop=True).then_inc(h2_made, 1)
                pe.wait_ge(h2_relu, b + 1)
                M(ps[0:PL, 3, 0:D], h2T[:], w3t[:], start=True, stop=True).then_inc(o_made, 1)

            n_l = pe.value_load(n_list[0:1, 0:1], min_val=1, max_val=LROWS // ET)
            with pe.Fori(0, n_l) as t:
                pe.wait_ge(l_dve, t * 8 + 1)
                M(ps[:, 0, 0:128], ones128[:], ldiag[:], start=True, stop=True).then_inc(l_pe, 1)
                pe.wait_ge(l_dve, t * 8 + 8)
                M(ps[:, 1, :], lS[:, 0:128], flat(lVC), start=True, stop=True)
                M(ps[:, 2, :], lS[:, 128:256], flat(lVC), start=True, stop=True).then_inc(l_pe, 1)

            with pe.Fori(0, NB) as b:
                pe.wait_ge(hrow_ready, b + 1)
                pe.wait_ge(diag_made, b + 1)
                M(ps[:, 1, 0:NTY * PL], row_b[:, 0:128], flat(diag[:]), start=True, stop=True)
                M(ps[:, 2, 0:NTY * PL], row_b[:, 128:256], flat(diag[:]), start=True, stop=True).then_inc(typed_turned, 1)
                pe.wait_ge(typedT_ready, b + 1)
                pe.wait_ge(q_copied, b + 1)
                for g in range(4):
                    w, o = (wk, wv)[g // 2], 128 * (g % 2)
                    for k in range(NTY):
                        for cc in range(2):
                            M(ps[:, 3, g * PL:g * PL + PL], w[:, k, cc, o:o + 128], typedT[:, cc, k * PL:k * PL + PL],
                              start=(k == 0 and cc == 0), stop=(k == NTY - 1 and cc == 1))
                for k in range(NTY):
                    for cc in range(2):
                        last = M(ps[0:PL, 0, 0:D], typedT[:, cc, k * PL:k * PL + PL], wq[:, k, cc, :],
                                 start=(k == 0 and cc == 0), stop=(k == NTY - 1 and cc == 1))
                last.then_inc(kvq_made, 1)
                pe.wait_ge(kvT_ready, b + 1)
                for m in range(8):
                    pe.wait_ge((bank_read_a, bank_read_v)[m % 2], b * 4 + (m // 2 + 1))
                    M(ps[0:PL, 4 + m % 4, :], kvT[:, m // 2, :], flat((bdk, bdm)[m // 4][:, m // 2 % 2, 4 * (m % 2):4 * (m % 2) + 4, :]),
                      start=True, stop=True).then_inc(bank_full, 1)

            with pe.Fori(0, NB) as b:
                lo, hi = bounds(pe, pairsB, b)
                with pe.Fori(lo, hi) as P:
                    for n in range(2):
                        t = P * 2 + n
                        pe.wait_ge(hot_made[1], t + 1)
                        nc.tensor.transpose(ps[0:PL, n, 0:128], hot[:, n, 0:PL], ident[:]).then_inc(hot_turned[1], 1)
                    for n in range(2):
                        t = P * 2 + n
                        pe.wait_ge(hotT_made[1], t + 1)
                        M(ps[:, 2 + n, 0:D], hotT[0:PL, n, :], flat(q[:, bass.ds(b, 1), :]), start=True, stop=True).then_inc(q_edge, 1)
                    for n in range(2):
                        t = P * 2 + n
                        pe.wait_ge(sdiag_ready, t + 1)
                        pe.wait_ge(max_read, t + 1)
                        M(ps[0:PL, 4 + n, :], hot[:, n, 0:PL], flat(sdiag[:, n]), start=True, stop=False)
                        M(ps[0:PL, 4 + n, :].rearrange("p (h e) -> p h e", h=NH), identb[0:PL, 0:PL],
                          neg[0:PL, n:n + 1, :].broadcast_to([PL, NH, 128]), start=False, stop=True).then_inc(tile_done[1], 1)
            pe.wait_ge(m_bucket, 2 * NB)
            with pe.Fori(0, NB) as b:
                lo, hi = bounds(pe, pairsB, b)
                pe.wait_ge(bucket_read[2], b + 1)
                open_sum(D + NH)
                with pe.Fori(lo, hi) as P:
                    for n in range(2):
                        t = P * 2 + n
                        pe.wait_ge(hot_made[2], t + 1)
                        nc.tensor.transpose(ps[0:PL, n, 0:128], hot[:, n, 0:PL], ident[:]).then_inc(hot_turned[2], 1)
                    for n in range(2):
                        t = P * 2 + n
                        pe.wait_ge(hotT_made[2], t + 1)
                        M(ps[:, 2 + n, 0:NH], hotT[0:PL, n, :], flat(m_all[:, bass.ds(b, 1), :]), start=True, stop=True).then_inc(m_edge, 1)
                    for n in range(2):
                        t = P * 2 + n
                        pe.wait_ge(row_used[2], t + (RING + 1))
                        M(ps[0:PL, 7, 0:D + NH], hot[:, n, 0:PL], wrow[:, n, :], start=False, stop=False).then_inc(tile_done[2], 1)
                close_sum(2, D + NH)
            with pe.Fori(0, NB) as b:
                pe.wait_ge(agg_ready, b + 1)
                M(ps[:, 1, 0:NTY * PL], row_b[:, 0:128], flat(diag[:]), start=True, stop=True)
                M(ps[:, 2, 0:NTY * PL], row_b[:, 128:256], flat(diag[:]), start=True, stop=True).then_inc(agg_turned, 1)
                pe.wait_ge(aggT_ready, b + 1)
                for k in range(NTY):
                    for cc in range(2):
                        last = M(ps[0:PL, 0, 0:D], typedT[:, cc, k * PL:k * PL + PL], wa[:, k, cc, :],
                                 start=(k == 0 and cc == 0), stop=(k == NTY - 1 and cc == 1))
                last.then_inc(att_made, 1)

            pe.wait_ge(gru_in, 64)
            for o, n, rows_b in ((0, 2 * D, 2), (2 * D, D, 1)):
                bank = ps[0:NE16 + 1, 1 + o // (2 * D), 0:n]
                M(bank, relt[:, 0, :], wih[:, 0, o:o + n], start=True, stop=False)
                M(bank, relt[:, 1, :], wih[:, 1, o:o + n], start=False, stop=False)
                M(bank, pick[0:rows_b, :], bias[0:rows_b, o:o + n], start=False, stop=True)
            M(ps[0:NE16 + 1, 2, D:2 * D], pick_h, bias[:, 2 * D:3 * D], start=True, stop=True).then_inc(relw_made, 1)

            with pe.Fori(0, NB) as b:
                lo, hi = bounds(pe, pairsB, b)
                pe.wait_ge(bucket_read[3], b + 1)
                open_sum(AW)
                with pe.Fori(lo, hi) as P:
                    for n in range(2):
                        t = P * 2 + n
                        pe.wait_ge(hot_made[3], t + 1)
                        pe.wait_ge(row_ready[3], t + 1)
                        M(ps[0:PL, 7, D:AW], hot[:, n, 0:PL], relhot[:, n, :], start=False, stop=False)
                        M(ps[0:PL, 7, 0:D], hot[:, n, 0:PL], flat(rows[:, bass.ds(P % (RING // 2) * 2 + n, 1), :]),
                          start=False, stop=False).then_inc(row_used[3], 1)
                close_sum(3, AW)
            spare_rows(pe, 3, pairsB, roundsB)

            pe.wait_ge(relw_ready, 1)
            with pe.Fori(0, NB) as b:
                pe.wait_ge(g_rows, b + 1)
                T = nc.tensor.transpose
                T(ps[:, 1, 0:PL], accrow[:, 0:128], ident[0:PL, 0:PL])
                T(ps[:, 1, PL:2 * PL], accrow[:, 128:256], ident[0:PL, 0:PL])
                T(ps[:, 1, 2 * PL:3 * PL], row_b[:, 0:128], ident[0:PL, 0:PL])
                T(ps[:, 1, 3 * PL:4 * PL], row_b[:, 128:256], ident[0:PL, 0:PL])
                T(ps[0:NE16 + 1, 2, 0:PL], accrow[:, D:AW + 1], ident[0:PL, 0:PL]).then_inc(g_turned, 1)
                pe.wait_ge(gT_ready, b + 1)
                pe.wait_ge(cntT_ready, b + 1)
                pe.wait_ge(gt_ready, b + 1)
                rzb, inb, hnb = ps[0:PL, 3, :], ps[0:PL, 4, 0:D], ps[0:PL, 5, 0:D]
                for bank, lo_, hi_ in ((rzb, 0, 2 * D), (inb, 2 * D, 3 * D)):
                    M(bank, gT[:, 0, :], wih[:, 0, lo_:hi_], start=True, stop=False)
                    M(bank, gT[:, 1, :], wih[:, 1, lo_:hi_], start=False, stop=False)
                    M(bank, cntT, relw[:, lo_:hi_], start=False, stop=bank is inb)
                M(rzb, gT[:, 2, :], whh[:, 0, 0:2 * D], start=False, stop=False)
                M(rzb, gT[:, 3, :], whh[:, 1, 0:2 * D], start=False, stop=True)
                M(hnb, gT[:, 2, :], whh[:, 0, 2 * D:3 * D], start=True, stop=False)
                M(hnb, gT[:, 3, :], whh[:, 1, 2 * D:3 * D], start=False, stop=False)
                M(hnb, cntT, bhn, start=False, stop=True).then_inc(gates_made, 1)

            with pe.Fori(0, NB) as b:
                pe.wait_ge(f_row, b + 1)
                nc.tensor.transpose(ps[:, 1, 0:PL], row_b[:, 0:128], ident[0:PL, 0:PL])
                nc.tensor.transpose(ps[:, 1, PL:2 * PL], row_b[:, 128:256], ident[0:PL, 0:PL]).then_inc(f_turned, 1)
                pe.wait_ge(fT_ready, b + 1)
                pe.wait_ge(out_ready, b + 1)
                M(ps[0:PL, 2, 0:D], rowT[:, 0, :], wout[:, 0, :], start=True, stop=False)
                M(ps[0:PL, 2, 0:D], rowT[:, 1, :], wout[:, 1, :], start=False, stop=True).then_inc(f_made, 1)


def kernel(**inputs):
    import numpy as _np
    import concourse.bacc as _bacc
    from concourse import mybir as _mybir
    from concourse.bass_utils import run_bass_kernel_spmd as _run

    def get(name):
        return _np.asarray(inputs[name])

    names = ["x", "src", "dst", "edge_type_16", "edge_type_8", "edge_weight", "node_type_4", "L0_gnn_w"]
    laid = [(n, get(n)) for n in names]
    laid += [
        ("w1t", get("L0_gnn_W1").T), ("w2t", get("L0_gnn_W2").T), ("w3t", get("L0_gnn_W3").T),
        ("wk", get("L1_gnn_k_linears")), ("wq", get("L1_gnn_q_linears")),
        ("wv", get("L1_gnn_v_linears")), ("wa", get("L1_gnn_a_linears")),
        ("att", get("L1_gnn_relation_att").transpose(3, 1, 0, 2)),
        ("msg", get("L1_gnn_relation_msg").transpose(2, 1, 0, 3)),
        ("pri", get("L1_gnn_relation_pri")), ("skip", get("L1_gnn_skip")),
        ("relt", get("L2_gnn_relvectors").T), ("wih", get("L2_gnn_w_ih").T), ("whh", get("L2_gnn_w_hh").T),
        ("bias", _np.stack([get("L2_gnn_b_ih"), get("L2_gnn_b_hh")])),
    ]
    nc = _bacc.Bacc("TRN2", target_bir_lowering=False, num_devices=1)
    arrays, args = {}, []
    for name, a in laid:
        a = _np.ascontiguousarray(a)
        arrays[f"in_{name}"] = a
        args.append(nc.dram_tensor(f"in_{name}", a.shape, _mybir.dt.from_np(a.dtype), kind="ExternalInput").ap())
    args.append(nc.dram_tensor("out_0", (N, D), _mybir.dt.float32, kind="ExternalOutput").ap())
    build(nc, *args)
    r = _run(nc, [arrays], core_ids=[0])
    return r.results[0]["out_0"]
```

```python
from contextlib import ExitStack

import concourse.bass as bass
from concourse import mybir

ALU = mybir.AluOpType
ACT = mybir.ActivationFunctionType
F32 = mybir.dt.float32
F16 = mybir.dt.float16
BF16 = mybir.dt.bfloat16
I32 = mybir.dt.int32
AX_X, AX_XY = mybir.AxisListType.X, mybir.AxisListType.XY

E, N, D = 50000, 3125, 256
PL = 125
NB = N // PL
EJ = E // PL
ET = 128
NP = -(-E // (2 * ET)) + 2 * (NB - 1)
RING = 8
ROUND = 2 * RING
NT = (2 * NP // ROUND + 1) * ROUND
NR, NH, DK, NTY, NE16 = 8, 4, 64, 4, 16
H1, H2 = 64, 32
EPS = 1e-5
MAGIC = 12582912.0
LROWS = (E // (PL * ET) + 1) * PL * ET
FAR = LROWS + 1.0
LOW = -1e30
AW = D + NE16


class Steps:

    def __init__(self, eng, sem):
        self.eng, self.sem, self.n, self.at = eng, sem, 0, 0

    def mark(self, ins):
        ins.then_inc(self.sem, 1)
        self.n += 1

    def settle(self):
        self.eng.wait_ge(self.sem, self.at + self.n)

    def then(self, ins):
        self.mark(ins)
        self.settle()

    def enter(self, i, per):
        self.outer, self.per = self.n, per
        self.at, self.n = self.outer + i * per, 0

    def leave(self, trips):
        assert self.n == self.per, (self.n, self.per)
        self.at, self.n = 0, self.outer + trips * self.per


class Carver:

    def __init__(self, tensor, at=0):
        self.tensor, self.at = tensor, at

    def take(self, lanes, *shape, dt=F32):
        words = 1
        for n in shape:
            words *= n
        words = (words + 1) // 2 if dt in (F16, BF16) else words
        assert self.at + words <= self.tensor.shape[1], (self.at, words)
        piece = self.tensor[0:lanes, self.at:self.at + words]
        self.at += words
        if dt != F32:
            piece = piece.bitcast(dt)
        names = "abcd"[:len(shape)]
        if len(shape) > 1:
            sizes = dict(zip(names, shape))
            piece = piece.rearrange(f"p ({' '.join(names)}) -> p {' '.join(names)}", **sizes)
        return piece


def build(nc, x_in, src_in, dst_in, r16_in, r8_in, ew_in, nty_in, w_in, w1t_in, w2t_in, w3t_in,
          wk_in, wq_in, wv_in, wa_in, att_in, msg_in, pri_in, skip_in, relt_in, wih_in, whh_in, bias_in, out):
    ctx = ExitStack()
    with ctx:
        def sb(name, shape, dt=F32):
            return ctx.enter_context(nc.sbuf_tensor(name, shape, dt))

        def sem(name):
            return ctx.enter_context(nc.semaphore(name))

        def dram(name, shape, dt=F32):
            return nc.dram_tensor(name, shape, dt).ap()

        ps = ctx.enter_context(nc.psum_tensor("ps", [128, 8, 512], F32))

        lane = sb("lane", [128, 1])
        col = sb("col", [128, NT])
        col16 = sb("col16", [128, NT], F16)
        ones = sb("ones", [PL, EJ])
        ident = sb("ident", [128, 128])
        identb = sb("identb", [128, 128], BF16)
        after = sb("after", [128, 128])
        after16 = sb("after16", [128, 128], F16)
        ones16 = sb("ones16", [128, 128], F16)
        zeros16 = sb("zeros16", [1, 512], F16)
        eps = sb("eps", [PL, 1])

        x = sb("x", [PL, NB, D])
        h = sb("h", [PL, NB, D])
        q = sb("q", [PL, NB, D])
        acc = sb("acc", [PL, NB, AW])
        m_all = sb("m_all", [PL, NB, NH])
        tmask = sb("tmask", [PL, NTY, NB])
        gmask = sb("gmask", [PL, NTY, NB])
        score = sb("score", [128, NT, NH])
        locA = sb("locA", [128, NT])
        idxA = sb("idxA", [128, NT], I32)
        locB = sb("locB", [128, NT])
        relB = sb("relB", [128, NT])
        idxR = sb("idxR", [128, NT], I32)
        idxS = sb("idxS", [128, NT], I32)
        pairsA = sb("pairsA", [PL, NB + 1], I32)
        pairsB = sb("pairsB", [PL, NB + 1], I32)
        roundsA = sb("roundsA", [PL, 1], I32)
        roundsB = sb("roundsB", [PL, 1], I32)
        rows = sb("rows", [128, RING, D])
        islot = sb("islot", [128, 2, RING], I32)
        wout = sb("wout", [128, 2, D])
        n_list = sb("n_list", [PL, 1], I32)

        st6 = sb("st6", [PL, NB, 6])
        mean = sb("mean", [PL, NB])
        var = sb("var", [PL, NB])
        std = sb("std", [PL, NB])
        rstd = sb("rstd", [PL, NB])
        shift = sb("shift", [PL, NB])
        half = sb("half", [PL, NB])

        w_sb = sb("w_sb", [PL, 1])
        w1t = sb("w1t", [128, 2, H1])
        w2t = sb("w2t", [H1, H2])
        w3t = sb("w3t", [H2, D])
        row_b = sb("row_b", [PL, D])
        rowT = sb("rowT", [128, 2, PL])
        h1T = sb("h1T", [H1, PL])
        h2T = sb("h2T", [H2, PL])

        arena = sb("arena", [128, 12288])
        c = Carver(arena)
        src_i, dst_i, r16_i, r8_i = (c.take(PL, EJ, dt=I32) for _ in range(4))
        ew = c.take(PL, EJ)
        rec = c.take(PL, EJ, 2)
        src, dst, r16, r8 = (c.take(PL, EJ) for _ in range(4))
        s_lane, s_tile, d_lane, d_tile = (c.take(PL, EJ) for _ in range(4))
        fa = c.take(PL, 2, EJ)
        fb = c.take(PL, 3, EJ)
        tmp, incl, pos, to_tile, to_lane = (c.take(PL, EJ) for _ in range(5))
        keyhot = c.take(PL, EJ, dt=F16)
        tilehot = c.take(PL, 4, NT, dt=F16)
        qc = Carver(q[:].rearrange("p b d -> p (b d)"))
        lanehot = qc.take(PL, 4, 3, ET, dt=F16)
        dest = qc.take(PL, EJ, dt=I32)
        dslot = qc.take(PL, 4, 1, dt=I32)
        rslot = qc.take(PL, 4, 2)
        base, rnd = qc.take(PL, 1), qc.take(PL, 1)
        rowoff = qc.take(PL, 2)
        fill = acc[0:PL, 0:4, :].rearrange("p a b -> p (a b)")[:, 0:LROWS * 2 // PL]
        sc = Carver(score[:].rearrange("p a b -> p (a b)"))
        dec, dec2 = sc.take(128, NT), sc.take(128, NT)

        c = Carver(arena)
        wk, wq, wv = (c.take(128, NTY, 2, D) for _ in range(3))
        wa_at = c.at
        wa = c.take(128, NTY, 2, D)
        bdk = c.take(128, 2, NR, 128)
        bdm = c.take(128, 2, NR, 128)
        ac = Carver(acc[:].rearrange("p b d -> p (b d)"))
        stage_k, stage_v = ac.take(PL, NR, D), ac.take(PL, NR, D)
        diag = sb("diag", [PL, NTY, PL])
        typedT = sb("typedT", [128, 2, NTY * PL])
        kvT = sb("kvT", [128, 4, PL])
        pri = sb("pri", [128, NR, NH])
        nty = sb("nty", [PL, NB], I32)
        skip = sb("skip", [PL, NTY])

        c = Carver(arena)
        relhot = c.take(128, 2, NE16)
        gru_at = c.at
        hotT = c.take(128, 2, 128)
        neg = c.take(128, 4, 2, 128, dt=BF16)
        sel = c.take(6 * NH, 2 * NH, PL, dt=BF16)
        sel1 = c.take(6 * NH, 2 * NH)
        s_parts = c.take(128, 3, 2 * NH, dt=BF16)
        sT = c.take(6 * NH, 128, dt=BF16)
        prod = c.take(128, 2, D)
        s4, s_rest = c.take(128, 2, NH), c.take(128, 2 * NH)
        wrow = c.take(128, 2, D + NH)
        m_run, m_new = c.take(128, NH), c.take(128, NH)
        den, rden = c.take(PL, NH), c.take(PL, NH)
        sd4, ex4 = c.take(128, 2, NH), c.take(128, 4, NH)
        hot = sb("hot", [128, 2, 128])
        hot16 = sb("hot16", [128, 2, 128], BF16)
        col1_16 = sb("col1_16", [128, 128], BF16)
        col1 = sb("col1", [128, 128])
        assert c.at <= wa_at
        c_edges = c.at
        c = Carver(arena, wa_at + NTY * 2 * D)
        wih = c.take(128, 2, 3 * D)
        whh = c.take(128, 2, 3 * D)
        relw = c.take(NE16 + 1, 3 * D)
        c = Carver(arena, c_edges)
        bhn = c.take(NE16 + 1, D)
        relt = c.take(128, 2, NE16 + 1)
        bias = c.take(2, 3 * D)
        pick, pick_h = c.take(2, NE16 + 1), c.take(2, NE16 + 1)
        assert c.at <= wa_at
        c = Carver(arena, gru_at)
        gT = c.take(128, 4, PL)
        cntT = c.take(NE16 + 1, PL)
        accrow = c.take(PL, AW + 1)
        rz, gn, gt = c.take(PL, 2 * D), c.take(PL, D), c.take(PL, D)
        assert c.at <= c_edges
        lrec = sb("lrec", [128, 2])
        lsd = sb("lsd", [128, 4])
        leq = sb("leq", [128, 128])
        ldiag = sb("ldiag", [128, 128])
        ones128 = sb("ones128", [128, 128])
        lS = rows[:, 0, :]
        lVC = rows[:, 1:3, :]
        lcov = rows[:, 3:5, :]

        elist = dram("elist", [LROWS, 2])
        tab_h0 = dram("tab_h0", [N, D])
        tab_h2 = dram("tab_h2", [N, D])
        tab_k = dram("tab_k", [N * NR, D])
        tab_v = dram("tab_v", [N * NR, D])

        edges_in, x_in_s, small_in, attn_in, gru_in = (sem(n) for n in ("edges_in", "x_in_s", "small_in", "attn_in", "gru_in"))
        dve_step, act_step = sem("dve_step"), sem("act_step")
        cols_made, consts = sem("cols_made"), sem("consts")
        key_ready, key_counted = sem("key_ready"), sem("key_counted")
        tot_ready, tot_summed = sem("tot_ready"), sem("tot_summed")
        hot_ready, hot_placed = sem("hot_ready"), sem("hot_placed")
        sorted_by = sem("sorted_by")
        fill_done, list_filled, dest_ready, slot_ready = (sem(n) for n in ("fill_done", "list_filled", "dest_ready", "slot_ready"))
        scattered = [sem(f"scattered{n}") for n in range(4)]
        var_ready, std_ready, rstd_ready, h_rows = (sem(n) for n in ("var_ready", "std_ready", "rstd_ready", "h_rows"))
        table_out, base_ready = sem("table_out"), sem("base_ready")
        landed = [[sem(f"landed{s}_{n}") for n in range(RING)] for s in range(2)]
        row_ready = [sem(f"row_ready{s}") for s in range(4)]
        row_used = [sem(f"row_used{s}") for s in range(4)]
        pool_pass, pe_pass, dve_pass = sem("pool_pass"), sem("pe_pass"), sem("dve_pass")
        islot_ready = [sem(f"islot_ready{s}") for s in range(4)]
        ring_idle = sem("ring_idle")
        hot_made = [sem(f"hot_made{s}") for s in range(4)]
        bucket_summed = [sem(f"bucket_summed{s}") for s in range(4)]
        bucket_read = [sem(f"bucket_read{s}") for s in range(4)]
        y_ready, y_turned, yT_ready, h1_made, h1_relu, h2_made, h2_relu, o_made, n1_step = (
            sem(n) for n in ("y_ready", "y_turned", "yT_ready", "h1_made", "h1_relu", "h2_made", "h2_relu", "o_made", "n1_step"))
        l_in, l_dve, l_pe, l_act, l_w = (sem(n) for n in ("l_in", "l_dve", "l_pe", "l_act", "l_w"))
        blocks_cleared, hrow_ready, diag_made, typed_turned, typedT_ready, kvq_made, kvT_ready, q_copied = (
            sem(n) for n in ("blocks_cleared", "hrow_ready", "diag_made", "typed_turned", "typedT_ready", "kvq_made", "kvT_ready", "q_copied"))
        bank_full, bank_read_a, bank_read_v, tabs_out, stage_free = (
            sem(n) for n in ("bank_full", "bank_read_a", "bank_read_v", "tabs_out", "stage_free"))
        hot_turned = [None] + [sem(f"hot_turned{s}") for s in (1, 2)]
        hotT_made = [None] + [sem(f"hotT_made{s}") for s in (1, 2)]
        tile_done = [None] + [sem(f"tile_done{s}") for s in (1, 2)]
        q_edge, s_ready, s_turned, sT_ready, s_split, max_read, m_step, m_bucket, m_cleared = (
            sem(n) for n in ("q_edge", "s_ready", "s_turned", "sT_ready", "s_split", "max_read", "m_step", "m_bucket", "m_cleared"))
        m_edge, sd_ready, ex_ready = (sem(n) for n in ("m_edge", "sd_ready", "ex_ready"))
        agg_ready, agg_turned, aggT_ready, att_made, n3_step = (
            sem(n) for n in ("agg_ready", "agg_turned", "aggT_ready", "att_made", "n3_step"))
        relt_cleared, relw_made, relw_ready, g_rows, g_turned, gT_ready, cntT_ready, gates_made = (
            sem(n) for n in ("relt_cleared", "relw_made", "relw_ready", "g_rows", "g_turned", "gT_ready", "cntT_ready", "gates_made"))
        rz_ready, gt_ready, gn_ready, gru_done, n5_step = (
            sem(n) for n in ("rz_ready", "gt_ready", "gn_ready", "gru_done", "n5_step"))
        gate_ready, score_kept = sem("gate_ready"), sem("score_kept")
        f_row, f_turned, fT_ready, f_made, out_ready = (sem(n) for n in ("f_row", "f_turned", "fT_ready", "f_made", "out_ready"))
        out_done = sem("out_done")

        block = ctx.enter_context(nc.Block())

        def flat(ap):
            return ap.rearrange("p a b -> p (a b)")

        def bounds(eng, pairs, b, least=0):
            lo = eng.value_load(pairs[0:1, bass.ds(b, 1)], min_val=least, max_val=NP - 2)
            hi = eng.value_load(pairs[0:1, bass.ds(b + 1, 1)], min_val=least + 2, max_val=NP)
            return lo, hi

        def spare_rows(eng, s, pairs, rings):
            first = eng.value_load(pairs[0:1, NB:NB + 1], min_val=1, max_val=NP)
            rounds = eng.value_load(rings[0:1, 0:1], min_val=1, max_val=NT // ROUND)
            with eng.Fori(first * 2, rounds * ROUND) as t:
                eng.wait_ge(row_used[s], t + RING)
                eng.wait_ge(row_ready[s], t + 3)
                eng.sem_inc(row_used[s], 1)

        def pairs_in_all(eng, pairs):
            return eng.value_load(pairs[0:1, NB:NB + 1], min_val=2 * NB, max_val=NP)

        @block.sync
        def _(sp):
            for t, a in ((src_i, src_in), (dst_i, dst_in), (r16_i, r16_in), (r8_i, r8_in), (ew, ew_in)):
                sp.dma_start(t, a.rearrange("(p j) -> p j", p=PL)).then_inc(edges_in, 16)
            sp.dma_start(x[:], x_in.rearrange("(p b) d -> p b d", p=PL)).then_inc(x_in_s, 16)
            sp.dma_start(nty[:], nty_in.rearrange("(p b) -> p b", p=PL)).then_inc(small_in, 16)
            sp.dma_start(w_sb[:], w_in.rearrange("(a b) -> a b", a=1).broadcast_to([PL, 1])).then_inc(small_in, 16)
            sp.dma_start(w1t[:], w1t_in.rearrange("(c p) n -> p c n", p=128)).then_inc(small_in, 16)
            sp.dma_start(w2t[:], w2t_in).then_inc(small_in, 16)
            sp.dma_start(w3t[:], w3t_in).then_inc(small_in, 16)
            sp.dma_start(pri[:], pri_in.rearrange("(a r) h -> a (r h)", a=1).broadcast_to([128, NR * NH]).rearrange("p (r h) -> p r h", r=NR)).then_inc(small_in, 16)
            sp.dma_start(skip[:], skip_in.rearrange("(a t) -> a t", a=1).broadcast_to([PL, NTY])).then_inc(small_in, 16)
            sp.wait_ge(fill_done, 1)
            sp.dma_start(elist.rearrange("(p c) k -> p (c k)", p=PL), fill).then_inc(list_filled, 16)

            def write_table(tab):
                sp.dma_start(tab.rearrange("(p b) d -> p b d", p=PL), h[:]).then_inc(table_out, 16)

            def relay(s, rings):
                count = sp.value_load(rings[0:1, 0:1], min_val=1, max_val=NT // ROUND)
                past = count * max(s - 1, 0) if s > 1 else 0
                with sp.Fori(past, past + count) as i:
                    for n in range(ROUND):
                        sp.wait_ge(landed[min(s, 1)][n % RING], i * 32 + 16 * (n // RING + 1))
                        sp.sem_inc(row_ready[s], 1)
                sp.sem_inc(ring_idle, 1)

            sp.wait_ge(h_rows, NB)
            write_table(tab_h0)
            sp.wait_ge(sorted_by, 1)
            relay(0, roundsA)
            sp.wait_ge(sorted_by, 2)
            for n in range(4):
                sp.wait_ge(scattered[n], 16 * EJ // 4)
            for t, a in ((wk, wk_in), (wq, wq_in), (wv, wv_in), (wa, wa_in)):
                for k in range(NTY):
                    sp.dma_start(t[:, k], a[k].rearrange("(c p) n -> p c n", p=128)).then_inc(attn_in, 16)
            sp.wait_ge(blocks_cleared, 1)
            for t, a in ((bdk, att_in), (bdm, msg_in)):
                for two in range(2):
                    for cc in range(2):
                        sp.dma_start(t[64 * two:64 * two + 64, cc, :, 64 * two:64 * two + 64],
                                     a[:, 2 * cc + two]).then_inc(attn_in, 16)
            n_l = sp.value_load(n_list[0:1, 0:1], min_val=1, max_val=LROWS // ET)
            with sp.Fori(0, n_l) as t:
                sp.wait_ge(l_w, t + 1)
                sp.dma_start(lrec[:].rearrange("p (a k) -> p a k", a=1),
                             elist.rearrange("(t p) k -> p t k", p=ET)[:, bass.ds(t, 1), :]).then_inc(l_in, 16)
            sp.sem_inc(stage_free, 1)
            with sp.Fori(0, NB) as b:
                sp.wait_ge(bank_read_a, b * 4 + 6)
                sp.wait_ge(bank_read_v, b * 4 + 6)
                for tab, stg in ((tab_k, stage_k), (tab_v, stage_v)):
                    sp.dma_start(tab.rearrange("(p b r) d -> p b (r d)", p=PL, r=NR)[:, bass.ds(b, 1), :],
                                 stg.rearrange("p (a r) n -> p a (r n)", a=1)).then_inc(tabs_out, 16)
                sp.wait_ge(tabs_out, b * 32 + 32)
                sp.sem_inc(stage_free, 1)
            sp.wait_ge(tabs_out, 32 * NB)
            sp.dma_start(wih, wih_in.rearrange("(c p) n -> p c n", p=128)).then_inc(gru_in, 16)
            sp.dma_start(whh, whh_in.rearrange("(c p) n -> p c n", p=128)).then_inc(gru_in, 16)
            sp.wait_ge(relt_cleared, 1)
            sp.dma_start(relt[:, :, 0:NE16], relt_in.rearrange("(c p) n -> p c n", p=128)).then_inc(gru_in, 16)
            sp.dma_start(bias, bias_in).then_inc(gru_in, 16)
            relay(1, roundsB)
            relay(2, roundsB)
            sp.wait_ge(h_rows, 3 * NB)
            write_table(tab_h2)
            relay(3, roundsB)
            with sp.Fori(0, NB) as b:
                sp.wait_ge(out_ready, b + 2)
                sp.dma_start(out.rearrange("(p b) d -> p b d", p=PL)[:, bass.ds(b, 1), :], x[:, bass.ds(b, 1), :]).then_inc(out_done, 16)
            sp.wait_ge(out_done, 16 * NB)
            sp.wait_ge(tabs_out, 32 * NB)
            sp.wait_ge(table_out, 32)
            sp.wait_ge(list_filled, 16)

        @block.gpsimd
        def _(pool):
            nc.gpsimd.iota(lane[:], [[0, 1]], base=0, channel_multiplier=1, allow_small_or_imprecise_dtypes=True)
            nc.gpsimd.iota(col[:], [[1, NT]], base=0, channel_multiplier=0,
                           allow_small_or_imprecise_dtypes=True).then_inc(cols_made, 1)
            nc.gpsimd.memset(fill, -1.0).then_inc(fill_done, 1)
            for s in range(4):
                pool.sem_inc(row_used[s], RING)

            pool.wait_ge(list_filled, 16)
            with pool.Fori(0, EJ // 4) as i:
                for n in range(4):
                    pool.wait_ge(slot_ready, i * 4 + (n + 1))
                    pool.sem_inc(pool_pass, 1)
                    pool.indirect_dma_start(
                        out=elist, out_offset=bass.IndirectOffsetOnAxis(ap=dslot[:, n, :], axis=0),
                        in_=rslot[:, n, :], in_offset=None, bounds_check=LROWS - 1, oob_is_err=False,
                    ).then_inc(scattered[n], 16)

            def gather(s, table, idx, rings):
                count = pool.value_load(rings[0:1, 0:1], min_val=1, max_val=NT // ROUND)
                with pool.Fori(0, count) as i:
                    for g in range(2):
                        pool.wait_ge(row_used[s], i * ROUND + (RING * g + 1))
                        pool.sem_inc(pool_pass, 1)
                        nc.gpsimd.tensor_copy(islot[:, g, :], idx[:, bass.ds(i * ROUND + RING * g, RING)]).then_inc(islot_ready[s], 1)
                        pool.wait_ge(islot_ready[s], i * 2 + (g + 1))
                        for n in range(RING):
                            pool.wait_ge(row_used[s], i * ROUND + (RING * g + n + 1))
                            pool.sem_inc(pool_pass, 1)
                            pool.indirect_dma_start(
                                out=rows[:, n, :], out_offset=None, in_=table,
                                in_offset=bass.IndirectOffsetOnAxis(ap=islot[:, g, n:n + 1], axis=0),
                            ).then_inc(landed[min(s, 1)][n], 16)
                pool.wait_ge(row_used[s], count * ROUND + RING)
                pool.sem_inc(pool_pass, 1)

            pool.wait_ge(sorted_by, 1)
            pool.wait_ge(table_out, 16)
            gather(0, tab_h0, idxA, roundsA)
            pool.wait_ge(ring_idle, 1)
            pool.wait_ge(tabs_out, 32 * NB)
            gather(1, tab_k, idxR, roundsB)
            pool.wait_ge(ring_idle, 2)
            gather(2, tab_v, idxR, roundsB)
            pool.wait_ge(ring_idle, 3)
            pool.wait_ge(table_out, 32)
            gather(3, tab_h2, idxS, roundsB)

        @block.vector
        def _(dve):
            st = Steps(dve, dve_step)
            V = nc.vector

            def rounded(out, x, shift, scale):
                st.then(V.tensor_scalar(out, x, shift, scale, ALU.add, ALU.mult))
                st.then(V.tensor_scalar(out, out, MAGIC, -MAGIC, ALU.add, ALU.add))

            def axpy(out, x, a, y):
                st.then(V.scalar_tensor_tensor(out, x, a, y, ALU.mult, ALU.add))

            def norm(k):
                st.settle()
                st.then(V.tensor_tensor(mean[:], st6[:, :, 1], st6[:, :, 4], ALU.add))
                V.tensor_scalar(mean[:], mean[:], 0.5, None, ALU.mult)
                V.tensor_tensor(half[:], st6[:, :, 1], st6[:, :, 4], ALU.subtract)
                st.then(V.tensor_tensor(var[:], st6[:, :, 2], st6[:, :, 5], ALU.add))
                st.then(V.tensor_tensor(half[:], half[:], half[:], ALU.mult))
                st.then(V.tensor_scalar(half[:], half[:], 0.25, None, ALU.mult))
                V.scalar_tensor_tensor(var[:], var[:], 1.0 / D, half[:], ALU.mult, ALU.add).then_inc(var_ready, 1)
                dve.wait_ge(std_ready, k)
                st.then(V.reciprocal(rstd[:], std[:]))
                V.scalar_tensor_tensor(shift[:], mean[:], -1.0, rstd[:], ALU.mult, ALU.mult).then_inc(rstd_ready, 1)

            dve.wait_ge(cols_made, 1)
            V.tensor_copy(col16[:], col[:])
            V.memset(ones[:], 1.0)
            V.memset(ones16[:], 1.0)
            V.memset(ones128[:], 1.0)
            V.memset(zeros16[:], 0.0)
            V.memset(eps[:], EPS)
            V.memset(wout[:], 0.0)
            V.tensor_scalar(col1[:], col[:, 0:128], 1.0, None, ALU.add)
            V.tensor_scalar(col1_16[:], col[:, 0:128], 1.0, None, ALU.add)
            V.tensor_scalar(ident[:], col[:, 0:128], lane[:, 0:1], None, ALU.is_equal)
            V.tensor_scalar(identb[:], col[:, 0:128], lane[:, 0:1], None, ALU.is_equal)
            V.tensor_scalar(after[:], col[:, 0:128], lane[:, 0:1], None, ALU.is_gt)
            V.tensor_scalar(after16[:], col[:, 0:128], lane[:, 0:1], -1.0, ALU.is_gt, ALU.add).then_inc(consts, 1)
            dve.wait_ge(consts, 1)
            dve.wait_ge(edges_in, 80)
            V.tensor_copy(src, src_i)
            V.tensor_copy(dst, dst_i)
            V.tensor_copy(r16, r16_i)
            V.tensor_copy(rec[:, :, 1], ew)
            st.then(V.tensor_copy(r8, r8_i))
            st.then(V.tensor_scalar(tmp, dst, float(D), None, ALU.is_lt))
            st.then(V.scalar_tensor_tensor(tmp, src, float(D), tmp, ALU.is_lt, ALU.mult))
            axpy(rec[:, :, 0], src, float(D), dst)
            V.tensor_tensor_scan(incl, ones[:], tmp, 0.0, ALU.mult, ALU.add).then_inc(tot_ready, 1)
            dve.wait_ge(tot_ready, 1)
            dve.wait_ge(tot_summed, 1)
            V.tensor_scalar(rowoff[:, 0:1], ps[0:PL, 0, 0:1], -1.0 - FAR, None, ALU.add)
            rounded(rowoff[:, 1:2], ps[0:PL, 0, 1:2], (ET - 1) / 2.0, 1.0 / ET)
            V.scalar_tensor_tensor(incl, incl, rowoff[:, 0:1], tmp, ALU.add, ALU.mult)
            st.then(V.tensor_scalar(n_list[:], rowoff[:, 1:2], 1.0, None, ALU.max))
            V.tensor_scalar(dest, incl, FAR, None, ALU.add).then_inc(dest_ready, 1)

            rounded(s_lane, src, -float(NB // 2), 1.0 / NB)
            axpy(s_tile, s_lane, -float(NB), src)
            rounded(d_lane, dst, -float(NB // 2), 1.0 / NB)
            axpy(d_tile, d_lane, -float(NB), dst)
            rounded(fa[:, 1, :], dst, -3.5, 1.0 / 8)
            axpy(tmp, fa[:, 1, :], -8.0, dst)
            st.then(V.tensor_scalar(tmp, tmp, 256.0, 1.0, ALU.mult, ALU.add))
            st.then(V.tensor_tensor(fa[:, 0, :], tmp, s_lane, ALU.add))
            axpy(tmp, r16, 128.0, d_lane)
            st.then(V.tensor_scalar(fb[:, 0, :], tmp, 1.0, None, ALU.add))
            axpy(tmp, src, float(NR), r8)
            rounded(fb[:, 1, :], tmp, -7.5, 1.0 / 16)
            axpy(fb[:, 2, :], fb[:, 1, :], -16.0, tmp)

            dve.wait_ge(x_in_s, 16)
            with dve.Fori(0, NB) as b:
                st.enter(b, 1)
                st.mark(V.bn_stats(st6[:, bass.ds(b, 1), :], x[:, bass.ds(b, 1), :]))
                st.leave(NB)
            norm(1)

            def rank(which, key, pairs, rings):
                V.memset(pos, 0.0)
                V.memset(pairs[:, 0:1], 0)
                st.then(V.memset(base, 0.0))
                with dve.Fori(0, NB) as b:
                    st.enter(b, 8)
                    V.tensor_scalar(keyhot, key, col[0:PL, bass.ds(b, 1)], None, ALU.is_equal).then_inc(key_ready, 1)
                    dve.wait_ge(key_counted, b + (1 + which * NB))
                    st.then(V.tensor_tensor_scan(incl, ones[:], ps[0:PL, 0, 0:EJ], 0.0, ALU.mult, ALU.add))
                    st.then(V.tensor_tensor(tmp, incl, ps[0:PL, 1, 0:EJ], ALU.add))
                    st.then(V.scalar_tensor_tensor(tmp, tmp, base, keyhot, ALU.add, ALU.mult))
                    st.mark(V.tensor_tensor(pos, pos, tmp, ALU.add))
                    st.then(V.tensor_scalar(rnd, incl[:, EJ - 1:EJ], ET - 0.5, 0.5 / ET, ALU.add, ALU.mult))
                    st.then(V.tensor_scalar(rnd, rnd, MAGIC, MAGIC + 2.0, ALU.add, ALU.max))
                    st.then(V.tensor_scalar(rnd, rnd, -MAGIC, 2.0 * ET, ALU.add, ALU.mult))
                    V.tensor_tensor(base, base, rnd, ALU.add).then_inc(base_ready, 1)
                    dve.wait_ge(base_ready, b + (1 + which * NB))
                    st.then(V.tensor_scalar(pairs[:, bass.ds(b + 1, 1)], base, 0.5 / ET, None, ALU.mult))
                    st.leave(NB)
                rounded(rnd, base, (ROUND // 2 + 1.0) * ET, 1.0 / (ROUND * ET))
                V.tensor_copy(rings[:], rnd)
                rounded(to_tile, pos, -(ET - 1) / 2.0, 1.0 / ET)
                axpy(to_lane, to_tile, -float(ET), pos)

            def place(which, fields, nf):
                def hots(n, j):
                    V.tensor_scalar(tilehot[:, n, :], col16[0:PL, :], to_tile[:, j], None, ALU.is_equal)
                    for f in range(nf):
                        last = V.tensor_scalar(lanehot[:, n, f, :], col16[0:PL, 0:ET], to_lane[:, j], fields[:, f, j],
                                               ALU.is_equal, ALU.mult)
                    last.then_inc(hot_ready, 1)

                for n in range(4):
                    hots(n, slice(n, n + 1))
                with dve.Fori(1, EJ // 4) as i:
                    for n in range(4):
                        dve.wait_ge(hot_placed, i * 4 + (n + which * EJ - 3))
                        hots(n, bass.ds(i * 4 + n, 1))
                dve.wait_ge(hot_placed, (which + 1) * EJ)

            rank(0, s_tile, pairsA, roundsA)
            place(0, fa, 2)
            rounded(dec, ps[:, 2, 0:NT], -64.0, 1.0 / 256)
            axpy(locA[:], dec, -256.0, ps[:, 2, 0:NT])
            axpy(dec, ps[:, 3, 0:NT], 8.0, dec)
            V.tensor_copy(idxA[:], dec).then_inc(sorted_by, 1)
            st.settle()
            dve.wait_ge(sorted_by, 1)

            def edge_hots(s, loc, n, t):
                dve.wait_ge(row_used[s], t + (RING - 1))
                V.tensor_scalar(hot[:, n, :], col1[:], loc[:, bass.ds(t, 1)], None, ALU.is_equal).then_inc(hot_made[s], 1)

            with dve.Fori(0, NB) as b:
                lo, hi = bounds(dve, pairsA, b)
                with dve.Fori(lo, hi) as P:
                    for n in range(2):
                        edge_hots(0, locA, n, P * 2 + n)

            rank(1, d_tile, pairsB, roundsB)
            place(1, fb, 3)
            rounded(relB[:], ps[:, 2, 0:NT], -62.5, 1.0 / 128)
            axpy(locB[:], relB[:], -128.0, ps[:, 2, 0:NT])
            st.then(V.tensor_copy(dec2, ps[:, 4, 0:NT]))
            axpy(dec2, ps[:, 3, 0:NT], 16.0, dec2)
            V.tensor_copy(idxR[:], dec2)
            rounded(dec, dec2, -3.5, 1.0 / NR)
            V.tensor_copy(idxS[:], dec).then_inc(sorted_by, 1)
            st.settle()
            dve.wait_ge(sorted_by, 2)

            V.memset(bdk, 0.0)
            V.memset(bdm, 0.0).then_inc(blocks_cleared, 1)

            dve.wait_ge(small_in, 16 * 7)
            dve.wait_ge(bucket_read[0], NB + 1)
            with dve.Fori(0, NB) as b:
                bb = bass.ds(b, 1)
                V.scalar_tensor_tensor(row_b[:], flat(h[:, bb, :]), w_sb[:, 0:1], flat(acc[:, bb, 0:D]),
                                       ALU.mult, ALU.add).then_inc(y_ready, 1)
                dve.wait_ge(o_made, b + 1)
                V.scalar_tensor_tensor(row_b[:], ps[0:PL, 3, 0:D], 0.0, flat(h[:, bb, :]), ALU.max, ALU.add).then_inc(n1_step, 1)
                dve.wait_ge(n1_step, b * 3 + 1)
                V.tensor_tensor(flat(x[:, bb, :]), flat(x[:, bb, :]), row_b[:], ALU.add).then_inc(n1_step, 1)
                dve.wait_ge(n1_step, b * 3 + 2)
                V.bn_stats(flat(st6[:, bb, :]), flat(x[:, bb, :])).then_inc(n1_step, 1)
            dve.wait_ge(n1_step, NB * 3)
            norm(2)

            n_l = dve.value_load(n_list[0:1, 0:1], min_val=1, max_val=LROWS // ET)
            dve.wait_ge(ring_idle, 1)
            dve.sem_inc(l_w, 1)
            with dve.Fori(0, n_l) as t:
                def seq(k, ins):
                    ins.then_inc(l_dve, 1)
                    dve.wait_ge(l_dve, t * 8 + k)
                dve.wait_ge(l_in, t * 16 + 16)
                seq(1, V.tensor_scalar(ldiag[:], ident[:], lrec[:, 0:1], None, ALU.mult))
                seq(2, V.tensor_scalar(lsd[:, 0:1], lrec[:, 0:1], -(D - 1) / 2.0, 1.0 / D, ALU.add, ALU.mult))
                seq(3, V.tensor_scalar(lsd[:, 0:1], lsd[:, 0:1], MAGIC, -MAGIC, ALU.add, ALU.add))
                seq(4, V.scalar_tensor_tensor(lsd[:, 1:2], lsd[:, 0:1], -float(D), lrec[:, 0:1], ALU.mult, ALU.add))
                dve.wait_ge(l_pe, t * 2 + 1)
                seq(5, V.scalar_tensor_tensor(leq[:], ps[:, 0, 0:128], lrec[:, 0:1], after[:], ALU.is_equal, ALU.mult))
                seq(6, V.tensor_reduce(lsd[:, 2:3], leq[:], AX_X, ALU.max))
                seq(7, V.tensor_scalar(lsd[:, 3:4], lsd[:, 2:3], -1.0, 1.0, ALU.mult, ALU.add))
                V.tensor_scalar(lS, col[:, 0:D], lsd[:, 0:1], lsd[:, 3:4], ALU.is_equal, ALU.mult)
                V.tensor_scalar(lVC[:, 0, :], col[:, 0:D], lsd[:, 1:2], lrec[:, 1:2], ALU.is_equal, ALU.mult)
                seq(8, V.tensor_scalar(lVC[:, 1, :], col[:, 0:D], lsd[:, 1:2], None, ALU.is_equal))
                dve.wait_ge(l_act, t + 1)
                dve.sem_inc(dve_pass, 1)
                V.copy_predicated(wout[:, 0, :], lcov[:, 0, :].bitcast(I32), ps[:, 1, 0:D])
                V.copy_predicated(wout[:, 1, :], lcov[:, 1, :].bitcast(I32), ps[:, 2, 0:D]).then_inc(l_w, 1)
                dve.wait_ge(l_w, t + 2)

            dve.wait_ge(attn_in, 16 * (4 * NTY + 8))
            st.then(V.tensor_copy(half[:], nty[:]))
            st.then(V.tensor_scalar(pri[:], pri[:], DK ** -0.5, None, ALU.mult))
            dve.wait_ge(gate_ready, 1)
            for k in range(NTY):
                st.then(V.tensor_scalar(tmask[:, k, :], half[:], float(k), None, ALU.is_equal))
                V.tensor_scalar(gmask[:, k, :], tmask[:, k, :], skip[:, k:k + 1], None, ALU.mult)
            for cc in range(2):
                for two in range(2):
                    blk = bdk[:, cc, :, 64 * two:64 * two + 64]
                    st.mark(V.tensor_tensor(blk, blk, pri[:, :, 2 * cc + two:2 * cc + two + 1].broadcast_to([128, NR, 64]), ALU.mult))
            st.settle()

            with dve.Fori(0, NB) as b:
                bb = bass.ds(b, 1)
                dve.wait_ge(typed_turned, b + 1)
                for k in range(NTY):
                    last = V.tensor_scalar(diag[:, k, :], ident[0:PL, 0:PL], tmask[:, k, bb], None, ALU.mult)
                last.then_inc(diag_made, 1)
                dve.wait_ge(kvq_made, b + 1)
                V.tensor_copy(flat(q[:, bb, :]), ps[0:PL, 0, 0:D]).then_inc(q_copied, 1)
                dve.wait_ge(stage_free, b + 1)
                for g in range(4):
                    dve.wait_ge(bank_full, b * 8 + (2 * g + 3))
                    V.tensor_copy((stage_k, stage_v)[g // 2][:, 4:8, 128 * (g % 2):128 * (g % 2) + 128],
                                  ps[0:PL, 4 + (2 * g + 1) % 4, :].rearrange("p (r n) -> p r n", r=4)).then_inc(bank_read_v, 1)

            dve.wait_ge(tabs_out, 32 * NB)
            V.memset(relt, 0.0).then_inc(relt_cleared, 1)
            st.then(V.memset(pick, 0.0))
            st.then(V.memset(pick[:, NE16:NE16 + 1], 1.0))
            V.tensor_scalar(pick_h, pick, lane[0:2, 0:1], None, ALU.mult)

            total = pairs_in_all(dve, pairsB)
            K3, K = 6 * NH, 2 * NH
            st.then(V.tensor_tensor(sel1, ident[0:K3, 0:K], ident[0:K3, K:2 * K], ALU.add))
            st.then(V.tensor_tensor(sel1, sel1, ident[0:K3, 2 * K:3 * K], ALU.add))
            st.then(V.tensor_copy(sel, sel1.rearrange("p (k a) -> p k a", a=1).broadcast_to([K3, K, PL])))

            def mark_hots(hots, P):
                return V.tensor_tensor(hots[:], col1[:].rearrange("p (n e) -> p n e", n=1).broadcast_to([128, 2, 128]),
                                       locB[:, bass.ds(P * 2, 2)].rearrange("p (n e) -> p n e", e=1).broadcast_to([128, 2, 128]), ALU.is_equal)

            def turn_hots(s, P):
                dve.wait_ge(hot_turned[s], P + 1)
                mark_hots(hot16, P).then_inc(hot_made[s], 1)

            def scores(P):
                dve.wait_ge(q_edge, P * 2 + 4)
                dve.wait_ge(row_ready[1], P * 2 + 4)
                V.tensor_tensor(prod, ps[:, 2:4, 0:D], rows[:, bass.ds(P % (RING // 2) * 2, 2), :], ALU.mult).then_inc(row_used[1], 2)
                turn_hots(1, P + 2)
                dve.wait_ge(score_kept, P + 1)
                dve.wait_ge(row_used[1], P * 2 + (RING + 2))
                V.tensor_reduce(s4.rearrange("p n h -> p (n h)"), prod.rearrange("p n (h d) -> p (n h) d", h=NH), AX_X, ALU.add).then_inc(s_ready, 1)
                flat4 = s4.rearrange("p n h -> p (n h)")

                def seq(k, ins):
                    ins.then_inc(s_split, 1)
                    dve.wait_ge(s_split, P * 4 + k)
                dve.wait_ge(s_ready, P + 1)
                seq(1, V.tensor_copy(s_parts[:, 0, :], flat4))
                seq(2, V.tensor_tensor(s_rest, flat4, s_parts[:, 0, :], ALU.subtract))
                seq(3, V.tensor_copy(s_parts[:, 1, :], s_rest))
                V.tensor_tensor(s_parts[:, 2, :], s_rest, s_parts[:, 1, :], ALU.subtract).then_inc(s_split, 1)

            def largest(P):
                dve.wait_ge(tile_done[1], P + 1)
                dve.wait_ge(m_step, P + 1)
                V.tensor_reduce(m_new[0:PL, :], ps[0:PL, bass.ds(P % 2 * 2 + 4, 2), :].rearrange("p n (h e) -> p h n e", h=NH),
                                AX_XY, ALU.max).then_inc(max_read, 1)
                dve.wait_ge(max_read, P + 3)
                V.tensor_tensor(m_run[0:PL, :], m_run[0:PL, :], m_new[0:PL, :], ALU.max).then_inc(m_step, 1)

            def node_tile_done(b, P):
                dve.wait_ge(m_step, P + 2)
                V.tensor_copy(flat(m_all[:, bass.ds(b, 1), :]), m_run[0:PL, :]).then_inc(m_bucket, 1)
                dve.wait_ge(m_bucket, b + 1)
                V.memset(m_run, LOW).then_inc(m_cleared, 1)
                dve.wait_ge(m_cleared, b + 2)
                dve.sem_inc(dve_pass, 1)

            V.memset(m_run, LOW).then_inc(m_cleared, 1)
            dve.wait_ge(m_cleared, 1)
            turn_hots(1, 0)
            turn_hots(1, 1)
            scores(0)
            lo, hi = bounds(dve, pairsB, 0)
            with dve.Fori(1, hi) as P:
                scores(P)
                largest(P - 1)
            with dve.Fori(1, NB) as b:
                lo, hi = bounds(dve, pairsB, b, 2)
                scores(lo)
                largest(lo - 1)
                node_tile_done(b - 1, lo - 1)
                with dve.Fori(lo + 1, hi) as P:
                    scores(P)
                    largest(P - 1)
            largest(total - 1)
            node_tile_done(NB - 1, total - 1)
            spare_rows(dve, 1, pairsB, roundsB)

            def exps(P):
                dve.wait_ge(ex_ready, P + 1)
                dve.wait_ge(m_edge, P + 2)
                V.tensor_tensor(sd4, score[:, bass.ds(P * 2, 2), :], ps[:, 2, 0:2 * NH].rearrange("p (n h) -> p n h", n=2),
                                ALU.subtract).then_inc(sd_ready, 1)
                turn_hots(2, P + 2)

            def weighted(P):
                dve.wait_ge(tile_done[2], P * 2 + 4)
                mark_hots(hot, P)
                dve.wait_ge(ex_ready, P + 2)
                dve.wait_ge(row_ready[2], P * 2 + 4)
                pair = bass.ds(P % 2 * 2, 2)
                V.tensor_copy(wrow[:, :, D:D + NH], ex4[:, pair, :])
                V.tensor_tensor(wrow[:, :, 0:D].rearrange("p n (h d) -> p n h d", h=NH),
                                rows[:, bass.ds(P % (RING // 2) * 2, 2), :].rearrange("p n (h d) -> p n h d", h=NH),
                                ex4[:, pair, :].rearrange("p n (h a) -> p n h a", a=1).broadcast_to([128, 2, NH, DK]),
                                ALU.mult).then_inc(row_used[2], 2)

            def sums_out(b):
                dve.wait_ge(bucket_summed[2], b + 1)
                V.tensor_copy(flat(acc[:, bass.ds(b, 1), 0:D + NH]), ps[0:PL, 7, 0:D + NH]).then_inc(bucket_read[2], 1)

            dve.wait_ge(hot_made[1], total + 2)
            turn_hots(2, 0)
            turn_hots(2, 1)
            exps(0)
            lo, hi = bounds(dve, pairsB, 0)
            with dve.Fori(1, hi) as P:
                exps(P)
                weighted(P - 1)
            with dve.Fori(1, NB) as b:
                lo, hi = bounds(dve, pairsB, b, 2)
                exps(lo)
                weighted(lo - 1)
                sums_out(b - 1)
                with dve.Fori(lo + 1, hi) as P:
                    exps(P)
                    weighted(P - 1)
            weighted(total - 1)
            sums_out(NB - 1)
            spare_rows(dve, 2, pairsB, roundsB)
            dve.wait_ge(bucket_read[2], NB + 1)

            with dve.Fori(0, NB) as b:
                bb = bass.ds(b, 1)
                V.tensor_scalar(den, flat(acc[:, bb, D:D + NH]), 1e-30, None, ALU.max).then_inc(n3_step, 1)
                dve.wait_ge(n3_step, b * 5 + 1)
                V.reciprocal(rden, den).then_inc(n3_step, 1)
                dve.wait_ge(n3_step, b * 5 + 2)
                dve.wait_ge(agg_turned, b + 1)
                V.tensor_tensor(row_b[:].rearrange("p (h d) -> p h d", h=NH), flat(acc[:, bb, 0:D]).rearrange("p (h d) -> p h d", h=NH),
                                rden.rearrange("p (h a) -> p h a", a=1).broadcast_to([PL, NH, DK]), ALU.mult).then_inc(n3_step, 1)
                for k in range(NTY):
                    last = V.tensor_scalar(diag[:, k, :], ident[0:PL, 0:PL], gmask[:, k, bb], None, ALU.mult)
                last.then_inc(agg_ready, 1)
                dve.wait_ge(n3_step, b * 5 + 3)
                dve.wait_ge(att_made, b + 1)
                V.tensor_tensor(flat(x[:, bb, :]), flat(x[:, bb, :]), ps[0:PL, 0, 0:D], ALU.add).then_inc(n3_step, 1)
                dve.wait_ge(n3_step, b * 5 + 4)
                V.bn_stats(flat(st6[:, bb, :]), flat(x[:, bb, :])).then_inc(n3_step, 1)
            dve.wait_ge(n3_step, NB * 5)
            norm(3)

            st.then(V.memset(accrow[:, AW:AW + 1], 1.0))
            with dve.Fori(0, NB) as b:
                lo, hi = bounds(dve, pairsB, b)
                with dve.Fori(lo, hi) as P:
                    for n in range(2):
                        t = P * 2 + n
                        dve.wait_ge(row_used[3], t + (RING - 1))
                        V.tensor_scalar(relhot[:, n, :], col[:, 0:NE16], relB[:, bass.ds(t, 1)], None, ALU.is_equal)
                        edge_hots(3, locB, n, t)

            dve.wait_ge(bucket_read[3], NB + 1)
            with dve.Fori(0, NB) as b:
                bb = bass.ds(b, 1)

                def seq(k, ins):
                    ins.then_inc(n5_step, 1)
                    dve.wait_ge(n5_step, b * 6 + k)
                dve.wait_ge(g_turned, b + 2)
                V.tensor_copy(flat(gT), ps[:, 1, 0:4 * PL]).then_inc(gT_ready, 1)
                dve.wait_ge(rz_ready, b + 1)
                seq(1, V.tensor_tensor(gt, rz[:, 0:D], ps[0:PL, 5, 0:D], ALU.mult))
                V.tensor_tensor(gt, gt, ps[0:PL, 4, 0:D], ALU.add).then_inc(gt_ready, 1)
                dve.wait_ge(gn_ready, b + 1)
                seq(2, V.tensor_tensor(gt, flat(h[:, bb, :]), gn, ALU.subtract))
                seq(3, V.tensor_tensor(gt, gt, rz[:, D:2 * D], ALU.mult))
                seq(4, V.tensor_tensor(gt, gt, gn, ALU.add))
                seq(5, V.tensor_tensor(flat(x[:, bb, :]), flat(x[:, bb, :]), gt, ALU.add))
                seq(6, V.bn_stats(flat(st6[:, bb, :]), flat(x[:, bb, :])))
            norm(4)

            with dve.Fori(0, NB) as b:
                bb = bass.ds(b, 1)
                dve.wait_ge(f_made, b + 1)
                V.tensor_tensor(flat(x[:, bb, :]), flat(x[:, bb, :]), ps[0:PL, 2, 0:D], ALU.add).then_inc(out_ready, 1)

        @block.scalar
        def _(act):
            A = nc.scalar

            def norm(k):
                act.wait_ge(var_ready, k)
                A.activation(std[:], var[:], ACT.Sqrt, bias=eps[:, 0:1]).then_inc(std_ready, 1)
                act.wait_ge(rstd_ready, k)
                if k in (2, 4):
                    act.wait_ge(table_out, 8 * k)
                with act.Fori(0, NB) as b:
                    bb = bass.ds(b, 1)
                    A.activation(flat(h[:, bb, :]), flat(x[:, bb, :]), ACT.Relu, bias=shift[:, bb],
                                 scale=rstd[:, bb]).then_inc(h_rows, 1)
                act.wait_ge(h_rows, k * NB)

            norm(1)
            act.wait_ge(dest_ready, 1)
            for n in range(4):
                A.copy(dslot[:, n, :], dest[:, n:n + 1])
                A.copy(rslot[:, n, :], rec[:, n, :]).then_inc(slot_ready, 1)
            with act.Fori(1, EJ // 4) as i:
                for n in range(4):
                    j = bass.ds(i * 4 + n, 1)
                    act.wait_ge(scattered[n], i * 16)
                    A.copy(dslot[:, n, :], dest[:, j])
                    A.copy(rslot[:, n, :], flat(rec[:, j, :])).then_inc(slot_ready, 1)

            act.wait_ge(list_filled, 16)
            with act.Fori(0, NB) as b:
                act.wait_ge(bucket_summed[0], b + 1)
                A.copy(flat(acc[:, bass.ds(b, 1), 0:D]), ps[0:PL, 7, 0:D]).then_inc(bucket_read[0], 1)
            with act.Fori(0, NB) as b:
                act.wait_ge(y_turned, b + 1)
                A.copy(flat(rowT[:]), ps[:, 1, 0:2 * PL]).then_inc(yT_ready, 1)
                act.wait_ge(h1_made, b + 1)
                A.activation(h1T[:], ps[0:H1, 2, 0:PL], ACT.Relu).then_inc(h1_relu, 1)
                act.wait_ge(h2_made, b + 1)
                A.activation(h2T[:], ps[0:H2, 4, 0:PL], ACT.Relu).then_inc(h2_relu, 1)
            norm(2)
            n_l = act.value_load(n_list[0:1, 0:1], min_val=1, max_val=LROWS // ET)
            with act.Fori(0, n_l) as t:
                act.wait_ge(l_pe, t * 2 + 2)
                A.copy(lcov[:, 0, :], ps[:, 1, D:2 * D])
                A.copy(lcov[:, 1, :], ps[:, 2, D:2 * D]).then_inc(l_act, 1)
            A.activation(skip[:], skip[:], ACT.Sigmoid).then_inc(gate_ready, 1)
            with act.Fori(0, NB) as b:
                act.wait_ge(typed_turned, b + 1)
                A.copy(row_b[:], flat(h[:, bass.ds(b, 1), :])).then_inc(hrow_ready, 1)
                act.wait_ge(typed_turned, b + 2)
                A.copy(typedT[:], ps[:, 1:3, 0:NTY * PL]).then_inc(typedT_ready, 1)
                act.wait_ge(kvq_made, b + 1)
                A.copy(flat(kvT[:]), ps[:, 3, 0:4 * PL]).then_inc(kvT_ready, 1)
                act.wait_ge(stage_free, b + 1)
                for g in range(4):
                    act.wait_ge(bank_full, b * 8 + (2 * g + 2))
                    A.copy((stage_k, stage_v)[g // 2][:, 0:4, 128 * (g % 2):128 * (g % 2) + 128],
                           ps[0:PL, 4 + (2 * g) % 4, :].rearrange("p (r n) -> p r n", r=4)).then_inc(bank_read_a, 1)

            total = pairs_in_all(act, pairsB)

            both = ps[0:PL, 0, 0:128].bitcast(BF16).rearrange("p (n e) -> p n e", n=2)

            def others(P):
                act.wait_ge(hot_turned[1], P + 2)
                A.activation(neg[0:PL, bass.ds(P % 4, 1), :, :].rearrange("p a n e -> p (a n) e"), both, ACT.Copy, scale=-LOW, bias=LOW)

            def turned_1(P):
                act.wait_ge(q_edge, P * 2 + 2)
                A.copy(hotT[0:PL, :, :], both).then_inc(hotT_made[1], 1)

            def score_rows(P):
                act.wait_ge(s_turned, P + 1)
                A.copy(sT, ps[0:6 * NH, 1, 0:64].bitcast(BF16)).then_inc(sT_ready, 1)
                A.copy(score[:, bass.ds(P * 2, 2), :], s4).then_inc(score_kept, 1)

            for k in range(2):
                others(k)
                turned_1(k)
            with act.Fori(1, total) as P:
                others(P + 1)
                score_rows(P - 1)
                turned_1(P + 1)
            score_rows(total - 1)

            def turned_2(P):
                act.wait_ge(hot_turned[2], P + 2)
                act.wait_ge(m_edge, P + 1)
                A.copy(hotT[0:PL, :, :], both).then_inc(hotT_made[2], 1)

            def exps(P):
                act.wait_ge(sd_ready, P + 2)
                act.wait_ge(row_used[2], P * 2 + (RING - 2))
                A.activation(ex4[:, bass.ds(P % 2 * 2, 2), :], sd4, ACT.Exp).then_inc(ex_ready, 1)

            turned_2(0)
            turned_2(1)
            exps(0)
            with act.Fori(1, total) as P:
                turned_2(P + 1)
                exps(P)
            with act.Fori(0, NB) as b:
                act.wait_ge(agg_turned, b + 2)
                A.copy(typedT[:], ps[:, 1:3, 0:NTY * PL]).then_inc(aggT_ready, 1)
            norm(3)
            act.wait_ge(relw_made, 1)
            A.copy(relw[:, 0:2 * D], ps[0:NE16 + 1, 1, :])
            A.copy(relw[:, 2 * D:3 * D], ps[0:NE16 + 1, 2, 0:D])
            A.copy(bhn, ps[0:NE16 + 1, 2, D:2 * D]).then_inc(relw_ready, 1)
            with act.Fori(0, NB) as b:
                act.wait_ge(bucket_summed[3], b + 1)
                A.copy(flat(acc[:, bass.ds(b, 1), :]), ps[0:PL, 7, 0:AW]).then_inc(bucket_read[3], 1)
            act.wait_ge(bucket_read[3], NB + 1)
            with act.Fori(0, NB) as b:
                bb = bass.ds(b, 1)
                act.wait_ge(g_turned, b + 1)
                A.copy(accrow[:, 0:AW], flat(acc[:, bb, :]))
                A.copy(row_b[:], flat(h[:, bb, :])).then_inc(g_rows, 1)
                act.wait_ge(g_turned, b + 2)
                A.copy(cntT, ps[0:NE16 + 1, 2, 0:PL]).then_inc(cntT_ready, 1)
                act.wait_ge(gates_made, b + 1)
                A.activation(rz, ps[0:PL, 3, :], ACT.Sigmoid).then_inc(rz_ready, 1)
                act.wait_ge(gt_ready, b + 2)
                A.activation(gn, gt, ACT.Tanh).then_inc(gn_ready, 1)
            norm(4)
            with act.Fori(0, NB) as b:
                act.wait_ge(f_turned, b + 1)
                A.copy(row_b[:], flat(h[:, bass.ds(b, 1), :])).then_inc(f_row, 1)
                act.wait_ge(f_turned, b + 2)
                A.copy(flat(rowT[:]), ps[:, 1, 0:2 * PL]).then_inc(fT_ready, 1)

        @block.tensor
        def _(pe):
            M = nc.tensor.matmul
            for one in (q_edge, *row_ready):
                pe.sem_inc(one, 2)
            pe.sem_inc(tile_done[2], 4)
            for one in (hot_turned[1], hot_turned[2], hotT_made[1], hotT_made[2], m_edge, score_kept, m_step, ex_ready, sd_ready):
                pe.sem_inc(one, 1)
            pe.sem_inc(bank_read_a, 2)
            pe.sem_inc(bank_read_v, 2)
            pe.sem_inc(max_read, 2)
            for one in (typed_turned, q_copied, agg_turned, g_turned, f_turned, gt_ready, out_ready, bank_full,
                        bucket_read[0], bucket_read[2], bucket_read[3]):
                pe.sem_inc(one, 1)
            pe.wait_ge(consts, 1)
            pe.wait_ge(tot_ready, 1)
            M(ps[0:PL, 0, 0:1], after[0:PL, 0:PL], incl[:, EJ - 1:EJ], start=True, stop=True)
            M(ps[0:PL, 0, 1:2], ones[0:PL, 0:PL], incl[:, EJ - 1:EJ], start=True, stop=True).then_inc(tot_summed, 1)

            def count_keys(which):
                with pe.Fori(0, NB) as b:
                    pe.wait_ge(key_ready, b + (1 + which * NB))
                    M(ps[0:PL, 0, 0:EJ], ones16[0:PL, 0:PL], keyhot, start=True, stop=True)
                    M(ps[0:PL, 1, 0:EJ], after16[0:PL, 0:PL], keyhot, start=True, stop=True).then_inc(key_counted, 1)

            def place_edges(which, nf):
                def products(n, start, stop):
                    for f in range(nf):
                        last = M(ps[:, 2 + f, 0:NT], lanehot[:, n, f, :], tilehot[:, n, :], start=start, stop=stop)
                    last.then_inc(hot_placed, 1)

                for n in range(4):
                    pe.wait_ge(hot_ready, which * EJ + n + 1)
                    products(n, n == 0, False)
                with pe.Fori(1, EJ // 4 - 1) as i:
                    for n in range(4):
                        pe.wait_ge(hot_ready, i * 4 + (which * EJ + n + 1))
                        products(n, False, False)
                for n in range(4):
                    pe.wait_ge(hot_ready, which * EJ + EJ - 3 + n)
                    products(n, False, n == 3)

            def open_sum(width):
                M(ps[0:PL, 7, 0:width], zeros16[0:1, 0:PL], zeros16[0:1, 0:width], start=True, stop=False)

            def close_sum(s, width):
                M(ps[0:PL, 7, 0:width], zeros16[0:1, 0:PL], zeros16[0:1, 0:width], start=False, stop=True).then_inc(bucket_summed[s], 1)

            count_keys(0)
            place_edges(0, 2)
            pe.wait_ge(sorted_by, 1)
            with pe.Fori(0, NB) as b:
                lo, hi = bounds(pe, pairsA, b)
                pe.wait_ge(bucket_read[0], b + 1)
                open_sum(D)
                with pe.Fori(lo, hi) as P:
                    for n in range(2):
                        t = P * 2 + n
                        pe.wait_ge(hot_made[0], t + 1)
                        pe.wait_ge(row_ready[0], t + 3)
                        M(ps[0:PL, 7, 0:D], hot[:, n, 0:PL], flat(rows[:, bass.ds(P % (RING // 2) * 2 + n, 1), :]),
                          start=False, stop=False).then_inc(row_used[0], 1)
                close_sum(0, D)
            spare_rows(pe, 0, pairsA, roundsA)
            count_keys(1)
            place_edges(1, 3)

            pe.wait_ge(small_in, 16 * 7)
            with pe.Fori(0, NB) as b:
                pe.wait_ge(y_ready, b + 1)
                nc.tensor.transpose(ps[:, 1, 0:PL], row_b[:, 0:128], ident[0:PL, 0:PL])
                nc.tensor.transpose(ps[:, 1, PL:2 * PL], row_b[:, 128:256], ident[0:PL, 0:PL]).then_inc(y_turned, 1)
                pe.wait_ge(yT_ready, b + 1)
                M(ps[0:H1, 2, 0:PL], w1t[:, 0, :], rowT[:, 0, :], start=True, stop=False)
                M(ps[0:H1, 2, 0:PL], w1t[:, 1, :], rowT[:, 1, :], start=False, stop=True).then_inc(h1_made, 1)
                pe.wait_ge(h1_relu, b + 1)
                pe.sem_inc(pe_pass, 1)
                M(ps[0:H2, 4, 0:PL], w2t[:], h1T[:], start=True, stop=True).then_inc(h2_made, 1)
                pe.wait_ge(h2_relu, b + 1)
                M(ps[0:PL, 3, 0:D], h2T[:], w3t[:], start=True, stop=True).then_inc(o_made, 1)

            n_l = pe.value_load(n_list[0:1, 0:1], min_val=1, max_val=LROWS // ET)
            with pe.Fori(0, n_l) as t:
                pe.wait_ge(l_dve, t * 8 + 1)
                M(ps[:, 0, 0:128], ones128[:], ldiag[:], start=True, stop=True).then_inc(l_pe, 1)
                pe.wait_ge(l_dve, t * 8 + 8)
                M(ps[:, 1, :], lS[:, 0:128], flat(lVC), start=True, stop=True)
                M(ps[:, 2, :], lS[:, 128:256], flat(lVC), start=True, stop=True).then_inc(l_pe, 1)

            with pe.Fori(0, NB) as b:
                pe.wait_ge(hrow_ready, b + 1)
                pe.wait_ge(diag_made, b + 1)
                M(ps[:, 1, 0:NTY * PL], row_b[:, 0:128], flat(diag[:]), start=True, stop=True)
                M(ps[:, 2, 0:NTY * PL], row_b[:, 128:256], flat(diag[:]), start=True, stop=True).then_inc(typed_turned, 1)
                pe.wait_ge(typedT_ready, b + 1)
                pe.wait_ge(q_copied, b + 1)
                for g in range(4):
                    w, o = (wk, wv)[g // 2], 128 * (g % 2)
                    for k in range(NTY):
                        for cc in range(2):
                            M(ps[:, 3, g * PL:g * PL + PL], w[:, k, cc, o:o + 128], typedT[:, cc, k * PL:k * PL + PL],
                              start=(k == 0 and cc == 0), stop=(k == NTY - 1 and cc == 1))
                for k in range(NTY):
                    for cc in range(2):
                        last = M(ps[0:PL, 0, 0:D], typedT[:, cc, k * PL:k * PL + PL], wq[:, k, cc, :],
                                 start=(k == 0 and cc == 0), stop=(k == NTY - 1 and cc == 1))
                last.then_inc(kvq_made, 1)
                pe.wait_ge(kvT_ready, b + 1)
                for m in range(8):
                    pe.wait_ge((bank_read_a, bank_read_v)[m % 2], b * 4 + (m // 2 + 1))
                    M(ps[0:PL, 4 + m % 4, :], kvT[:, m // 2, :], flat((bdk, bdm)[m // 4][:, m // 2 % 2, 4 * (m % 2):4 * (m % 2) + 4, :]),
                      start=True, stop=True).then_inc(bank_full, 1)

            total = pairs_in_all(pe, pairsB)

            def turn_hots(s, P):
                pe.wait_ge(hot_made[s], P + 1)
                pe.wait_ge(hotT_made[s], P + 1)
                nc.tensor.transpose(ps[0:PL, 0, 0:64].bitcast(BF16), hot16[:, 0, 0:PL], identb[:])
                nc.tensor.transpose(ps[0:PL, 0, 64:128].bitcast(BF16), hot16[:, 1, 0:PL], identb[:]).then_inc(hot_turned[s], 1)

            def turn_scores(P):
                pe.wait_ge(s_split, P * 4 + 4)
                nc.tensor.transpose(ps[0:6 * NH, 1, 0:64].bitcast(BF16), s_parts.rearrange("p a k -> p (a k)"), identb[:]).then_inc(s_turned, 1)

            def queries(b, P):
                turn_hots(1, P + 1)
                pe.wait_ge(hotT_made[1], P + 2)
                for n in range(2):
                    pe.wait_ge(row_used[1], P * 2 + RING)
                    M(ps[:, 2 + n, 0:D], hotT[0:PL, n, :], flat(q[:, bass.ds(b, 1), :]), start=True, stop=True).then_inc(q_edge, 1)

            def spread(P):
                pe.wait_ge(max_read, P + 1)
                banks = [bass.ds(P % 2 * 2 + (4 + n), 1) for n in range(2)]
                for n, bank in enumerate(banks):
                    M(ps[0:PL, bank, :].rearrange("p a (h e) -> p (a h) e", h=NH), identb[0:PL, 0:PL],
                      neg[0:PL, bass.ds(P % 4, 1), n:n + 1, :].rearrange("p a n e -> p (a n) e").broadcast_to([PL, NH, 128]),
                      start=True, stop=False)
                pe.wait_ge(sT_ready, P + 1)
                pe.sem_inc(pe_pass, 1)
                for n, bank in enumerate(banks):
                    for k in range(NH):
                        last = M(flat(ps[0:PL, bank, 128 * k:128 * k + 128]), sel[:, n * NH + k, :], sT, start=False, stop=k == NH - 1)
                last.then_inc(tile_done[1], 1)

            turn_hots(1, 0)
            queries(0, 0)
            lo, hi = bounds(pe, pairsB, 0)
            with pe.Fori(1, hi) as P:
                queries(0, P)
                turn_scores(P - 1)
                spread(P - 1)
            with pe.Fori(1, NB) as b:
                lo, hi = bounds(pe, pairsB, b, 2)
                queries(b, lo)
                turn_scores(lo - 1)
                spread(lo - 1)
                with pe.Fori(lo + 1, hi) as P:
                    queries(b, P)
                    turn_scores(P - 1)
                    spread(P - 1)
            turn_scores(total - 1)
            spread(total - 1)

            def largest(b, P):
                turn_hots(2, P + 1)
                pe.wait_ge(hotT_made[2], P + 2)
                pe.wait_ge(sd_ready, P + 1)
                for n in range(2):
                    last = M(ps[:, 2, n * NH:n * NH + NH], hotT[0:PL, n, :], flat(m_all[:, bass.ds(b, 1), :]), start=True, stop=True)
                last.then_inc(m_edge, 1)

            def add(P):
                pe.wait_ge(row_used[2], P * 2 + (RING + 2))
                for n in range(2):
                    M(ps[0:PL, 7, 0:D + NH], hot[:, n, 0:PL], wrow[:, n, :], start=False, stop=False).then_inc(tile_done[2], 1)

            pe.wait_ge(m_bucket, NB)
            pe.wait_ge(hotT_made[1], total + 2)
            turn_hots(2, 0)
            pe.wait_ge(bucket_read[2], 1)
            open_sum(D + NH)
            largest(0, 0)
            lo, hi = bounds(pe, pairsB, 0)
            with pe.Fori(1, hi) as P:
                largest(0, P)
                add(P - 1)
            with pe.Fori(1, NB) as b:
                lo, hi = bounds(pe, pairsB, b, 2)
                largest(b, lo)
                add(lo - 1)
                close_sum(2, D + NH)
                pe.wait_ge(bucket_read[2], b + 1)
                open_sum(D + NH)
                with pe.Fori(lo + 1, hi) as P:
                    largest(b, P)
                    add(P - 1)
            add(total - 1)
            close_sum(2, D + NH)
            with pe.Fori(0, NB) as b:
                pe.wait_ge(agg_ready, b + 1)
                M(ps[:, 1, 0:NTY * PL], row_b[:, 0:128], flat(diag[:]), start=True, stop=True)
                M(ps[:, 2, 0:NTY * PL], row_b[:, 128:256], flat(diag[:]), start=True, stop=True).then_inc(agg_turned, 1)
                pe.wait_ge(aggT_ready, b + 1)
                for k in range(NTY):
                    for cc in range(2):
                        last = M(ps[0:PL, 0, 0:D], typedT[:, cc, k * PL:k * PL + PL], wa[:, k, cc, :],
                                 start=(k == 0 and cc == 0), stop=(k == NTY - 1 and cc == 1))
                last.then_inc(att_made, 1)

            pe.wait_ge(gru_in, 64)
            for o, n, rows_b in ((0, 2 * D, 2), (2 * D, D, 1)):
                bank = ps[0:NE16 + 1, 1 + o // (2 * D), 0:n]
                M(bank, relt[:, 0, :], wih[:, 0, o:o + n], start=True, stop=False)
                M(bank, relt[:, 1, :], wih[:, 1, o:o + n], start=False, stop=False)
                M(bank, pick[0:rows_b, :], bias[0:rows_b, o:o + n], start=False, stop=True)
            M(ps[0:NE16 + 1, 2, D:2 * D], pick_h, bias[:, 2 * D:3 * D], start=True, stop=True).then_inc(relw_made, 1)

            with pe.Fori(0, NB) as b:
                lo, hi = bounds(pe, pairsB, b)
                pe.wait_ge(bucket_read[3], b + 1)
                open_sum(AW)
                with pe.Fori(lo, hi) as P:
                    for n in range(2):
                        t = P * 2 + n
                        pe.wait_ge(hot_made[3], t + 1)
                        pe.wait_ge(row_ready[3], t + 3)
                        M(ps[0:PL, 7, D:AW], hot[:, n, 0:PL], relhot[:, n, :], start=False, stop=False)
                        M(ps[0:PL, 7, 0:D], hot[:, n, 0:PL], flat(rows[:, bass.ds(P % (RING // 2) * 2 + n, 1), :]),
                          start=False, stop=False).then_inc(row_used[3], 1)
                close_sum(3, AW)
            spare_rows(pe, 3, pairsB, roundsB)

            pe.wait_ge(relw_ready, 1)
            with pe.Fori(0, NB) as b:
                pe.wait_ge(g_rows, b + 1)
                T = nc.tensor.transpose
                T(ps[:, 1, 0:PL], accrow[:, 0:128], ident[0:PL, 0:PL])
                T(ps[:, 1, PL:2 * PL], accrow[:, 128:256], ident[0:PL, 0:PL])
                T(ps[:, 1, 2 * PL:3 * PL], row_b[:, 0:128], ident[0:PL, 0:PL])
                T(ps[:, 1, 3 * PL:4 * PL], row_b[:, 128:256], ident[0:PL, 0:PL])
                T(ps[0:NE16 + 1, 2, 0:PL], accrow[:, D:AW + 1], ident[0:PL, 0:PL]).then_inc(g_turned, 1)
                pe.wait_ge(gT_ready, b + 1)
                pe.wait_ge(cntT_ready, b + 1)
                pe.wait_ge(gt_ready, b + 1)
                rzb, inb, hnb = ps[0:PL, 3, :], ps[0:PL, 4, 0:D], ps[0:PL, 5, 0:D]
                for bank, lo_, hi_ in ((rzb, 0, 2 * D), (inb, 2 * D, 3 * D)):
                    M(bank, gT[:, 0, :], wih[:, 0, lo_:hi_], start=True, stop=False)
                    M(bank, gT[:, 1, :], wih[:, 1, lo_:hi_], start=False, stop=False)
                    M(bank, cntT, relw[:, lo_:hi_], start=False, stop=bank is inb)
                M(rzb, gT[:, 2, :], whh[:, 0, 0:2 * D], start=False, stop=False)
                M(rzb, gT[:, 3, :], whh[:, 1, 0:2 * D], start=False, stop=True)
                M(hnb, gT[:, 2, :], whh[:, 0, 2 * D:3 * D], start=True, stop=False)
                M(hnb, gT[:, 3, :], whh[:, 1, 2 * D:3 * D], start=False, stop=False)
                M(hnb, cntT, bhn, start=False, stop=True).then_inc(gates_made, 1)

            with pe.Fori(0, NB) as b:
                pe.wait_ge(f_row, b + 1)
                nc.tensor.transpose(ps[:, 1, 0:PL], row_b[:, 0:128], ident[0:PL, 0:PL])
                nc.tensor.transpose(ps[:, 1, PL:2 * PL], row_b[:, 128:256], ident[0:PL, 0:PL]).then_inc(f_turned, 1)
                pe.wait_ge(fT_ready, b + 1)
                pe.wait_ge(out_ready, b + 1)
                M(ps[0:PL, 2, 0:D], rowT[:, 0, :], wout[:, 0, :], start=True, stop=False)
                M(ps[0:PL, 2, 0:D], rowT[:, 1, :], wout[:, 1, :], start=False, stop=True).then_inc(f_made, 1)


def kernel(**inputs):
    import numpy as _np
    import concourse.bacc as _bacc
    from concourse import mybir as _mybir
    from concourse.bass_utils import run_bass_kernel_spmd as _run

    def get(name):
        return _np.asarray(inputs[name])

    names = ["x", "src", "dst", "edge_type_16", "edge_type_8", "edge_weight", "node_type_4", "L0_gnn_w"]
    laid = [(n, get(n)) for n in names]
    laid += [
        ("w1t", get("L0_gnn_W1").T), ("w2t", get("L0_gnn_W2").T), ("w3t", get("L0_gnn_W3").T),
        ("wk", get("L1_gnn_k_linears")), ("wq", get("L1_gnn_q_linears")),
        ("wv", get("L1_gnn_v_linears")), ("wa", get("L1_gnn_a_linears")),
        ("att", get("L1_gnn_relation_att").transpose(3, 1, 0, 2)),
        ("msg", get("L1_gnn_relation_msg").transpose(2, 1, 0, 3)),
        ("pri", get("L1_gnn_relation_pri")), ("skip", get("L1_gnn_skip")),
        ("relt", get("L2_gnn_relvectors").T), ("wih", get("L2_gnn_w_ih").T), ("whh", get("L2_gnn_w_hh").T),
        ("bias", _np.stack([get("L2_gnn_b_ih"), get("L2_gnn_b_hh")])),
    ]
    nc = _bacc.Bacc("TRN2", target_bir_lowering=False, num_devices=1)
    arrays, args = {}, []
    for name, a in laid:
        a = _np.ascontiguousarray(a)
        arrays[f"in_{name}"] = a
        args.append(nc.dram_tensor(f"in_{name}", a.shape, _mybir.dt.from_np(a.dtype), kind="ExternalInput").ap())
    args.append(nc.dram_tensor("out_0", (N, D), _mybir.dt.float32, kind="ExternalOutput").ap())
    build(nc, *args)
    r = _run(nc, [arrays], core_ids=[0])
    return r.results[0]["out_0"]
```

```python
from collections import namedtuple
from contextlib import ExitStack

import concourse.bass as bass
from concourse import mybir

ALU = mybir.AluOpType
ACT = mybir.ActivationFunctionType
F32 = mybir.dt.float32
F16 = mybir.dt.float16
BF16 = mybir.dt.bfloat16
I32 = mybir.dt.int32
AX_X, AX_XY = mybir.AxisListType.X, mybir.AxisListType.XY

E, N, D = 50000, 3125, 256
PL = 125
NB = N // PL
EJ = E // PL
ET = 128
NP = -(-E // (2 * ET)) + 2 * (NB - 1)
EJP = 2 * NP + 2
RING = 8
ROUND = 2 * RING
NT = (2 * NP // ROUND + 1) * ROUND
NR, NH, DK, NTY, NE16 = 8, 4, 64, 4, 16
H1, H2 = 64, 32
EPS = 1e-5
MAGIC = 12582912.0
LROWS = (E // (PL * ET) + 1) * PL * ET
FAR = LROWS + 1.0
LOW = -1e30
AW = D + NE16


Sort = namedtuple("Sort", "key hots cum work pos base count pairs rings tile lane bank")


class Steps:

    def __init__(self, eng, sem):
        self.eng, self.sem, self.n, self.at = eng, sem, 0, 0

    def mark(self, ins):
        ins.then_inc(self.sem, 1)
        self.n += 1

    def settle(self):
        self.eng.wait_ge(self.sem, self.at + self.n)

    def then(self, ins):
        self.mark(ins)
        self.settle()

    def enter(self, i, per):
        self.outer, self.per = self.n, per
        self.at, self.n = self.outer + i * per, 0

    def leave(self, trips):
        assert self.n == self.per, (self.n, self.per)
        self.at, self.n = 0, self.outer + trips * self.per


class Carver:

    def __init__(self, tensor, at=0):
        self.tensor, self.at = tensor, at

    def take(self, lanes, *shape, dt=F32):
        words = 1
        for n in shape:
            words *= n
        words = (words + 1) // 2 if dt in (F16, BF16) else words
        assert self.at + words <= self.tensor.shape[1], (self.at, words)
        piece = self.tensor[0:lanes, self.at:self.at + words]
        self.at += words
        if dt != F32:
            piece = piece.bitcast(dt)
        names = "abcd"[:len(shape)]
        if len(shape) > 1:
            sizes = dict(zip(names, shape))
            piece = piece.rearrange(f"p ({' '.join(names)}) -> p {' '.join(names)}", **sizes)
        return piece


def build(nc, x_in, src_in, dst_in, r16_in, r8_in, ew_in, nty_in, w_in, w1t_in, w2t_in, w3t_in,
          wk_in, wq_in, wv_in, wa_in, att_in, msg_in, pri_in, skip_in, relt_in, wih_in, whh_in, bias_in, out):
    ctx = ExitStack()
    with ctx:
        def sb(name, shape, dt=F32):
            return ctx.enter_context(nc.sbuf_tensor(name, shape, dt))

        def sem(name):
            return ctx.enter_context(nc.semaphore(name))

        def dram(name, shape, dt=F32):
            return nc.dram_tensor(name, shape, dt).ap()

        ps = ctx.enter_context(nc.psum_tensor("ps", [128, 8, 512], F32))

        lane = sb("lane", [128, 1])
        col = sb("col", [128, NT])
        col16 = sb("col16", [128, NT], F16)
        ones = sb("ones", [PL, EJ])
        ident = sb("ident", [128, 128])
        identb = sb("identb", [128, 128], BF16)
        after = sb("after", [128, 128])
        after16 = sb("after16", [128, 128], F16)
        ones16 = sb("ones16", [128, 128], F16)
        zeros16 = sb("zeros16", [1, 512], F16)
        eps = sb("eps", [PL, 1])

        x = sb("x", [PL, NB, D])
        h = sb("h", [PL, NB, D])
        q = sb("q", [PL, NB, D])
        acc = sb("acc", [PL, NB, AW])
        m_all = sb("m_all", [PL, NB, 3 * NH], BF16)
        tmask = sb("tmask", [PL, NTY, NB])
        gmask = sb("gmask", [PL, NTY, NB])
        score = sb("score", [128, NT, NH])
        locA = sb("locA", [128, NT])
        idxA = sb("idxA", [128, NT], I32)
        locB = sb("locB", [128, NT])
        relB = sb("relB", [128, NT])
        idxR = sb("idxR", [128, NT], I32)
        idxS = sb("idxS", [128, NT], I32)
        pairsA = sb("pairsA", [PL, NB + 1], I32)
        pairsB = sb("pairsB", [PL, NB + 1], I32)
        roundsA = sb("roundsA", [PL, 1], I32)
        roundsB = sb("roundsB", [PL, 1], I32)
        ring = sb("ring", [128, RING, AW])
        rows = ring[:, :, 0:D]
        islot = sb("islot", [128, 2, RING], I32)
        wout = sb("wout", [128, 2, D])
        n_list = sb("n_list", [PL, 1], I32)

        st6 = sb("st6", [PL, NB, 6])
        mean = sb("mean", [PL, NB])
        var = sb("var", [PL, NB])
        std = sb("std", [PL, NB])
        rstd = sb("rstd", [PL, NB])
        shift = sb("shift", [PL, NB])
        half = sb("half", [PL, NB])

        w_sb = sb("w_sb", [PL, 1])
        w1t = sb("w1t", [128, 2, H1])
        w2t = sb("w2t", [H1, H2])
        w3t = sb("w3t", [H2, D])
        row_b = sb("row_b", [PL, D])
        rowT = sb("rowT", [128, 2, PL])
        h1T = sb("h1T", [H1, PL])
        h2T = sb("h2T", [H2, PL])

        arena = sb("arena", [128, 12288])
        c = Carver(arena)
        src_i, dst_i, r16_i, r8_i = (c.take(PL, EJ, dt=I32) for _ in range(4))
        ew = c.take(PL, EJ)
        bc = Carver(arena)
        tile_b, lane_b = bc.take(PL, EJP), bc.take(PL, EJP)
        tmp_b, incl_b = bc.take(PL, EJ), bc.take(PL, EJ)
        keyhot_b = bc.take(PL, EJ, dt=F16)
        assert bc.at <= c.at
        rec = c.take(PL, EJ, 2)
        src, dst, r16, r8 = (c.take(PL, EJ) for _ in range(4))
        s_lane, s_tile, d_lane, d_tile = (c.take(PL, EJ) for _ in range(4))
        fa = c.take(PL, 2, EJ)
        fb = c.take(PL, 3, EJP)
        pos_b = r16
        tmp, incl, pos, to_tile, to_lane = (c.take(PL, EJ) for _ in range(5))
        keyhot = c.take(PL, EJ, dt=F16)
        tilehot = c.take(PL, 4, NT, dt=F16)
        qc = Carver(q[:].rearrange("p b d -> p (b d)"))
        lanehot, onehot = qc.take(PL, 4, 3, ET, dt=F16), qc.take(PL, 4, ET, dt=F16)
        dest = qc.take(PL, EJ, dt=I32)
        dslot = qc.take(PL, 4, 1, dt=I32)
        rslot = qc.take(PL, 4, 2)
        base, rnd, base_b, rnd_b = (qc.take(PL, 1) for _ in range(4))
        rowoff = qc.take(PL, 2)
        fill = acc[0:PL, 0:4, :].rearrange("p a b -> p (a b)")[:, 0:LROWS * 2 // PL]
        sc = Carver(score[:].rearrange("p a b -> p (a b)"))
        dec, dec2 = sc.take(128, NT), sc.take(128, NT)

        c = Carver(arena)
        wk, wq, wv = (c.take(128, NTY, 2, D) for _ in range(3))
        wa_at = c.at
        wa = c.take(128, NTY, 2, D)
        bdk = c.take(128, 2, NR, 128)
        bdm = c.take(128, 2, NR, 128)
        ac = Carver(acc[:].rearrange("p b d -> p (b d)"))
        stage_k, stage_v = ac.take(PL, NR, D), ac.take(PL, NR, D)
        diag = sb("diag", [PL, NTY, PL])
        typedT = sb("typedT", [128, 2, NTY * PL])
        kvT = sb("kvT", [128, 4, PL])
        pri = sb("pri", [128, NR, NH])
        nty = sb("nty", [PL, NB], I32)
        skip = sb("skip", [PL, NTY])

        c = Carver(arena)
        gru_at = c.at
        hotT = c.take(128, 2, 128)
        neg = c.take(128, 4, 2, 128, dt=BF16)
        sel = c.take(6 * NH, 2 * NH, PL, dt=BF16)
        sel1 = c.take(6 * NH, 2 * NH)
        s_parts = c.take(128, 3, 2 * NH, dt=BF16)
        sT = c.take(6 * NH, 128, dt=BF16)
        prod = c.take(128, 2, D)
        s_rest = c.take(128, 2 * NH)
        m_run, m_new, m_rest = (c.take(128, NH) for _ in range(3))
        m_edges = c.take(128, 2 * NH)
        hotT16 = c.take(128, 2, 128, dt=BF16)
        den, rden = c.take(PL, NH), c.take(PL, NH)
        apart = c.take(128, 2, 128)
        sd4 = c.take(128, 2, NH)
        hot = sb("hot", [128, 2, 128])
        hot16 = sb("hot16", [128, 2, 128], BF16)
        col1 = sb("col1", [128, 128])
        assert c.at <= wa_at
        c_edges = c.at
        c = Carver(arena, wa_at + NTY * 2 * D)
        wih = c.take(128, 2, 3 * D)
        whh = c.take(128, 2, 3 * D)
        relw = c.take(NE16 + 1, 3 * D)
        c = Carver(arena, c_edges)
        bhn = c.take(NE16 + 1, D)
        relt = c.take(128, 2, NE16 + 1)
        bias = c.take(2, 3 * D)
        pick, pick_h = c.take(2, NE16 + 1), c.take(2, NE16 + 1)
        assert c.at <= wa_at
        c = Carver(arena, gru_at)
        gT = c.take(128, 4, PL)
        cntT = c.take(NE16 + 1, PL)
        accrow = c.take(PL, AW + 1)
        rz, gn, gt = c.take(PL, 2 * D), c.take(PL, D), c.take(PL, D)
        assert c.at <= c_edges
        lrec = sb("lrec", [128, 2])
        lsd = sb("lsd", [128, 4])
        leq = sb("leq", [128, 128])
        ldiag = sb("ldiag", [128, 128])
        ones128 = sb("ones128", [128, 128])
        rc = Carver(ring[:].rearrange("p a b -> p (a b)"))
        lS, lVC, lcov = rc.take(128, D), rc.take(128, 2, D), rc.take(128, 2, D)

        elist = dram("elist", [LROWS, 2])
        tab_h0 = dram("tab_h0", [N, D])
        tab_h2 = dram("tab_h2", [N, D])
        tab_k = dram("tab_k", [N * NR, D])
        tab_v = dram("tab_v", [N * NR, D])

        edges_in, x_in_s, small_in, attn_in, gru_in = (sem(n) for n in ("edges_in", "x_in_s", "small_in", "attn_in", "gru_in"))
        dve_step = sem("dve_step")
        cols_made, consts = sem("cols_made"), sem("consts")
        key_ready, key_counted = sem("key_ready"), sem("key_counted")
        tot_ready, tot_summed = sem("tot_ready"), sem("tot_summed")
        hot_ready, hot_placed = sem("hot_ready"), sem("hot_placed")
        lane_marked, hot_ready_b, hot_placed_b, placed_b = (sem(n) for n in ("lane_marked", "hot_ready_b", "hot_placed_b", "placed_b"))
        sorted_by = sem("sorted_by")
        fill_done, list_filled, dest_ready, slot_ready = (sem(n) for n in ("fill_done", "list_filled", "dest_ready", "slot_ready"))
        scattered = [sem(f"scattered{n}") for n in range(4)]
        var_ready, std_ready, rstd_ready, h_rows = (sem(n) for n in ("var_ready", "std_ready", "rstd_ready", "h_rows"))
        table_out, base_ready = sem("table_out"), sem("base_ready")
        landed = [[sem(f"landed{s}_{n}") for n in range(RING)] for s in range(2)]
        row_ready = [sem(f"row_ready{s}") for s in range(4)]
        row_used = [sem(f"row_used{s}") for s in range(4)]
        pool_pass, pe_pass, dve_pass = sem("pool_pass"), sem("pe_pass"), sem("dve_pass")
        islot_ready = [sem(f"islot_ready{s}") for s in range(4)]
        ring_idle = sem("ring_idle")
        hot_made = [sem(f"hot_made{s}") for s in range(4)]
        bucket_summed = [sem(f"bucket_summed{s}") for s in range(4)]
        bucket_read = [sem(f"bucket_read{s}") for s in range(4)]
        y_ready, y_turned, yT_ready, h1_made, h1_relu, h2_made, h2_relu, o_made, n1_step = (
            sem(n) for n in ("y_ready", "y_turned", "yT_ready", "h1_made", "h1_relu", "h2_made", "h2_relu", "o_made", "n1_step"))
        l_in, l_dve, l_pe, l_act, l_w = (sem(n) for n in ("l_in", "l_dve", "l_pe", "l_act", "l_w"))
        blocks_cleared, hrow_ready, diag_made, typed_turned, typedT_ready, kv_made, q_made, kvT_ready, q_copied = (
            sem(n) for n in ("blocks_cleared", "hrow_ready", "diag_made", "typed_turned", "typedT_ready", "kv_made", "q_made", "kvT_ready", "q_copied"))
        bank_full, bank_read_a, bank_read_v, tabs_out, stage_free = (
            sem(n) for n in ("bank_full", "bank_read_a", "bank_read_v", "tabs_out", "stage_free"))
        hot_turned = [None] + [sem(f"hot_turned{s}") for s in (1, 2)]
        apart_made = [None] + [sem(f"apart_made{s}") for s in (1, 2)]
        hotT_made = [None] + [sem(f"hotT_made{s}") for s in (1, 2)]
        tile_done, row_weighted = sem("tile_done"), sem("row_weighted")
        q_edge, s_ready, s_turned, sT_ready, s_split, max_read, m_step, m_bucket, m_cleared = (
            sem(n) for n in ("q_edge", "s_ready", "s_turned", "sT_ready", "s_split", "max_read", "m_step", "m_bucket", "m_cleared"))
        m_edge, m_summed, sd_ready, ex_ready = (sem(n) for n in ("m_edge", "m_summed", "sd_ready", "ex_ready"))
        agg_ready, agg_turned, aggT_ready, att_made, n3_step = (
            sem(n) for n in ("agg_ready", "agg_turned", "aggT_ready", "att_made", "n3_step"))
        relt_cleared, relw_made, relw_ready, g_turned, gT_ready, gates_made = (
            sem(n) for n in ("relt_cleared", "relw_made", "relw_ready", "g_turned", "gT_ready", "gates_made"))
        rz_ready, gt_ready, gn_ready, n5_step = (
            sem(n) for n in ("rz_ready", "gt_ready", "gn_ready", "n5_step"))
        gate_ready = sem("gate_ready")
        f_row, f_turned, fT_ready, f_made, out_ready = (sem(n) for n in ("f_row", "f_turned", "fT_ready", "f_made", "out_ready"))
        out_done = sem("out_done")

        block = ctx.enter_context(nc.Block())

        def flat(ap):
            return ap.rearrange("p a b -> p (a b)")

        def bounds(eng, pairs, b, least=0):
            lo = eng.value_load(pairs[0:1, bass.ds(b, 1)], min_val=least, max_val=NP - 2)
            hi = eng.value_load(pairs[0:1, bass.ds(b + 1, 1)], min_val=least + 2, max_val=NP)
            return lo, hi

        def spare_rows(eng, s, pairs, rings):
            first = eng.value_load(pairs[0:1, NB:NB + 1], min_val=1, max_val=NP)
            rounds = eng.value_load(rings[0:1, 0:1], min_val=1, max_val=NT // ROUND)
            with eng.Fori(first * 2, rounds * ROUND) as t:
                eng.wait_ge(row_used[s], t + RING)
                eng.wait_ge(row_ready[s], t + 3)
                eng.sem_inc(row_used[s], 1)

        def pairs_in_all(eng, pairs):
            return eng.value_load(pairs[0:1, NB:NB + 1], min_val=2 * NB, max_val=NP)

        @block.sync
        def _(sp):
            for t, a in ((src_i, src_in), (dst_i, dst_in), (r16_i, r16_in), (r8_i, r8_in), (ew, ew_in)):
                sp.dma_start(t, a.rearrange("(p j) -> p j", p=PL)).then_inc(edges_in, 16)
            sp.dma_start(x[:], x_in.rearrange("(p b) d -> p b d", p=PL)).then_inc(x_in_s, 16)
            sp.dma_start(nty[:], nty_in.rearrange("(p b) -> p b", p=PL)).then_inc(small_in, 16)
            sp.dma_start(w_sb[:], w_in.rearrange("(a b) -> a b", a=1).broadcast_to([PL, 1])).then_inc(small_in, 16)
            sp.dma_start(w1t[:], w1t_in.rearrange("(c p) n -> p c n", p=128)).then_inc(small_in, 16)
            sp.dma_start(w2t[:], w2t_in).then_inc(small_in, 16)
            sp.dma_start(w3t[:], w3t_in).then_inc(small_in, 16)
            sp.dma_start(pri[:], pri_in.rearrange("(a r) h -> a (r h)", a=1).broadcast_to([128, NR * NH]).rearrange("p (r h) -> p r h", r=NR)).then_inc(small_in, 16)
            sp.dma_start(skip[:], skip_in.rearrange("(a t) -> a t", a=1).broadcast_to([PL, NTY])).then_inc(small_in, 16)
            sp.wait_ge(fill_done, 1)
            sp.dma_start(elist.rearrange("(p c) k -> p (c k)", p=PL), fill).then_inc(list_filled, 16)

            def write_table(tab):
                sp.dma_start(tab.rearrange("(p b) d -> p b d", p=PL), h[:]).then_inc(table_out, 16)

            def relay(s, rings):
                count = sp.value_load(rings[0:1, 0:1], min_val=1, max_val=NT // ROUND)
                past = count * max(s - 1, 0) if s > 1 else 0
                with sp.Fori(past, past + count) as i:
                    for n in range(ROUND):
                        sp.wait_ge(landed[min(s, 1)][n % RING], i * 32 + 16 * (n // RING + 1))
                        sp.sem_inc(row_ready[s], 1)
                sp.sem_inc(ring_idle, 1)

            sp.wait_ge(h_rows, NB)
            write_table(tab_h0)
            sp.wait_ge(sorted_by, 1)
            relay(0, roundsA)
            sp.wait_ge(sorted_by, 2)
            for n in range(4):
                sp.wait_ge(scattered[n], 16 * EJ // 4)
            for t, a in ((wk, wk_in), (wq, wq_in), (wv, wv_in), (wa, wa_in)):
                for k in range(NTY):
                    sp.dma_start(t[:, k], a[k].rearrange("(c p) n -> p c n", p=128)).then_inc(attn_in, 16)
            sp.wait_ge(blocks_cleared, 1)
            for t, a in ((bdk, att_in), (bdm, msg_in)):
                for two in range(2):
                    for cc in range(2):
                        sp.dma_start(t[64 * two:64 * two + 64, cc, :, 64 * two:64 * two + 64],
                                     a[:, 2 * cc + two]).then_inc(attn_in, 16)
            n_l = sp.value_load(n_list[0:1, 0:1], min_val=1, max_val=LROWS // ET)
            with sp.Fori(0, n_l) as t:
                sp.wait_ge(l_w, t + 1)
                sp.dma_start(lrec[:].rearrange("p (a k) -> p a k", a=1),
                             elist.rearrange("(t p) k -> p t k", p=ET)[:, bass.ds(t, 1), :]).then_inc(l_in, 16)
            sp.sem_inc(stage_free, 1)
            with sp.Fori(0, NB) as b:
                sp.wait_ge(bank_read_a, b * 4 + 6)
                sp.wait_ge(bank_read_v, b * 4 + 6)
                for tab, stg in ((tab_k, stage_k), (tab_v, stage_v)):
                    sp.dma_start(tab.rearrange("(p b r) d -> p b (r d)", p=PL, r=NR)[:, bass.ds(b, 1), :],
                                 stg.rearrange("p (a r) n -> p a (r n)", a=1)).then_inc(tabs_out, 16)
                sp.wait_ge(tabs_out, b * 32 + 32)
                sp.sem_inc(stage_free, 1)
            sp.wait_ge(tabs_out, 32 * NB)
            sp.dma_start(wih, wih_in.rearrange("(c p) n -> p c n", p=128)).then_inc(gru_in, 16)
            sp.dma_start(whh, whh_in.rearrange("(c p) n -> p c n", p=128)).then_inc(gru_in, 16)
            sp.wait_ge(relt_cleared, 1)
            sp.dma_start(relt[:, :, 0:NE16], relt_in.rearrange("(c p) n -> p c n", p=128)).then_inc(gru_in, 16)
            sp.dma_start(bias, bias_in).then_inc(gru_in, 16)
            relay(1, roundsB)
            relay(2, roundsB)
            sp.wait_ge(h_rows, 3 * NB)
            write_table(tab_h2)
            relay(3, roundsB)
            with sp.Fori(0, NB) as b:
                sp.wait_ge(out_ready, b + 2)
                sp.dma_start(out.rearrange("(p b) d -> p b d", p=PL)[:, bass.ds(b, 1), :], x[:, bass.ds(b, 1), :]).then_inc(out_done, 16)
            sp.wait_ge(out_done, 16 * NB)
            sp.wait_ge(tabs_out, 32 * NB)
            sp.wait_ge(table_out, 32)
            sp.wait_ge(list_filled, 16)

        @block.gpsimd
        def _(pool):
            nc.gpsimd.iota(lane[:], [[0, 1]], base=0, channel_multiplier=1, allow_small_or_imprecise_dtypes=True)
            nc.gpsimd.iota(col[:], [[1, NT]], base=0, channel_multiplier=0,
                           allow_small_or_imprecise_dtypes=True).then_inc(cols_made, 1)
            nc.gpsimd.memset(fill, -1.0).then_inc(fill_done, 1)
            for s in range(4):
                pool.sem_inc(row_used[s], RING)

            pool.wait_ge(list_filled, 16)
            with pool.Fori(0, EJ // 4) as i:
                for n in range(4):
                    pool.wait_ge(slot_ready, i * 4 + (n + 1))
                    pool.sem_inc(pool_pass, 1)
                    pool.indirect_dma_start(
                        out=elist, out_offset=bass.IndirectOffsetOnAxis(ap=dslot[:, n, :], axis=0),
                        in_=rslot[:, n, :], in_offset=None, bounds_check=LROWS - 1, oob_is_err=False,
                    ).then_inc(scattered[n], 16)

            def gather(s, table, idx, rings):
                count = pool.value_load(rings[0:1, 0:1], min_val=1, max_val=NT // ROUND)
                with pool.Fori(0, count) as i:
                    for g in range(2):
                        pool.wait_ge(row_used[s], i * ROUND + (RING * g + 1))
                        pool.sem_inc(pool_pass, 1)
                        nc.gpsimd.tensor_copy(islot[:, g, :], idx[:, bass.ds(i * ROUND + RING * g, RING)]).then_inc(islot_ready[s], 1)
                        pool.wait_ge(islot_ready[s], i * 2 + (g + 1))
                        for n in range(RING):
                            pool.wait_ge(row_used[s], i * ROUND + (RING * g + n + 1))
                            pool.sem_inc(pool_pass, 1)
                            pool.indirect_dma_start(
                                out=rows[:, n, :], out_offset=None, in_=table,
                                in_offset=bass.IndirectOffsetOnAxis(ap=islot[:, g, n:n + 1], axis=0),
                            ).then_inc(landed[min(s, 1)][n], 16)
                pool.wait_ge(row_used[s], count * ROUND + RING)
                pool.sem_inc(pool_pass, 1)

            pool.wait_ge(sorted_by, 1)
            pool.wait_ge(table_out, 16)
            gather(0, tab_h0, idxA, roundsA)
            pool.wait_ge(ring_idle, 1)
            pool.wait_ge(tabs_out, 32 * NB)
            gather(1, tab_k, idxR, roundsB)
            pool.wait_ge(ring_idle, 2)
            gather(2, tab_v, idxR, roundsB)
            pool.wait_ge(ring_idle, 3)
            pool.wait_ge(table_out, 32)
            gather(3, tab_h2, idxS, roundsB)

        @block.vector
        def _(dve):
            st = Steps(dve, dve_step)
            V = nc.vector

            def rounded(out, x, shift, scale):
                st.then(V.tensor_scalar(out, x, shift, scale, ALU.add, ALU.mult))
                st.then(V.tensor_scalar(out, out, MAGIC, -MAGIC, ALU.add, ALU.add))

            def axpy(out, x, a, y):
                st.then(V.scalar_tensor_tensor(out, x, a, y, ALU.mult, ALU.add))

            def norm(k):
                st.settle()
                st.then(V.tensor_tensor(mean[:], st6[:, :, 1], st6[:, :, 4], ALU.add))
                V.tensor_scalar(mean[:], mean[:], 0.5, None, ALU.mult)
                V.tensor_tensor(half[:], st6[:, :, 1], st6[:, :, 4], ALU.subtract)
                st.then(V.tensor_tensor(var[:], st6[:, :, 2], st6[:, :, 5], ALU.add))
                st.then(V.tensor_tensor(half[:], half[:], half[:], ALU.mult))
                st.then(V.tensor_scalar(half[:], half[:], 0.25, None, ALU.mult))
                V.scalar_tensor_tensor(var[:], var[:], 1.0 / D, half[:], ALU.mult, ALU.add).then_inc(var_ready, 1)
                dve.wait_ge(std_ready, k)
                st.then(V.reciprocal(rstd[:], std[:]))
                V.scalar_tensor_tensor(shift[:], mean[:], -1.0, rstd[:], ALU.mult, ALU.mult).then_inc(rstd_ready, 1)

            dve.wait_ge(cols_made, 1)
            V.tensor_copy(col16[:], col[:])
            V.memset(ones[:], 1.0)
            V.memset(ones16[:], 1.0)
            V.memset(ones128[:], 1.0)
            V.memset(zeros16[:], 0.0)
            V.memset(eps[:], EPS)
            V.memset(wout[:], 0.0)
            V.tensor_scalar(col1[:], col[:, 0:128], 1.0, None, ALU.add)
            V.tensor_scalar(ident[:], col[:, 0:128], lane[:, 0:1], None, ALU.is_equal)
            V.tensor_scalar(identb[:], col[:, 0:128], lane[:, 0:1], None, ALU.is_equal)
            V.tensor_scalar(after[:], col[:, 0:128], lane[:, 0:1], None, ALU.is_gt)
            V.tensor_scalar(after16[:], col[:, 0:128], lane[:, 0:1], -1.0, ALU.is_gt, ALU.add).then_inc(consts, 1)
            dve.wait_ge(consts, 1)
            dve.wait_ge(edges_in, 80)
            V.tensor_copy(src, src_i)
            V.tensor_copy(dst, dst_i)
            V.tensor_copy(r16, r16_i)
            V.tensor_copy(rec[:, :, 1], ew)
            st.then(V.tensor_copy(r8, r8_i))
            st.then(V.tensor_scalar(tmp, dst, float(D), None, ALU.is_lt))
            st.then(V.scalar_tensor_tensor(tmp, src, float(D), tmp, ALU.is_lt, ALU.mult))
            axpy(rec[:, :, 0], src, float(D), dst)
            V.tensor_tensor_scan(incl, ones[:], tmp, 0.0, ALU.mult, ALU.add).then_inc(tot_ready, 1)
            dve.wait_ge(tot_ready, 1)
            dve.wait_ge(tot_summed, 1)
            V.tensor_scalar(rowoff[:, 0:1], ps[0:PL, 0, 0:1], -1.0 - FAR, None, ALU.add)
            rounded(rowoff[:, 1:2], ps[0:PL, 0, 1:2], (ET - 1) / 2.0, 1.0 / ET)
            V.scalar_tensor_tensor(incl, incl, rowoff[:, 0:1], tmp, ALU.add, ALU.mult)
            st.then(V.tensor_scalar(n_list[:], rowoff[:, 1:2], 1.0, None, ALU.max))
            V.tensor_scalar(dest, incl, FAR, None, ALU.add).then_inc(dest_ready, 1)

            rounded(s_lane, src, -float(NB // 2), 1.0 / NB)
            axpy(s_tile, s_lane, -float(NB), src)
            rounded(d_lane, dst, -float(NB // 2), 1.0 / NB)
            axpy(d_tile, d_lane, -float(NB), dst)
            rounded(fa[:, 1, :], dst, -3.5, 1.0 / 8)
            axpy(tmp, fa[:, 1, :], -8.0, dst)
            st.then(V.tensor_scalar(tmp, tmp, 256.0, 1.0, ALU.mult, ALU.add))
            st.then(V.tensor_tensor(fa[:, 0, :], tmp, s_lane, ALU.add))
            axpy(tmp, r16, 128.0, d_lane)
            st.then(V.tensor_scalar(fb[:, 0, 0:EJ], tmp, 1.0, None, ALU.add))
            axpy(tmp, src, float(NR), r8)
            rounded(fb[:, 1, 0:EJ], tmp, -7.5, 1.0 / 16)
            axpy(fb[:, 2, 0:EJ], fb[:, 1, 0:EJ], -16.0, tmp)

            dve.wait_ge(x_in_s, 16)
            with dve.Fori(0, NB) as b:
                st.enter(b, 1)
                st.mark(V.bn_stats(st6[:, bass.ds(b, 1), :], x[:, bass.ds(b, 1), :]))
                st.leave(NB)
            norm(1)

            sorts = (Sort(s_tile, keyhot, incl, tmp, pos, base, rnd, pairsA, roundsA, to_tile, to_lane, 0),
                     Sort(d_tile, keyhot_b, incl_b, tmp_b, pos_b, base_b, rnd_b, pairsB, roundsB, tile_b[:, 0:EJ], lane_b[:, 0:EJ], 2))
            V.memset(fb[:, :, EJ:EJP], 0.0)
            V.memset(tile_b[:, EJ:EJP], 0.0)
            V.memset(lane_b[:, EJ:EJP], 0.0)
            for s in sorts:
                V.memset(s.pos, 0.0)
                V.memset(s.pairs[:, 0:1], 0)
                st.mark(V.memset(s.base, 0.0))
            st.settle()
            with dve.Fori(0, NB) as b:
                st.enter(b, 16)
                for s in sorts:
                    V.tensor_scalar(s.hots, s.key, col[0:PL, bass.ds(b, 1)], None, ALU.is_equal).then_inc(key_ready, 1)
                dve.wait_ge(key_counted, b * 2 + 2)
                for s in sorts:
                    st.mark(V.tensor_tensor_scan(s.cum, ones[:], ps[0:PL, s.bank, 0:EJ], 0.0, ALU.mult, ALU.add))
                st.settle()
                for s in sorts:
                    st.mark(V.tensor_tensor(s.work, s.cum, ps[0:PL, s.bank + 1, 0:EJ], ALU.add))
                    st.mark(V.tensor_scalar(s.count, s.cum[:, EJ - 1:EJ], ET - 0.5, 0.5 / ET, ALU.add, ALU.mult))
                st.settle()
                for s in sorts:
                    st.mark(V.scalar_tensor_tensor(s.work, s.work, s.base, s.hots, ALU.add, ALU.mult))
                    st.mark(V.tensor_scalar(s.count, s.count, MAGIC, MAGIC + 2.0, ALU.add, ALU.max))
                st.settle()
                for s in sorts:
                    st.mark(V.tensor_tensor(s.pos, s.pos, s.work, ALU.add))
                    st.mark(V.tensor_scalar(s.count, s.count, -MAGIC, 2.0 * ET, ALU.add, ALU.mult))
                st.settle()
                for s in sorts:
                    V.tensor_tensor(s.base, s.base, s.count, ALU.add).then_inc(base_ready, 1)
                dve.wait_ge(base_ready, b * 2 + 2)
                for s in sorts:
                    st.mark(V.tensor_scalar(s.pairs[:, bass.ds(b + 1, 1)], s.base, 0.5 / ET, None, ALU.mult))
                st.settle()
                st.leave(NB)
            for s in sorts:
                rounded(s.count, s.base, (ROUND // 2 + 1.0) * ET, 1.0 / (ROUND * ET))
                V.tensor_copy(s.rings[:], s.count)
                rounded(s.tile, s.pos, -(ET - 1) / 2.0, 1.0 / ET)
                axpy(s.lane, s.tile, -float(ET), s.pos)

            def hots(n, j):
                V.tensor_scalar(tilehot[:, n, :], col16[0:PL, :], to_tile[:, j], None, ALU.is_equal)
                for f in range(2):
                    last = V.tensor_scalar(lanehot[:, n, f, :], col16[0:PL, 0:ET], to_lane[:, j], fa[:, f, j],
                                           ALU.is_equal, ALU.mult)
                last.then_inc(hot_ready, 1)

            for n in range(4):
                hots(n, slice(n, n + 1))
            with dve.Fori(1, EJ // 4) as i:
                for n in range(4):
                    dve.wait_ge(hot_placed, i * 4 + (n - 3))
                    hots(n, bass.ds(i * 4 + n, 1))
            dve.wait_ge(hot_placed, EJ)
            rounded(dec, ps[:, 2, 0:NT], -64.0, 1.0 / 256)
            axpy(locA[:], dec, -256.0, ps[:, 2, 0:NT])
            axpy(dec, ps[:, 3, 0:NT], 8.0, dec)
            V.tensor_copy(idxA[:], dec).then_inc(sorted_by, 1)
            st.settle()
            dve.wait_ge(sorted_by, 1)

            def edge_hots(s, loc, n, t):
                dve.wait_ge(row_used[s], t + (RING - 1))
                V.tensor_scalar(hot[:, n, :], col1[:], loc[:, bass.ds(t, 1)], None, ALU.is_equal).then_inc(hot_made[s], 1)

            def mark_b(P):
                for n in range(2):
                    j = P * 2 + n
                    slot = bass.ds(P % 2 * 2 + n, 1)
                    dve.wait_ge(hot_placed_b, j + 1)
                    V.tensor_scalar(flat(tilehot[:, slot, :]), col16[0:PL, :], tile_b[:, bass.ds(j, 1)], None, ALU.is_equal)
                    V.tensor_scalar(flat(onehot[:, slot, :]), col16[0:PL, 0:ET], lane_b[:, bass.ds(j, 1)], None,
                                    ALU.is_equal).then_inc(lane_marked, 1)

            def source_marks(b):
                lo, hi = bounds(dve, pairsA, b)
                with dve.Fori(lo, hi) as P:
                    mark_b(P)
                    for n in range(2):
                        edge_hots(0, locA, n, P * 2 + n)

            def first_in(b):
                dve.wait_ge(bucket_read[0], b + 2)
                dve.sem_inc(dve_pass, 1)
                V.scalar_tensor_tensor(row_b[:], flat(h[:, bass.ds(b, 1), :]), w_sb[:, 0:1], flat(acc[:, bass.ds(b, 1), 0:D]),
                                       ALU.mult, ALU.add).then_inc(y_ready, 1)

            def first_out(b):
                bb = bass.ds(b, 1)
                dve.wait_ge(o_made, b + 1)
                V.scalar_tensor_tensor(row_b[:], ps[0:PL, 6, 0:D], 0.0, flat(h[:, bb, :]), ALU.max, ALU.add).then_inc(n1_step, 1)
                dve.wait_ge(n1_step, b * 3 + 1)
                V.tensor_tensor(flat(x[:, bb, :]), flat(x[:, bb, :]), row_b[:], ALU.add).then_inc(n1_step, 1)
                dve.wait_ge(n1_step, b * 3 + 2)
                V.bn_stats(flat(st6[:, bb, :]), flat(x[:, bb, :])).then_inc(n1_step, 1)
                dve.wait_ge(n1_step, b * 3 + 3)

            dve.wait_ge(small_in, 16 * 7)
            source_marks(0)
            first_in(0)
            with dve.Fori(1, NB) as b:
                source_marks(b)
                first_out(b - 1)
                first_in(b)
            first_out(NB - 1)
            all_a = pairs_in_all(dve, pairsA)
            with dve.Fori(all_a, EJ // 2 + 1) as P:
                mark_b(P)
            norm(2)
            dve.wait_ge(placed_b, 1)
            rounded(relB[:], ps[:, 2, 0:NT], -62.5, 1.0 / 128)
            axpy(locB[:], relB[:], -128.0, ps[:, 2, 0:NT])
            st.then(V.tensor_copy(dec2, ps[:, 4, 0:NT]))
            axpy(dec2, ps[:, 3, 0:NT], 16.0, dec2)
            V.tensor_copy(idxR[:], dec2)
            rounded(dec, dec2, -3.5, 1.0 / NR)
            V.tensor_copy(idxS[:], dec).then_inc(sorted_by, 1)
            st.settle()
            dve.wait_ge(sorted_by, 2)

            V.memset(bdk, 0.0)
            V.memset(bdm, 0.0).then_inc(blocks_cleared, 1)

            n_l = dve.value_load(n_list[0:1, 0:1], min_val=1, max_val=LROWS // ET)
            dve.wait_ge(ring_idle, 1)
            dve.sem_inc(l_w, 1)
            with dve.Fori(0, n_l) as t:
                def seq(k, ins):
                    ins.then_inc(l_dve, 1)
                    dve.wait_ge(l_dve, t * 8 + k)
                dve.wait_ge(l_in, t * 16 + 16)
                seq(1, V.tensor_scalar(ldiag[:], ident[:], lrec[:, 0:1], None, ALU.mult))
                seq(2, V.tensor_scalar(lsd[:, 0:1], lrec[:, 0:1], -(D - 1) / 2.0, 1.0 / D, ALU.add, ALU.mult))
                seq(3, V.tensor_scalar(lsd[:, 0:1], lsd[:, 0:1], MAGIC, -MAGIC, ALU.add, ALU.add))
                seq(4, V.scalar_tensor_tensor(lsd[:, 1:2], lsd[:, 0:1], -float(D), lrec[:, 0:1], ALU.mult, ALU.add))
                dve.wait_ge(l_pe, t * 2 + 1)
                seq(5, V.scalar_tensor_tensor(leq[:], ps[:, 0, 0:128], lrec[:, 0:1], after[:], ALU.is_equal, ALU.mult))
                seq(6, V.tensor_reduce(lsd[:, 2:3], leq[:], AX_X, ALU.max))
                seq(7, V.tensor_scalar(lsd[:, 3:4], lsd[:, 2:3], -1.0, 1.0, ALU.mult, ALU.add))
                V.tensor_scalar(lS, col[:, 0:D], lsd[:, 0:1], lsd[:, 3:4], ALU.is_equal, ALU.mult)
                V.tensor_scalar(lVC[:, 0, :], col[:, 0:D], lsd[:, 1:2], lrec[:, 1:2], ALU.is_equal, ALU.mult)
                seq(8, V.tensor_scalar(lVC[:, 1, :], col[:, 0:D], lsd[:, 1:2], None, ALU.is_equal))
                dve.wait_ge(l_act, t + 1)
                dve.sem_inc(dve_pass, 1)
                V.copy_predicated(wout[:, 0, :], lcov[:, 0, :].bitcast(I32), ps[:, 1, 0:D])
                V.copy_predicated(wout[:, 1, :], lcov[:, 1, :].bitcast(I32), ps[:, 2, 0:D]).then_inc(l_w, 1)
                dve.wait_ge(l_w, t + 2)

            dve.wait_ge(attn_in, 16 * (4 * NTY + 8))
            st.then(V.tensor_copy(half[:], nty[:]))
            st.then(V.tensor_scalar(pri[:], pri[:], DK ** -0.5, None, ALU.mult))
            dve.wait_ge(gate_ready, 1)
            for k in range(NTY):
                st.then(V.tensor_scalar(tmask[:, k, :], half[:], float(k), None, ALU.is_equal))
                V.tensor_scalar(gmask[:, k, :], tmask[:, k, :], skip[:, k:k + 1], None, ALU.mult)
            for cc in range(2):
                for two in range(2):
                    blk = bdk[:, cc, :, 64 * two:64 * two + 64]
                    st.mark(V.tensor_tensor(blk, blk, pri[:, :, 2 * cc + two:2 * cc + two + 1].broadcast_to([128, NR, 64]), ALU.mult))
            st.settle()

            def type_masks(b):
                dve.wait_ge(typed_turned, b + 1)
                for k in range(NTY):
                    last = V.tensor_scalar(diag[:, k, :], ident[0:PL, 0:PL], tmask[:, k, bass.ds(b, 1)], None, ALU.mult)
                last.then_inc(diag_made, 1)

            def tables(b):
                dve.wait_ge(q_made, b + 1)
                V.tensor_copy(flat(q[:, bass.ds(b, 1), :]), ps[0:PL, 0, 0:D]).then_inc(q_copied, 1)
                dve.wait_ge(stage_free, b + 1)
                for g in range(4):
                    dve.wait_ge(bank_full, b * 8 + (2 * g + 3))
                    V.tensor_copy((stage_k, stage_v)[g // 2][:, 4:8, 128 * (g % 2):128 * (g % 2) + 128],
                                  ps[0:PL, 4 + (2 * g + 1) % 4, :].rearrange("p (r n) -> p r n", r=4)).then_inc(bank_read_v, 1)

            type_masks(0)
            with dve.Fori(0, NB - 1) as b:
                type_masks(b + 1)
                tables(b)
            tables(NB - 1)

            dve.wait_ge(tabs_out, 32 * NB)
            V.memset(relt, 0.0).then_inc(relt_cleared, 1)
            st.then(V.memset(pick, 0.0))
            st.then(V.memset(pick[:, NE16:NE16 + 1], 1.0))
            V.tensor_scalar(pick_h, pick, lane[0:2, 0:1], None, ALU.mult)

            total = pairs_in_all(dve, pairsB)
            K3, K = 6 * NH, 2 * NH
            st.then(V.tensor_tensor(sel1, ident[0:K3, 0:K], ident[0:K3, K:2 * K], ALU.add))
            st.then(V.tensor_tensor(sel1, sel1, ident[0:K3, 2 * K:3 * K], ALU.add))
            st.then(V.tensor_copy(sel, sel1.rearrange("p (k a) -> p k a", a=1).broadcast_to([K3, K, PL])))

            def scores(P):
                dve.wait_ge(q_edge, P * 2 + 4)
                dve.wait_ge(row_ready[1], P * 2 + 4)
                V.tensor_tensor(prod, ps[:, 2:4, 0:D], rows[:, bass.ds(P % (RING // 2) * 2, 2), :], ALU.mult).then_inc(row_used[1], 2)
                dve.wait_ge(row_used[1], P * 2 + (RING + 2))
                V.tensor_reduce(flat(score[:, bass.ds(P * 2, 2), :]), prod.rearrange("p n (h d) -> p (n h) d", h=NH), AX_X, ALU.add).then_inc(s_ready, 1)

            def parts(P, last):
                flat4 = flat(score[:, bass.ds(P * 2, 2), :])

                def seq(k, ins):
                    ins.then_inc(s_split, 1)
                    dve.wait_ge(s_split, P * 4 + k)
                if last is not None:
                    dve.wait_ge(tile_done, last + 1)
                    dve.wait_ge(m_step, last + 1)
                    V.tensor_reduce(m_new[0:PL, :], ps[0:PL, bass.ds(last % 2 * 2 + 4, 2), :].rearrange("p n (h e) -> p h n e", h=NH),
                                    AX_XY, ALU.max).then_inc(max_read, 1)
                dve.wait_ge(s_ready, P + 1)
                dve.wait_ge(s_turned, P + 1)
                dve.sem_inc(dve_pass, 1)
                V.tensor_copy(s_parts[:, 0, :], flat4).then_inc(s_split, 1)
                if last is not None:
                    dve.wait_ge(max_read, last + 3)
                    V.tensor_tensor(m_run[0:PL, :], m_run[0:PL, :], m_new[0:PL, :], ALU.max).then_inc(m_step, 1)
                dve.wait_ge(s_split, P * 4 + 1)
                seq(2, V.tensor_tensor(s_rest, flat4, s_parts[:, 0, :], ALU.subtract))
                seq(3, V.tensor_copy(s_parts[:, 1, :], s_rest))
                V.tensor_tensor(s_parts[:, 2, :], s_rest, s_parts[:, 1, :], ALU.subtract).then_inc(s_split, 1)

            def largest(P):
                dve.wait_ge(tile_done, P + 1)
                dve.wait_ge(m_step, P + 1)
                V.tensor_reduce(m_new[0:PL, :], ps[0:PL, bass.ds(P % 2 * 2 + 4, 2), :].rearrange("p n (h e) -> p h n e", h=NH),
                                AX_XY, ALU.max).then_inc(max_read, 1)
                dve.wait_ge(max_read, P + 3)
                V.tensor_tensor(m_run[0:PL, :], m_run[0:PL, :], m_new[0:PL, :], ALU.max).then_inc(m_step, 1)

            def node_tile_done(b, P):
                dve.wait_ge(m_step, P + 2)
                part = [flat(m_all[:, bass.ds(b, 1), k * NH:(k + 1) * NH]) for k in range(3)]

                def seq(k, ins):
                    ins.then_inc(m_bucket, 1)
                    dve.wait_ge(m_bucket, b * 4 + k)
                seq(1, V.tensor_copy(part[0], m_run[0:PL, :]))
                seq(2, V.tensor_tensor(m_rest[0:PL, :], m_run[0:PL, :], part[0], ALU.subtract))
                seq(3, V.tensor_copy(part[1], m_rest[0:PL, :]))
                seq(4, V.tensor_tensor(part[2], m_rest[0:PL, :], part[1], ALU.subtract))
                V.memset(m_run, LOW).then_inc(m_cleared, 1)
                dve.wait_ge(m_cleared, b + 2)
                dve.sem_inc(dve_pass, 1)

            V.memset(m_run, LOW).then_inc(m_cleared, 1)
            dve.wait_ge(m_cleared, 1)
            scores(0)
            parts(0, None)
            lo, hi = bounds(dve, pairsB, 0)
            with dve.Fori(1, hi) as P:
                scores(P)
                parts(P, P - 1)
            with dve.Fori(1, NB) as b:
                lo, hi = bounds(dve, pairsB, b, 2)
                scores(lo)
                parts(lo, lo - 1)
                node_tile_done(b - 1, lo - 1)
                with dve.Fori(lo + 1, hi) as P:
                    scores(P)
                    parts(P, P - 1)
            largest(total - 1)
            node_tile_done(NB - 1, total - 1)
            spare_rows(dve, 1, pairsB, roundsB)

            def exps(P):
                dve.wait_ge(ex_ready, P + 1)
                dve.wait_ge(m_edge, P + 2)
                V.tensor_reduce(m_edges, ps[:, 2, 0:6 * NH].rearrange("p (n a h) -> p n h a", n=2, a=3), AX_X, ALU.add).then_inc(m_summed, 1)
                dve.wait_ge(m_summed, P + 1)
                V.tensor_tensor(sd4, score[:, bass.ds(P * 2, 2), :], m_edges.rearrange("p (n h) -> p n h", n=2),
                                ALU.subtract).then_inc(sd_ready, 1)

            def weighted(P):
                for n in range(2):
                    t = P * 2 + n
                    dve.wait_ge(row_used[2], t + (RING - 1))
                    V.tensor_scalar(hot[:, n, :], col1[:], locB[:, bass.ds(t, 1)], None, ALU.is_equal)
                    if n == 0:
                        dve.wait_ge(ex_ready, P + 2)
                    dve.wait_ge(row_ready[2], t + 3)
                    slot = bass.ds(P % (RING // 2) * 2 + n, 1)
                    row = flat(ring[:, slot, 0:D]).rearrange("p (h d) -> p h d", h=NH)
                    V.tensor_tensor(row, row, ring[:, slot, D:D + NH].rearrange("p a h -> p h a").broadcast_to([128, NH, DK]),
                                    ALU.mult).then_inc(row_weighted, 1)

            def sums_out(b):
                dve.wait_ge(bucket_summed[2], b + 1)
                V.tensor_copy(flat(acc[:, bass.ds(b, 1), 0:D + NH]), ps[0:PL, 7, 0:D + NH]).then_inc(bucket_read[2], 1)

            def over_sums(b):
                dve.wait_ge(bucket_read[2], b + 2)
                V.tensor_scalar(den, flat(acc[:, bass.ds(b, 1), D:D + NH]), 1e-30, None, ALU.max).then_inc(n3_step, 1)
                dve.wait_ge(n3_step, b * 5 + 1)
                V.reciprocal(rden, den).then_inc(n3_step, 1)
                dve.wait_ge(n3_step, b * 5 + 2)
                dve.wait_ge(agg_turned, b + 1)
                V.tensor_tensor(row_b[:].rearrange("p (h d) -> p h d", h=NH), flat(acc[:, bass.ds(b, 1), 0:D]).rearrange("p (h d) -> p h d", h=NH),
                                rden.rearrange("p (h a) -> p h a", a=1).broadcast_to([PL, NH, DK]), ALU.mult).then_inc(n3_step, 1)
                for k in range(NTY):
                    last = V.tensor_scalar(diag[:, k, :], ident[0:PL, 0:PL], gmask[:, k, bass.ds(b, 1)], None, ALU.mult)
                last.then_inc(agg_ready, 1)

            def add_attention(b):
                bb = bass.ds(b, 1)
                dve.wait_ge(att_made, b + 1)
                V.tensor_tensor(flat(x[:, bb, :]), flat(x[:, bb, :]), ps[0:PL, 5, 0:D], ALU.add).then_inc(n3_step, 1)
                dve.wait_ge(n3_step, b * 5 + 4)
                V.bn_stats(flat(st6[:, bb, :]), flat(x[:, bb, :])).then_inc(n3_step, 1)
                dve.wait_ge(n3_step, b * 5 + 5)

            exps(0)
            lo, hi = bounds(dve, pairsB, 0)
            with dve.Fori(1, hi) as P:
                weighted(P - 1)
                exps(P)

            def node_tile(b, first=False):
                lo, hi = bounds(dve, pairsB, b, 2)
                weighted(lo - 1)
                exps(lo)
                sums_out(b - 1)
                if not first:
                    add_attention(b - 2)
                over_sums(b - 1)
                with dve.Fori(lo + 1, hi) as P:
                    weighted(P - 1)
                    exps(P)

            node_tile(1, first=True)
            with dve.Fori(2, NB) as b:
                node_tile(b)
            add_attention(NB - 2)
            weighted(total - 1)
            sums_out(NB - 1)
            over_sums(NB - 1)
            add_attention(NB - 1)
            dve.wait_ge(n3_step, NB * 5)
            norm(3)

            st.then(V.memset(accrow[:, AW:AW + 1], 1.0))

            def marks(b):
                lo, hi = bounds(dve, pairsB, b)
                with dve.Fori(lo, hi) as P:
                    for n in range(2):
                        t = P * 2 + n
                        dve.wait_ge(row_used[3], t + (RING - 1))
                        V.tensor_scalar(flat(ring[:, bass.ds(P % (RING // 2) * 2 + n, 1), D:AW]), col[:, 0:NE16],
                                        relB[:, bass.ds(t, 1)], None, ALU.is_equal)
                        edge_hots(3, locB, n, t)

            def combine(b):
                bb = bass.ds(b, 1)

                def seq(k, ins):
                    ins.then_inc(n5_step, 1)
                    dve.wait_ge(n5_step, b * 6 + (k + 6))
                dve.wait_ge(rz_ready, b + 1)
                seq(1, V.tensor_tensor(gt, rz[:, 0:D], ps[0:PL, 5, 0:D], ALU.mult))
                V.tensor_tensor(gt, gt, ps[0:PL, 4, 0:D], ALU.add).then_inc(gt_ready, 1)
                dve.wait_ge(gn_ready, b + 1)
                seq(2, V.tensor_tensor(gt, flat(h[:, bb, :]), gn, ALU.subtract))
                seq(3, V.tensor_tensor(gt, gt, rz[:, D:2 * D], ALU.mult))
                seq(4, V.tensor_tensor(gt, gt, gn, ALU.add))
                seq(5, V.tensor_tensor(flat(x[:, bb, :]), flat(x[:, bb, :]), gt, ALU.add))
                seq(6, V.bn_stats(flat(st6[:, bb, :]), flat(x[:, bb, :])))

            marks(0)
            with dve.Fori(1, NB) as b:
                marks(b)
                combine(b - 1)
            combine(NB - 1)
            norm(4)

            with dve.Fori(0, NB) as b:
                bb = bass.ds(b, 1)
                dve.wait_ge(f_made, b + 1)
                V.tensor_tensor(flat(x[:, bb, :]), flat(x[:, bb, :]), ps[0:PL, 2, 0:D], ALU.add).then_inc(out_ready, 1)

        @block.scalar
        def _(act):
            A = nc.scalar

            def norm(k):
                act.wait_ge(var_ready, k)
                A.activation(std[:], var[:], ACT.Sqrt, bias=eps[:, 0:1]).then_inc(std_ready, 1)
                act.wait_ge(rstd_ready, k)
                if k in (2, 4):
                    act.wait_ge(table_out, 8 * k)
                with act.Fori(0, NB) as b:
                    bb = bass.ds(b, 1)
                    A.activation(flat(h[:, bb, :]), flat(x[:, bb, :]), ACT.Relu, bias=shift[:, bb],
                                 scale=rstd[:, bb]).then_inc(h_rows, 1)
                act.wait_ge(h_rows, k * NB)

            norm(1)
            act.wait_ge(dest_ready, 1)
            for n in range(4):
                A.copy(dslot[:, n, :], dest[:, n:n + 1])
                A.copy(rslot[:, n, :], rec[:, n, :]).then_inc(slot_ready, 1)
            with act.Fori(1, EJ // 4) as i:
                for n in range(4):
                    j = bass.ds(i * 4 + n, 1)
                    act.wait_ge(scattered[n], i * 16)
                    A.copy(dslot[:, n, :], dest[:, j])
                    A.copy(rslot[:, n, :], flat(rec[:, j, :])).then_inc(slot_ready, 1)

            act.wait_ge(list_filled, 16)
            def fields_b(P):
                for n in range(2):
                    j = P * 2 + n
                    act.wait_ge(lane_marked, j + 1)
                    slot = bass.ds(P % 2 * 2 + n, 1)
                    for f in range(3):
                        last = A.activation(lanehot[:, slot, f:f + 1, :].rearrange("p a f e -> p (a f e)"), flat(onehot[:, slot, :]),
                                            ACT.Copy, scale=fb[:, f, bass.ds(j, 1)])
                    last.then_inc(hot_ready_b, 1)

            act.wait_ge(sorted_by, 1)
            with act.Fori(0, NB) as b:
                lo, hi = bounds(act, pairsA, b)
                with act.Fori(lo, hi) as P:
                    fields_b(P)
                act.wait_ge(bucket_summed[0], b + 1)
                A.copy(flat(acc[:, bass.ds(b, 1), 0:D]), ps[0:PL, 7, 0:D]).then_inc(bucket_read[0], 1)
                act.wait_ge(y_turned, b + 1)
                A.copy(flat(rowT[:]), ps[:, 1, 0:2 * PL]).then_inc(yT_ready, 1)
                act.wait_ge(h1_made, b + 1)
                A.activation(h1T[:], ps[0:H1, 0, 0:PL], ACT.Relu).then_inc(h1_relu, 1)
                act.wait_ge(h2_made, b + 1)
                A.activation(h2T[:], ps[0:H2, 5, 0:PL], ACT.Relu).then_inc(h2_relu, 1)
            all_a = pairs_in_all(act, pairsA)
            with act.Fori(all_a, EJ // 2 + 1) as P:
                fields_b(P)
            norm(2)
            n_l = act.value_load(n_list[0:1, 0:1], min_val=1, max_val=LROWS // ET)
            with act.Fori(0, n_l) as t:
                act.wait_ge(l_pe, t * 2 + 2)
                A.copy(lcov[:, 0, :], ps[:, 1, D:2 * D])
                A.copy(lcov[:, 1, :], ps[:, 2, D:2 * D]).then_inc(l_act, 1)
            A.activation(skip[:], skip[:], ACT.Sigmoid).then_inc(gate_ready, 1)
            def node_rows(b):
                act.wait_ge(typed_turned, b + 1)
                A.copy(row_b[:], flat(h[:, bass.ds(b, 1), :])).then_inc(hrow_ready, 1)

            def typed_rows(b):
                act.wait_ge(typed_turned, b + 2)
                A.copy(typedT[:], ps[:, 1:3, 0:NTY * PL]).then_inc(typedT_ready, 1)

            def keys_values(b):
                act.wait_ge(kv_made, b + 1)
                A.copy(flat(kvT[:]), ps[:, 3, 0:4 * PL]).then_inc(kvT_ready, 1)

            def tables(b):
                act.wait_ge(stage_free, b + 1)
                for g in range(4):
                    act.wait_ge(bank_full, b * 8 + (2 * g + 2))
                    A.copy((stage_k, stage_v)[g // 2][:, 0:4, 128 * (g % 2):128 * (g % 2) + 128],
                           ps[0:PL, 4 + (2 * g) % 4, :].rearrange("p (r n) -> p r n", r=4)).then_inc(bank_read_a, 1)

            node_rows(0)
            typed_rows(0)
            with act.Fori(0, NB - 1) as b:
                node_rows(b + 1)
                keys_values(b)
                typed_rows(b + 1)
                tables(b)
            keys_values(NB - 1)
            tables(NB - 1)

            total = pairs_in_all(act, pairsB)

            both = ps[0:PL, 0, 0:128].bitcast(BF16).rearrange("p (n e) -> p n e", n=2)

            def others(P):
                act.wait_ge(hot_turned[1], P + 2)
                A.activation(neg[0:PL, bass.ds(P % 4, 1), :, :].rearrange("p a n e -> p (a n) e"), both, ACT.Copy, scale=-LOW, bias=LOW)

            def turned_1(P):
                act.wait_ge(q_edge, P * 2 + 2)
                A.copy(hotT[0:PL, :, :], both).then_inc(hotT_made[1], 1)

            def score_rows(P):
                act.wait_ge(s_turned, P + 2)
                A.copy(sT, ps[0:6 * NH, 1, 0:64].bitcast(BF16)).then_inc(sT_ready, 1)

            def turn_hots(s, P):
                act.wait_ge(hot_turned[s], P + 1)
                for n in range(2):
                    last = A.activation(apart[:, n, :], col1[:], ACT.Square, scale=-1.0, bias=locB[:, bass.ds(P * 2 + n, 1)])
                last.then_inc(apart_made[s], 1)
                act.wait_ge(apart_made[s], P + 1)
                A.activation(hot16[:], apart, ACT.Relu, scale=-1.0, bias=ones128[:, 0:1]).then_inc(hot_made[s], 1)

            turn_hots(1, 0)
            for k in range(2):
                others(k)
                if k == 0:
                    turn_hots(1, 1)
                turned_1(k)
            turn_hots(1, 2)
            with act.Fori(1, total) as P:
                others(P + 1)
                turn_hots(1, P + 2)
                score_rows(P - 1)
                turned_1(P + 1)
            score_rows(total - 1)

            def turned_2(P):
                act.wait_ge(hot_turned[2], P + 2)
                act.wait_ge(m_edge, P + 1)
                A.copy(hotT16[0:PL, :, :], both).then_inc(hotT_made[2], 1)

            def exps(P):
                act.wait_ge(sd_ready, P + 2)
                act.wait_ge(row_used[2], P * 2 + 2)
                A.activation(ring[:, bass.ds(P % (RING // 2) * 2, 2), D:D + NH], sd4, ACT.Exp).then_inc(ex_ready, 1)

            def typed_sums(b):
                act.wait_ge(agg_turned, b + 2)
                A.copy(typedT[:], ps[:, 3:5, 0:NTY * PL]).then_inc(aggT_ready, 1)

            act.wait_ge(hot_made[1], total + 2)
            turn_hots(2, 0)
            turned_2(0)
            turn_hots(2, 1)
            turn_hots(2, 2)
            turned_2(1)
            exps(0)
            lo, hi = bounds(act, pairsB, 0)
            with act.Fori(1, hi) as P:
                turn_hots(2, P + 2)
                turned_2(P + 1)
                exps(P)
            with act.Fori(1, NB) as b:
                lo, hi = bounds(act, pairsB, b, 2)
                with act.Fori(lo, hi) as P:
                    turn_hots(2, P + 2)
                    turned_2(P + 1)
                    exps(P)
                typed_sums(b - 1)
            typed_sums(NB - 1)
            norm(3)
            act.wait_ge(relw_made, 1)
            A.copy(relw[:, 0:2 * D], ps[0:NE16 + 1, 1, :])
            A.copy(relw[:, 2 * D:3 * D], ps[0:NE16 + 1, 2, 0:D])
            A.copy(bhn, ps[0:NE16 + 1, 2, D:2 * D]).then_inc(relw_ready, 1)
            def turned_rows(b):
                bb = bass.ds(b, 1)
                act.wait_ge(g_turned, b + 1)
                A.copy(row_b[:], flat(h[:, bb, :]))
                act.wait_ge(bucket_summed[3], b + 1)
                A.copy(accrow[:, 0:AW], ps[0:PL, 7, 0:AW]).then_inc(bucket_read[3], 1)
                act.wait_ge(g_turned, b + 2)
                A.copy(flat(gT), ps[:, 1, 0:4 * PL])
                A.copy(cntT, ps[0:NE16 + 1, 2, 0:PL]).then_inc(gT_ready, 1)

            def reset_update(b):
                act.wait_ge(gates_made, b + 1)
                act.wait_ge(n5_step, b * 6 + 3)
                A.activation(rz, ps[0:PL, 3, :], ACT.Sigmoid).then_inc(rz_ready, 1)

            def new(b):
                act.wait_ge(gt_ready, b + 2)
                A.activation(gn, gt, ACT.Tanh).then_inc(gn_ready, 1)

            turned_rows(0)
            reset_update(0)
            with act.Fori(1, NB) as b:
                new(b - 1)
                turned_rows(b)
                reset_update(b)
            new(NB - 1)
            norm(4)
            with act.Fori(0, NB) as b:
                act.wait_ge(f_turned, b + 1)
                A.copy(row_b[:], flat(h[:, bass.ds(b, 1), :])).then_inc(f_row, 1)
                act.wait_ge(f_turned, b + 2)
                A.copy(flat(rowT[:]), ps[:, 1, 0:2 * PL]).then_inc(fT_ready, 1)

        @block.tensor
        def _(pe):
            M = nc.tensor.matmul
            for one in (q_edge, row_weighted, *row_ready):
                pe.sem_inc(one, 2)
            pe.sem_inc(n5_step, 6)
            pe.sem_inc(hot_placed_b, 4)
            for one in (hot_turned[1], hot_turned[2], hotT_made[1], hotT_made[2], m_edge, s_turned, m_step, ex_ready, sd_ready):
                pe.sem_inc(one, 1)
            pe.sem_inc(bank_read_a, 2)
            pe.sem_inc(bank_read_v, 2)
            pe.sem_inc(max_read, 2)
            for one in (typed_turned, q_copied, agg_turned, g_turned, f_turned, gt_ready, out_ready, bank_full,
                        bucket_read[0], bucket_read[2], bucket_read[3]):
                pe.sem_inc(one, 1)
            pe.wait_ge(consts, 1)
            pe.wait_ge(tot_ready, 1)
            M(ps[0:PL, 0, 0:1], after[0:PL, 0:PL], incl[:, EJ - 1:EJ], start=True, stop=True)
            M(ps[0:PL, 0, 1:2], ones[0:PL, 0:PL], incl[:, EJ - 1:EJ], start=True, stop=True).then_inc(tot_summed, 1)

            with pe.Fori(0, NB) as b:
                for which, hots in enumerate((keyhot, keyhot_b)):
                    pe.wait_ge(key_ready, b * 2 + (which + 1))
                    M(ps[0:PL, 2 * which, 0:EJ], ones16[0:PL, 0:PL], hots, start=True, stop=True)
                    M(ps[0:PL, 2 * which + 1, 0:EJ], after16[0:PL, 0:PL], hots, start=True, stop=True).then_inc(key_counted, 1)

            def products(n, start, stop):
                for f in range(2):
                    last = M(ps[:, 2 + f, 0:NT], lanehot[:, n, f, :], tilehot[:, n, :], start=start, stop=stop)
                last.then_inc(hot_placed, 1)

            for n in range(4):
                pe.wait_ge(hot_ready, n + 1)
                products(n, n == 0, False)
            with pe.Fori(1, EJ // 4 - 1) as i:
                for n in range(4):
                    pe.wait_ge(hot_ready, i * 4 + (n + 1))
                    products(n, False, False)
            for n in range(4):
                pe.wait_ge(hot_ready, EJ - 3 + n)
                products(n, False, n == 3)

            def place_b(P):
                for n in range(2):
                    slot = bass.ds(P % 2 * 2 + n, 1)
                    pe.wait_ge(hot_ready_b, P * 2 + (n + 1))
                    pe.sem_inc(pe_pass, 1)
                    for f in range(3):
                        last = M(ps[:, 2 + f, 0:NT], lanehot[:, slot, f:f + 1, :].rearrange("p a f e -> p (a f e)"),
                                 flat(tilehot[:, slot, :]), start=False, stop=False)
                    last.then_inc(hot_placed_b, 1)

            def open_sum(width):
                M(ps[0:PL, 7, 0:width], zeros16[0:1, 0:PL], zeros16[0:1, 0:width], start=True, stop=False)

            def close_sum(s, width):
                M(ps[0:PL, 7, 0:width], zeros16[0:1, 0:PL], zeros16[0:1, 0:width], start=False, stop=True).then_inc(bucket_summed[s], 1)

            pe.wait_ge(sorted_by, 1)
            pe.wait_ge(small_in, 16 * 7)
            for f in range(3):
                M(ps[:, 2 + f, 0:NT], zeros16[0:1, 0:128], zeros16[0:1, 0:NT], start=True, stop=False)
            with pe.Fori(0, NB) as b:
                lo, hi = bounds(pe, pairsA, b)
                pe.wait_ge(bucket_read[0], b + 1)
                open_sum(D)
                with pe.Fori(lo, hi) as P:
                    for n in range(2):
                        t = P * 2 + n
                        pe.wait_ge(hot_made[0], t + 1)
                        pe.wait_ge(row_ready[0], t + 3)
                        M(ps[0:PL, 7, 0:D], hot[:, n, 0:PL], flat(rows[:, bass.ds(P % (RING // 2) * 2 + n, 1), :]),
                          start=False, stop=False).then_inc(row_used[0], 1)
                    place_b(P)
                close_sum(0, D)
                pe.wait_ge(y_ready, b + 1)
                nc.tensor.transpose(ps[:, 1, 0:PL], row_b[:, 0:128], ident[0:PL, 0:PL])
                nc.tensor.transpose(ps[:, 1, PL:2 * PL], row_b[:, 128:256], ident[0:PL, 0:PL]).then_inc(y_turned, 1)
                pe.wait_ge(yT_ready, b + 1)
                M(ps[0:H1, 0, 0:PL], w1t[:, 0, :], rowT[:, 0, :], start=True, stop=False)
                M(ps[0:H1, 0, 0:PL], w1t[:, 1, :], rowT[:, 1, :], start=False, stop=True).then_inc(h1_made, 1)
                pe.wait_ge(h1_relu, b + 1)
                pe.sem_inc(pe_pass, 1)
                M(ps[0:H2, 5, 0:PL], w2t[:], h1T[:], start=True, stop=True).then_inc(h2_made, 1)
                pe.wait_ge(h2_relu, b + 1)
                M(ps[0:PL, 6, 0:D], h2T[:], w3t[:], start=True, stop=True).then_inc(o_made, 1)
            spare_rows(pe, 0, pairsA, roundsA)
            all_a = pairs_in_all(pe, pairsA)
            with pe.Fori(all_a, EJ // 2 + 1) as P:
                place_b(P)
            for f in range(3):
                last = M(ps[:, 2 + f, 0:NT], zeros16[0:1, 0:128], zeros16[0:1, 0:NT], start=False, stop=True)
            last.then_inc(placed_b, 1)

            n_l = pe.value_load(n_list[0:1, 0:1], min_val=1, max_val=LROWS // ET)
            with pe.Fori(0, n_l) as t:
                pe.wait_ge(l_dve, t * 8 + 1)
                M(ps[:, 0, 0:128], ones128[:], ldiag[:], start=True, stop=True).then_inc(l_pe, 1)
                pe.wait_ge(l_dve, t * 8 + 8)
                M(ps[:, 1, :], lS[:, 0:128], flat(lVC), start=True, stop=True)
                M(ps[:, 2, :], lS[:, 128:256], flat(lVC), start=True, stop=True).then_inc(l_pe, 1)

            def typed_rows(b):
                pe.wait_ge(hrow_ready, b + 1)
                pe.wait_ge(diag_made, b + 1)
                M(ps[:, 1, 0:NTY * PL], row_b[:, 0:128], flat(diag[:]), start=True, stop=True)
                M(ps[:, 2, 0:NTY * PL], row_b[:, 128:256], flat(diag[:]), start=True, stop=True).then_inc(typed_turned, 1)

            def keys_values_queries(b):
                pe.wait_ge(typedT_ready, b + 1)
                for g in range(4):
                    w, o = (wk, wv)[g // 2], 128 * (g % 2)
                    for k in range(NTY):
                        for cc in range(2):
                            last = M(ps[:, 3, g * PL:g * PL + PL], w[:, k, cc, o:o + 128], typedT[:, cc, k * PL:k * PL + PL],
                                     start=(k == 0 and cc == 0), stop=(k == NTY - 1 and cc == 1))
                last.then_inc(kv_made, 1)
                pe.wait_ge(q_copied, b + 1)
                for k in range(NTY):
                    for cc in range(2):
                        last = M(ps[0:PL, 0, 0:D], typedT[:, cc, k * PL:k * PL + PL], wq[:, k, cc, :],
                                 start=(k == 0 and cc == 0), stop=(k == NTY - 1 and cc == 1))
                last.then_inc(q_made, 1)

            def tables(b):
                pe.wait_ge(kvT_ready, b + 1)
                for m in range(8):
                    pe.wait_ge((bank_read_a, bank_read_v)[m % 2], b * 4 + (m // 2 + 1))
                    M(ps[0:PL, 4 + m % 4, :], kvT[:, m // 2, :], flat((bdk, bdm)[m // 4][:, m // 2 % 2, 4 * (m % 2):4 * (m % 2) + 4, :]),
                      start=True, stop=True).then_inc(bank_full, 1)

            typed_rows(0)
            with pe.Fori(0, NB - 1) as b:
                keys_values_queries(b)
                typed_rows(b + 1)
                tables(b)
            keys_values_queries(NB - 1)
            tables(NB - 1)

            total = pairs_in_all(pe, pairsB)

            def turn_hots(s, P):
                pe.wait_ge(hot_made[s], P + 1)
                pe.wait_ge(hotT_made[s], P + 1)
                nc.tensor.transpose(ps[0:PL, 0, 0:64].bitcast(BF16), hot16[:, 0, 0:PL], identb[:])
                nc.tensor.transpose(ps[0:PL, 0, 64:128].bitcast(BF16), hot16[:, 1, 0:PL], identb[:]).then_inc(hot_turned[s], 1)

            def turn_scores(P):
                pe.wait_ge(s_split, P * 4 + 4)
                nc.tensor.transpose(ps[0:6 * NH, 1, 0:64].bitcast(BF16), s_parts.rearrange("p a k -> p (a k)"), identb[:]).then_inc(s_turned, 1)

            def queries(b, P):
                turn_hots(1, P + 1)
                pe.wait_ge(hotT_made[1], P + 2)
                for n in range(2):
                    pe.wait_ge(row_used[1], P * 2 + RING)
                    M(ps[:, 2 + n, 0:D], hotT[0:PL, n, :], flat(q[:, bass.ds(b, 1), :]), start=True, stop=True).then_inc(q_edge, 1)

            def spread(P):
                pe.wait_ge(max_read, P + 1)
                banks = [bass.ds(P % 2 * 2 + (4 + n), 1) for n in range(2)]
                for n, bank in enumerate(banks):
                    M(ps[0:PL, bank, :].rearrange("p a (h e) -> p (a h) e", h=NH), identb[0:PL, 0:PL],
                      neg[0:PL, bass.ds(P % 4, 1), n:n + 1, :].rearrange("p a n e -> p (a n) e").broadcast_to([PL, NH, 128]),
                      start=True, stop=False)
                    if n == 0:
                        turn_scores(P)
                pe.wait_ge(sT_ready, P + 1)
                pe.sem_inc(pe_pass, 1)
                for n, bank in enumerate(banks):
                    for k in range(NH):
                        last = M(flat(ps[0:PL, bank, 128 * k:128 * k + 128]), sel[:, n * NH + k, :], sT, start=False, stop=k == NH - 1)
                last.then_inc(tile_done, 1)

            turn_hots(1, 0)
            queries(0, 0)
            lo, hi = bounds(pe, pairsB, 0)
            with pe.Fori(1, hi) as P:
                queries(0, P)
                spread(P - 1)
            with pe.Fori(1, NB) as b:
                lo, hi = bounds(pe, pairsB, b, 2)
                queries(b, lo)
                spread(lo - 1)
                with pe.Fori(lo + 1, hi) as P:
                    queries(b, P)
                    spread(P - 1)
            spread(total - 1)

            def largest(b, P):
                turn_hots(2, P + 1)
                pe.wait_ge(hotT_made[2], P + 2)
                pe.wait_ge(sd_ready, P + 1)
                for n in range(2):
                    last = M(ps[:, 2, 3 * n * NH:3 * (n + 1) * NH], hotT16[0:PL, n, :], flat(m_all[:, bass.ds(b, 1), :]), start=True, stop=True)
                last.then_inc(m_edge, 1)

            def add(P):
                for n in range(2):
                    pe.wait_ge(row_weighted, P * 2 + (n + 3))
                    M(ps[0:PL, 7, 0:D + NH], hot[:, n, 0:PL], flat(ring[:, bass.ds(P % (RING // 2) * 2 + n, 1), 0:D + NH]),
                      start=False, stop=False).then_inc(row_used[2], 1)

            def through_a(b):
                pe.wait_ge(agg_ready, b + 1)
                M(ps[:, 3, 0:NTY * PL], row_b[:, 0:128], flat(diag[:]), start=True, stop=True)
                M(ps[:, 4, 0:NTY * PL], row_b[:, 128:256], flat(diag[:]), start=True, stop=True).then_inc(agg_turned, 1)
                pe.wait_ge(aggT_ready, b + 1)
                for k in range(NTY):
                    for cc in range(2):
                        last = M(ps[0:PL, 5, 0:D], typedT[:, cc, k * PL:k * PL + PL], wa[:, k, cc, :],
                                 start=(k == 0 and cc == 0), stop=(k == NTY - 1 and cc == 1))
                last.then_inc(att_made, 1)

            pe.wait_ge(m_bucket, 4 * NB)
            pe.wait_ge(hotT_made[1], total + 2)
            turn_hots(2, 0)
            pe.wait_ge(bucket_read[2], 1)
            open_sum(D + NH)
            largest(0, 0)
            lo, hi = bounds(pe, pairsB, 0)
            with pe.Fori(1, hi) as P:
                largest(0, P)
                add(P - 1)
            with pe.Fori(1, NB) as b:
                lo, hi = bounds(pe, pairsB, b, 2)
                largest(b, lo)
                add(lo - 1)
                close_sum(2, D + NH)
                pe.wait_ge(bucket_read[2], b + 1)
                open_sum(D + NH)
                with pe.Fori(lo + 1, hi) as P:
                    largest(b, P)
                    add(P - 1)
                through_a(b - 1)
            add(total - 1)
            close_sum(2, D + NH)
            through_a(NB - 1)
            spare_rows(pe, 2, pairsB, roundsB)
            pe.wait_ge(gru_in, 64)
            for o, n, rows_b in ((0, 2 * D, 2), (2 * D, D, 1)):
                bank = ps[0:NE16 + 1, 1 + o // (2 * D), 0:n]
                M(bank, relt[:, 0, :], wih[:, 0, o:o + n], start=True, stop=False)
                M(bank, relt[:, 1, :], wih[:, 1, o:o + n], start=False, stop=False)
                M(bank, pick[0:rows_b, :], bias[0:rows_b, o:o + n], start=False, stop=True)
            M(ps[0:NE16 + 1, 2, D:2 * D], pick_h, bias[:, 2 * D:3 * D], start=True, stop=True).then_inc(relw_made, 1)

            pe.wait_ge(relw_ready, 1)
            with pe.Fori(0, NB) as b:
                lo, hi = bounds(pe, pairsB, b)
                pe.wait_ge(bucket_read[3], b + 1)
                open_sum(AW)
                with pe.Fori(lo, hi) as P:
                    for n in range(2):
                        t = P * 2 + n
                        pe.wait_ge(hot_made[3], t + 1)
                        pe.wait_ge(row_ready[3], t + 3)
                        M(ps[0:PL, 7, 0:AW], hot[:, n, 0:PL], flat(ring[:, bass.ds(P % (RING // 2) * 2 + n, 1), :]),
                          start=False, stop=False).then_inc(row_used[3], 1)
                close_sum(3, AW)
                pe.wait_ge(bucket_read[3], b + 2)
                pe.sem_inc(pe_pass, 1)
                T = nc.tensor.transpose
                T(ps[:, 1, 0:PL], accrow[:, 0:128], ident[0:PL, 0:PL])
                T(ps[:, 1, PL:2 * PL], accrow[:, 128:256], ident[0:PL, 0:PL])
                T(ps[:, 1, 2 * PL:3 * PL], row_b[:, 0:128], ident[0:PL, 0:PL])
                T(ps[:, 1, 3 * PL:4 * PL], row_b[:, 128:256], ident[0:PL, 0:PL])
                T(ps[0:NE16 + 1, 2, 0:PL], accrow[:, D:AW + 1], ident[0:PL, 0:PL]).then_inc(g_turned, 1)
                pe.wait_ge(gT_ready, b + 1)
                pe.wait_ge(gt_ready, b + 1)
                rzb, inb, hnb = ps[0:PL, 3, :], ps[0:PL, 4, 0:D], ps[0:PL, 5, 0:D]
                for bank, lo_, hi_ in ((rzb, 0, 2 * D), (inb, 2 * D, 3 * D)):
                    M(bank, gT[:, 0, :], wih[:, 0, lo_:hi_], start=True, stop=False)
                    M(bank, gT[:, 1, :], wih[:, 1, lo_:hi_], start=False, stop=False)
                    M(bank, cntT, relw[:, lo_:hi_], start=False, stop=bank is inb)
                M(rzb, gT[:, 2, :], whh[:, 0, 0:2 * D], start=False, stop=False)
                M(rzb, gT[:, 3, :], whh[:, 1, 0:2 * D], start=False, stop=True)
                M(hnb, gT[:, 2, :], whh[:, 0, 2 * D:3 * D], start=True, stop=False)
                M(hnb, gT[:, 3, :], whh[:, 1, 2 * D:3 * D], start=False, stop=False)
                M(hnb, cntT, bhn, start=False, stop=True).then_inc(gates_made, 1)
            spare_rows(pe, 3, pairsB, roundsB)

            with pe.Fori(0, NB) as b:
                pe.wait_ge(f_row, b + 1)
                nc.tensor.transpose(ps[:, 1, 0:PL], row_b[:, 0:128], ident[0:PL, 0:PL])
                nc.tensor.transpose(ps[:, 1, PL:2 * PL], row_b[:, 128:256], ident[0:PL, 0:PL]).then_inc(f_turned, 1)
                pe.wait_ge(fT_ready, b + 1)
                pe.wait_ge(out_ready, b + 1)
                M(ps[0:PL, 2, 0:D], rowT[:, 0, :], wout[:, 0, :], start=True, stop=False)
                M(ps[0:PL, 2, 0:D], rowT[:, 1, :], wout[:, 1, :], start=False, stop=True).then_inc(f_made, 1)


def kernel(**inputs):
    import numpy as _np
    import concourse.bacc as _bacc
    from concourse import mybir as _mybir
    from concourse.bass_utils import run_bass_kernel_spmd as _run

    def get(name):
        return _np.asarray(inputs[name])

    names = ["x", "src", "dst", "edge_type_16", "edge_type_8", "edge_weight", "node_type_4", "L0_gnn_w"]
    laid = [(n, get(n)) for n in names]
    laid += [
        ("w1t", get("L0_gnn_W1").T), ("w2t", get("L0_gnn_W2").T), ("w3t", get("L0_gnn_W3").T),
        ("wk", get("L1_gnn_k_linears")), ("wq", get("L1_gnn_q_linears")),
        ("wv", get("L1_gnn_v_linears")), ("wa", get("L1_gnn_a_linears")),
        ("att", get("L1_gnn_relation_att").transpose(3, 1, 0, 2)),
        ("msg", get("L1_gnn_relation_msg").transpose(2, 1, 0, 3)),
        ("pri", get("L1_gnn_relation_pri")), ("skip", get("L1_gnn_skip")),
        ("relt", get("L2_gnn_relvectors").T), ("wih", get("L2_gnn_w_ih").T), ("whh", get("L2_gnn_w_hh").T),
        ("bias", _np.stack([get("L2_gnn_b_ih"), get("L2_gnn_b_hh")])),
    ]
    nc = _bacc.Bacc("TRN2", target_bir_lowering=False, num_devices=1)
    arrays, args = {}, []
    for name, a in laid:
        a = _np.ascontiguousarray(a)
        arrays[f"in_{name}"] = a
        args.append(nc.dram_tensor(f"in_{name}", a.shape, _mybir.dt.from_np(a.dtype), kind="ExternalInput").ap())
    args.append(nc.dram_tensor("out_0", (N, D), _mybir.dt.float32, kind="ExternalOutput").ap())
    build(nc, *args)
    r = _run(nc, [arrays], core_ids=[0])
    return r.results[0]["out_0"]
```
